# Optimizing a Trainium2 kernel written in Bass

```python
import numpy as np
import jax
import jax.numpy as jnp

def _softmax(x, axis=-1):
    return jax.nn.softmax(x, axis=axis)

def _gelu(x):
    return jax.nn.gelu(x, approximate=True)

def _silu(x):
    return jax.nn.silu(x)

def _sigmoid(x):
    return jax.nn.sigmoid(x)

def _layernorm(x, axis=-1, eps=1e-05):
    m = jnp.mean(x, axis=axis, keepdims=True)
    v = jnp.var(x, axis=axis, keepdims=True)
    return (x - m) / jnp.sqrt(v + eps)

def _scatter_add(tgt, idx, src, axis=0):
    return tgt.at[idx].add(src)

def _segment_sum(src, seg, n):
    return jax.ops.segment_sum(src, seg, n)
kernel_name = 'mk_gps_d2_gnn_r8_e6cf32'

def setup_inputs(seed: int=0):
    np.random.seed(seed)
    _w = jnp.asarray

    def _rec_inputs():
        import jax
        import jax.numpy as jnp
        _gk = jax.random.key(seed)
        x = -6.415e-05 + 1 * jax.random.normal(jax.random.fold_in(_gk, 1), (1250, 512), jnp.float32)
        _s = jax.random.randint(jax.random.fold_in(_gk, 2), (20000,), 0, 1250, jnp.int32)
        _d = jax.random.randint(jax.random.fold_in(_gk, 3), (20000,), 0, 1250, jnp.int32)
        _loop = jnp.arange(1250, dtype=jnp.int32)
        src = jnp.concatenate([_s, _d, _loop])
        dst = jnp.concatenate([_d, _s, _loop])
        _o = jnp.argsort(dst, stable=True)
        src = src[_o]
        dst = dst[_o]
        return (x, src, dst)
    x, src, dst = _rec_inputs()

    def _L0_gnn_setup():
        import jax, jax.numpy as jnp
        import numpy as np
        N_NODES = 2500
        N_EDGES = 40000
        D = 512
        L = 3
        key = jax.random.key(seed)
        ks = jax.random.split(key, 6)
        x = jax.random.normal(ks[0], (N_NODES, D), dtype=jnp.float32)
        Ws_self = jax.random.normal(ks[1], (L, D, D), dtype=jnp.float32) * 0.05
        Ws_neigh = jax.random.normal(ks[2], (L, D, D), dtype=jnp.float32) * 0.05
        bs = jax.random.normal(ks[3], (L, D), dtype=jnp.float32) * 0.05
        src = jax.random.randint(ks[4], (N_EDGES,), 0, N_NODES, dtype=jnp.int64)
        dst = jax.random.randint(ks[5], (N_EDGES,), 0, N_NODES, dtype=jnp.int64)
        return {'x': x, 'Ws_self': Ws_self, 'Ws_neigh': Ws_neigh, 'bs': bs, 'src': src, 'dst': dst}
    _L0_gnn_all = _L0_gnn_setup()
    _L0_gnn_in = {k: v for k, v in _L0_gnn_all.items() if k in ('Ws_self', 'Ws_neigh', 'bs')}
    del _L0_gnn_all

    def _L0_mix_setup():
        import jax, jax.numpy as jnp
        import numpy as np
        NUM_HEADS = 8
        EPS = 1e-06
        key = jax.random.key(seed)
        k1, k2, k3 = jax.random.split(key, 3)
        B, N, C = (8, 512, 512)
        x = jax.random.normal(k1, (B, N, C), dtype=jnp.float32)
        Wq = jax.random.normal(k2, (C, C), dtype=jnp.float32) * (1.0 / np.sqrt(C))
        Wkv = jax.random.normal(k3, (2 * C, C), dtype=jnp.float32) * (1.0 / np.sqrt(C))
        return {'x': x, 'Wq': Wq, 'Wkv': Wkv}
    _L0_mix_all = _L0_mix_setup()
    _L0_mix_in = {k: v for k, v in _L0_mix_all.items() if k in ('Wq', 'Wkv')}
    del _L0_mix_all

    def _L0_ffn_setup():
        import jax, jax.numpy as jnp
        import numpy as np
        B, N, DIM = (1, 256, 512)
        DH, H = (64, 8)
        E, FF = (8, 256)

        def _layernorm(x, g, b, eps=1e-05):
            mu = jnp.mean(x, axis=-1, keepdims=True)
            var = jnp.mean(jnp.square(x - mu), axis=-1, keepdims=True)
            return (x - mu) * jax.lax.rsqrt(var + eps) * g + b

        def _l2norm(x, eps=1e-12):
            return x / jnp.sqrt(jnp.sum(jnp.square(x), axis=-1, keepdims=True) + eps)
        key = jax.random.key(seed)
        ks = jax.random.split(key, 12)
        g = lambda k, shape: jax.random.normal(k, shape, jnp.float32) * 0.02
        return {'x': jax.random.normal(ks[0], (B, N, DIM), jnp.float32), 'ln_g': jnp.ones((DIM,), jnp.float32), 'ln_b': jnp.zeros((DIM,), jnp.float32), 'Wq': g(ks[1], (DIM, DIM)), 'Wk': g(ks[2], (DIM, DIM)), 'Wv': g(ks[3], (DIM, DIM)), 'Wo': g(ks[4], (DIM, DIM)), 'qn_g': jnp.ones((DH,), jnp.float32), 'kn_g': jnp.ones((DH,), jnp.float32), 'gate_W': g(ks[5], (DIM, E)), 'gate_b': jnp.zeros((E,), jnp.float32), 'W1': g(ks[6], (E, DIM, FF)), 'b1': jnp.zeros((E, FF), jnp.float32), 'W2': g(ks[7], (E, FF, DIM)), 'b2': jnp.zeros((E, DIM), jnp.float32)}
    _L0_ffn_all = _L0_ffn_setup()
    _L0_ffn_in = {k: v for k, v in _L0_ffn_all.items() if k in ('ln_g', 'ln_b', 'Wq', 'Wk', 'Wv', 'Wo', 'qn_g', 'kn_g', 'gate_W', 'gate_b', 'W1', 'b1', 'W2', 'b2')}
    del _L0_ffn_all

    def _L1_gnn_setup():
        import jax, jax.numpy as jnp
        import numpy as np
        N_NODES = 12500
        D_IN = 512
        D_OUT = 512
        N_EDGES = 400000
        key = jax.random.key(seed)
        k_x, k_w, k_e = jax.random.split(key, 3)
        x = jax.random.normal(k_x, (N_NODES, D_IN), dtype=jnp.float32)
        weight = jax.random.normal(k_w, (D_IN, D_OUT), dtype=jnp.float32) * np.sqrt(2.0 / D_IN)
        edge_indices = jax.random.randint(k_e, (2, N_EDGES), 0, N_NODES, dtype=jnp.int32)
        return {'x': x, 'weight': weight, 'edge_indices': edge_indices}
    _L1_gnn_all = _L1_gnn_setup()
    _L1_gnn_in = {k: v for k, v in _L1_gnn_all.items() if k in ('weight',)}
    del _L1_gnn_all

    def _L1_mix_setup():
        import jax, jax.numpy as jnp
        import numpy as np
        DIM = 512
        HEADS = 8
        DIM_HEAD = 64
        SLICE = 32
        INNER = HEADS * DIM_HEAD
        key = jax.random.key(seed)
        ks = jax.random.split(key, 8)
        B, N = (8, 1024)
        s = 0.02
        return {'x': jax.random.normal(ks[0], (B, N, DIM), dtype=jnp.float32), 'W_in': jax.random.normal(ks[1], (DIM, INNER), dtype=jnp.float32) * s, 'b_in': jnp.zeros((INNER,), dtype=jnp.float32), 'Wq': jax.random.normal(ks[2], (DIM_HEAD, SLICE), dtype=jnp.float32) * s, 'Wk': jax.random.normal(ks[3], (DIM_HEAD, SLICE), dtype=jnp.float32) * s, 'Wv': jax.random.normal(ks[4], (DIM_HEAD, DIM_HEAD), dtype=jnp.float32) * s, 'W_out': jax.random.normal(ks[5], (INNER, DIM), dtype=jnp.float32) * s, 'b_out': jnp.zeros((DIM,), dtype=jnp.float32)}
    _L1_mix_all = _L1_mix_setup()
    _L1_mix_in = {k: v for k, v in _L1_mix_all.items() if k in ('W_in', 'b_in', 'Wq', 'Wk', 'Wv', 'W_out', 'b_out')}
    del _L1_mix_all

    def _L1_ffn_setup():
        import math
        import jax, jax.numpy as jnp
        import numpy as np
        B, T, H, E, K, F = (4, 512, 512, 8, 2, 256)
        CAP_FACTOR, ROUND_TO = (0.3125, 128)

        def _capacity(num_tokens):
            cap = math.ceil(CAP_FACTOR * num_tokens)
            cap = ROUND_TO * math.ceil(cap / ROUND_TO)
            return max(1, min(cap, num_tokens))
        key = jax.random.key(seed)
        k0, k1, k2, k3 = jax.random.split(key, 4)
        x = jax.random.normal(k0, (B, T, H), jnp.float32)
        router_w = jax.random.normal(k1, (H, E), jnp.float32) * 0.02
        w1 = jax.random.normal(k2, (E, H, F), jnp.float32) * (1.0 / np.sqrt(H))
        b1 = jnp.zeros((E, F), jnp.float32)
        w2 = jax.random.normal(k3, (E, F, H), jnp.float32) * (1.0 / np.sqrt(F))
        b2 = jnp.zeros((E, H), jnp.float32)
        return {'x': x, 'router_w': router_w, 'w1': w1, 'b1': b1, 'w2': w2, 'b2': b2}
    _L1_ffn_all = _L1_ffn_setup()
    _L1_ffn_in = {k: v for k, v in _L1_ffn_all.items() if k in ('router_w', 'w1', 'b1', 'w2', 'b2')}
    del _L1_ffn_all
    return {'x': x, 'src': src, 'dst': dst, 'L0_gnn_Ws_self': _L0_gnn_in['Ws_self'], 'L0_gnn_Ws_neigh': _L0_gnn_in['Ws_neigh'], 'L0_gnn_bs': _L0_gnn_in['bs'], 'L0_mix_Wq': _L0_mix_in['Wq'], 'L0_mix_Wkv': _L0_mix_in['Wkv'], 'L0_ffn_ln_g': _L0_ffn_in['ln_g'], 'L0_ffn_ln_b': _L0_ffn_in['ln_b'], 'L0_ffn_Wq': _L0_ffn_in['Wq'], 'L0_ffn_Wk': _L0_ffn_in['Wk'], 'L0_ffn_Wv': _L0_ffn_in['Wv'], 'L0_ffn_Wo': _L0_ffn_in['Wo'], 'L0_ffn_qn_g': _L0_ffn_in['qn_g'], 'L0_ffn_kn_g': _L0_ffn_in['kn_g'], 'L0_ffn_gate_W': _L0_ffn_in['gate_W'], 'L0_ffn_gate_b': _L0_ffn_in['gate_b'], 'L0_ffn_W1': _L0_ffn_in['W1'], 'L0_ffn_b1': _L0_ffn_in['b1'], 'L0_ffn_W2': _L0_ffn_in['W2'], 'L0_ffn_b2': _L0_ffn_in['b2'], 'L1_gnn_weight': _L1_gnn_in['weight'], 'L1_mix_W_in': _L1_mix_in['W_in'], 'L1_mix_b_in': _L1_mix_in['b_in'], 'L1_mix_Wq': _L1_mix_in['Wq'], 'L1_mix_Wk': _L1_mix_in['Wk'], 'L1_mix_Wv': _L1_mix_in['Wv'], 'L1_mix_W_out': _L1_mix_in['W_out'], 'L1_mix_b_out': _L1_mix_in['b_out'], 'L1_ffn_router_w': _L1_ffn_in['router_w'], 'L1_ffn_w1': _L1_ffn_in['w1'], 'L1_ffn_b1': _L1_ffn_in['b1'], 'L1_ffn_w2': _L1_ffn_in['w2'], 'L1_ffn_b2': _L1_ffn_in['b2']}

def reference(x, src, dst, L0_gnn_Ws_self, L0_gnn_Ws_neigh, L0_gnn_bs, L0_mix_Wq, L0_mix_Wkv, L0_ffn_ln_g, L0_ffn_ln_b, L0_ffn_Wq, L0_ffn_Wk, L0_ffn_Wv, L0_ffn_Wo, L0_ffn_qn_g, L0_ffn_kn_g, L0_ffn_gate_W, L0_ffn_gate_b, L0_ffn_W1, L0_ffn_b1, L0_ffn_W2, L0_ffn_b2, L1_gnn_weight, L1_mix_W_in, L1_mix_b_in, L1_mix_Wq, L1_mix_Wk, L1_mix_Wv, L1_mix_W_out, L1_mix_b_out, L1_ffn_router_w, L1_ffn_w1, L1_ffn_b1, L1_ffn_w2, L1_ffn_b2):
    import jax
    import jax.numpy as jnp

    def _L0_gnn_ref(x, Ws_self, Ws_neigh, bs, src, dst):
        import jax, jax.numpy as jnp
        import numpy as np
        N_NODES = 2500
        N_EDGES = 40000
        D = 512
        L = 3
        n = x.shape[0]
        deg = jax.ops.segment_sum(jnp.ones_like(dst, dtype=x.dtype), dst, num_segments=n)
        inv_deg = (1.0 / jnp.clip(deg, 1.0))[:, None]
        h = x
        n_layers = Ws_self.shape[0]
        for l in range(n_layers):
            neigh = jax.ops.segment_sum(h[src], dst, num_segments=n) * inv_deg
            h = h @ Ws_self[l] + neigh @ Ws_neigh[l] + bs[l]
            if l != n_layers - 1:
                h = jax.nn.relu(h)
        return h

    def _L0_mix_ref(x, Wq, Wkv):
        import jax, jax.numpy as jnp
        import numpy as np
        NUM_HEADS = 8
        EPS = 1e-06
        B, N, C = x.shape
        h = NUM_HEADS
        d = C // h
        q = (x @ Wq.T).reshape(B, N, h, d)
        kv = (x @ Wkv.T).reshape(B, N, 2, h, d)
        k = kv[:, :, 0]
        v = kv[:, :, 1]
        Q = jax.nn.elu(q) + 1.0
        K = jax.nn.elu(k) + 1.0
        v_length = v.shape[1]
        v = v / v_length
        KV = jnp.einsum('nshd,nshv->nhdv', K, v)
        Z = 1.0 / (jnp.einsum('nlhd,nhd->nlh', Q, K.sum(axis=1)) + EPS)
        out = jnp.einsum('nlhd,nhdv,nlh->nlhv', Q, KV, Z) * v_length
        return out.reshape(B, N, C)

    def _L0_ffn_ref(x, ln_g, ln_b, Wq, Wk, Wv, Wo, qn_g, kn_g, gate_W, gate_b, W1, b1, W2, b2):
        import jax, jax.numpy as jnp
        import numpy as np
        B, N, DIM = (1, 256, 512)
        DH, H = (64, 8)
        E, FF = (8, 256)

        def _layernorm(x, g, b, eps=1e-05):
            mu = jnp.mean(x, axis=-1, keepdims=True)
            var = jnp.mean(jnp.square(x - mu), axis=-1, keepdims=True)
            return (x - mu) * jax.lax.rsqrt(var + eps) * g + b

        def _l2norm(x, eps=1e-12):
            return x / jnp.sqrt(jnp.sum(jnp.square(x), axis=-1, keepdims=True) + eps)
        b, n, d = x.shape
        dh = qn_g.shape[0]
        h = d // dh
        hx = _layernorm(x, ln_g, ln_b)
        q = (hx @ Wq).reshape(b, n, h, dh).transpose(0, 2, 1, 3)
        k = (hx @ Wk).reshape(b, n, h, dh).transpose(0, 2, 1, 3)
        v = (hx @ Wv).reshape(b, n, h, dh).transpose(0, 2, 1, 3)
        scale = jnp.sqrt(jnp.float32(dh))
        q = _l2norm(q) * scale * qn_g
        k = _l2norm(k) * scale * kn_g
        scores = jnp.einsum('bhqd,bhkd->bhqk', q, k) * dh ** (-0.5)
        causal = jnp.tril(jnp.ones((n, n), bool))
        scores = jnp.where(causal, scores, jnp.finfo(scores.dtype).min)
        attn = jax.nn.softmax(scores, axis=-1)
        o = jnp.einsum('bhqk,bhkd->bhqd', attn, v)
        y = o.transpose(0, 2, 1, 3).reshape(b, n, d) @ Wo
        gate = jax.nn.softmax(y @ gate_W + gate_b, axis=-1)
        hid = jax.nn.gelu(jnp.einsum('bnd,edf->bnef', y, W1) + b1)
        eo = jnp.einsum('bnef,efd->bned', hid, W2) + b2
        out = jnp.einsum('bned,bne->bnd', eo, gate)
        return out

    def _L1_gnn_ref(x, weight, edge_indices):
        import jax, jax.numpy as jnp
        import numpy as np
        N_NODES = 12500
        D_IN = 512
        D_OUT = 512
        N_EDGES = 400000
        N = x.shape[0]
        loops = jnp.arange(N, dtype=edge_indices.dtype)
        row = jnp.concatenate([edge_indices[0], loops])
        col = jnp.concatenate([edge_indices[1], loops])
        deg = jax.ops.segment_sum(jnp.ones_like(row, dtype=x.dtype), row, num_segments=N)
        deg_rsqrt = jax.lax.rsqrt(deg)
        vals = deg_rsqrt[row] * deg_rsqrt[col]
        agg = jax.ops.segment_sum(vals[:, None] * x[col], row, num_segments=N)
        return jax.nn.relu(agg @ weight)

    def _L1_mix_ref(x, W_in, b_in, Wq, Wk, Wv, W_out, b_out):
        import jax, jax.numpy as jnp
        import numpy as np
        DIM = 512
        HEADS = 8
        DIM_HEAD = 64
        SLICE = 32
        INNER = HEADS * DIM_HEAD
        B, N, C = x.shape
        x_mid = (x @ W_in + b_in).reshape(B, N, HEADS, DIM_HEAD).transpose(0, 2, 1, 3)
        q = x_mid @ Wq
        k = x_mid @ Wk
        v = x_mid @ Wv
        q = jax.nn.softmax(q, axis=-1)
        k = jax.nn.softmax(k, axis=-2)
        kv = jnp.einsum('bhns,bhnc->bhsc', k, v)
        qkv = jnp.einsum('bhns,bhsc->bhnc', q, kv)
        qkv = qkv.transpose(0, 2, 1, 3).reshape(B, N, INNER)
        return qkv @ W_out + b_out

    def _L1_ffn_ref(x, router_w, w1, b1, w2, b2):
        import math
        import jax, jax.numpy as jnp
        import numpy as np
        B, T, H, E, K, F = (4, 512, 512, 8, 2, 256)
        CAP_FACTOR, ROUND_TO = (0.3125, 128)

        def _capacity(num_tokens):
            cap = math.ceil(CAP_FACTOR * num_tokens)
            cap = ROUND_TO * math.ceil(cap / ROUND_TO)
            return max(1, min(cap, num_tokens))
        Bc, Tc, Hc = x.shape
        n = Bc * Tc
        cap = _capacity(n)
        flat = x.reshape(n, Hc)
        logits = (flat @ router_w).astype(jnp.float32)
        sel_logits, expert_idx = jax.lax.top_k(logits, K)
        weights = jax.nn.softmax(sel_logits, axis=-1)
        fe = expert_idx.reshape(-1).astype(jnp.int32)
        fw = weights.reshape(-1)
        tok = jnp.broadcast_to(jnp.arange(n, dtype=jnp.int32)[:, None], expert_idx.shape).reshape(-1)
        order = jnp.argsort(fe)
        se, st, sw = (fe[order], tok[order], fw[order])
        counts = jnp.bincount(se, length=E)
        offsets = (jnp.cumsum(counts) - counts).astype(jnp.int32)
        slot = jnp.arange(se.shape[0], dtype=jnp.int32) - offsets[se]
        keep = slot < cap
        sw = jnp.where(keep, sw, 0.0)
        sx = flat[st]
        expert_inputs = jnp.zeros((E, cap, Hc), flat.dtype).at[se, slot].set(sx, mode='drop')
        h = jax.nn.gelu(jnp.einsum('ech,ehf->ecf', expert_inputs, w1) + b1[:, None, :])
        out = jnp.einsum('ecf,efh->ech', h, w2) + b2[:, None, :]
        clipped = jnp.minimum(counts, cap)
        valid = (jnp.arange(cap, dtype=jnp.int32)[None, :] < clipped[:, None])[..., None]
        out = jnp.where(valid, out, 0)
        slot_c = jnp.minimum(slot, cap - 1)
        gathered = out[se, slot_c] * sw[:, None].astype(out.dtype)
        combined = jnp.zeros((n, Hc), out.dtype).at[st].add(gathered)
        return combined.reshape(Bc, Tc, Hc)
    edge_index = jnp.stack([src, dst])
    xn = _layernorm(x, axis=-1)
    x = x + _L0_gnn_ref(xn, L0_gnn_Ws_self, L0_gnn_Ws_neigh, L0_gnn_bs, src, dst) + _L0_mix_ref(xn[None], L0_mix_Wq, L0_mix_Wkv)[0]
    x = x + _L0_ffn_ref(_layernorm(x, axis=-1)[None], L0_ffn_ln_g, L0_ffn_ln_b, L0_ffn_Wq, L0_ffn_Wk, L0_ffn_Wv, L0_ffn_Wo, L0_ffn_qn_g, L0_ffn_kn_g, L0_ffn_gate_W, L0_ffn_gate_b, L0_ffn_W1, L0_ffn_b1, L0_ffn_W2, L0_ffn_b2)[0]
    xn = _layernorm(x, axis=-1)
    x = x + _L1_gnn_ref(xn, L1_gnn_weight, edge_index) + _L1_mix_ref(xn[None], L1_mix_W_in, L1_mix_b_in, L1_mix_Wq, L1_mix_Wk, L1_mix_Wv, L1_mix_W_out, L1_mix_b_out)[0]
    x = x + _L1_ffn_ref(_layernorm(x, axis=-1)[None], L1_ffn_router_w, L1_ffn_w1, L1_ffn_b1, L1_ffn_w2, L1_ffn_b2)[0]
    return x

_drawn_inputs = setup_inputs


def setup_inputs(seed=0):
    import zlib

    import numpy as np

    out = dict(_drawn_inputs(seed))
    spreads = {'L0_ffn_ln_g': (1.0, 0.6),
     'L0_ffn_ln_b': (0.0, 0.8),
     'L0_ffn_qn_g': (1.0, 0.6),
     'L0_ffn_kn_g': (1.0, 0.6),
     'L0_ffn_gate_b': (0.0, 0.37),
     'L0_ffn_b1': (0.0, 0.422),
     'L0_ffn_b2': (0.0, 0.1),
     'L1_mix_b_in': (0.0, 0.551),
     'L1_mix_b_out': (0.0, 0.1),
     'L1_ffn_b1': (0.0, 0.304),
     'L1_ffn_b2': (0.0, 0.1)}
    factors = {'L0_mix_Wq': 74.569,
     'L0_ffn_Wq': 8.0,
     'L0_ffn_Wk': 8.0,
     'L0_ffn_Wo': 3.315,
     'L0_ffn_gate_W': 4.542,
     'L0_ffn_W1': 3.795,
     'L0_ffn_W2': 3.514,
     'L1_mix_Wq': 200.0,
     'L1_mix_Wk': 176.448}
    for name, (base, spread) in spreads.items():
        noise = np.random.default_rng([zlib.crc32(name.encode()), seed]).standard_normal(out[name].shape)
        drawn = base * np.exp(spread * noise) if base else spread * noise
        out[name] = jnp.asarray(drawn.astype(out[name].dtype))
    for name, factor in factors.items():
        out[name] = (out[name] * factor).astype(out[name].dtype)
    return out
```

```python
from contextlib import ExitStack

import numpy as np
import concourse.bass as bass
from concourse import mybir

F32 = mybir.dt.float32
F32R = mybir.dt.float32r
BF16 = mybir.dt.bfloat16
I32 = mybir.dt.int32
I16 = mybir.dt.int16
ALU = mybir.AluOpType
ACT = mybir.ActivationFunctionType
AX = mybir.AxisListType

N = 1250
D = 512
P = 125
T = N // P
KC = D // 128
EDGES = 41250
SUPERS = 110
SUB = 3
W = 250
WINDOWS = N * T // W
RING = 4
COLS = [(0, 418), (418, 416), (834, 416)]
EPS = 1e-5


class Chip:

    def __init__(self, nc, ctx):
        def sb(name, shape, dt):
            return ctx.enter_context(nc.sbuf_tensor(name, shape, dt))

        self.nc = nc
        self.in_use = []
        self.named = 0
        self.adj = sb("adj", [128, T, N], F32)
        self.x = sb("x", [128, T, D], F32)
        self.xt = sb("xt", [128, KC, N], F32)
        self.nat = sb("nat", [128, T, D], F32)
        self.w = sb("w", [128, 3, KC, D], F32)
        self.ident = sb("ident", [128, 128], F32)
        self.ones = sb("ones", [128, 128], F32)
        self.inv_n = sb("inv_n", [128, T], F32)
        self.out_n = sb("out_n", [128, T], F32)
        self.gain = sb("gain", [128, 16], F32)
        self.small = sb("small", [128, 512], F32)
        self.bounds = sb("bounds", [1, 3 * WINDOWS], I32)
        self.ps = ctx.enter_context(nc.psum_tensor("ps", [128, 8, 512], F32))

    def semaphore(self, name):
        self.named += 1
        handle = self.nc.alloc_semaphore(name=f"{name}_{self.named}")
        self.in_use.append(handle)
        return handle

    def recycle(self):
        self.nc.clear_and_free_semaphores(self.in_use)
        self.nc.all_engine_barrier()
        self.in_use = []

    def work(self, ctx, name, columns, rounded=0):
        self.big = ctx.enter_context(self.nc.sbuf_tensor(name, [128, columns], F32))
        if rounded:
            self.rounded = ctx.enter_context(self.nc.sbuf_tensor(name + "_r", [128, rounded], F32R))
        return self.big


def stage_prepare(c, x, src, dst, w_next):
    nc = c.nc
    codes = c.big[:, 0:750].bitcast(I32).rearrange("p (a e) -> p a e", a=2)
    f = c.big[:, 750:750 + 6 * 375].rearrange("p (a e) -> p a e", a=6)
    srcf, dstf, tile, local, code, spare = (f[0:SUPERS, k, :] for k in range(6))
    wbase = c.small[0:SUPERS, 0:WINDOWS]
    rowno = c.small[0:SUPERS, 50:51]
    least, most = c.small[0:SUPERS, 51:52], c.small[0:SUPERS, 52:53]
    meets = c.small[0:SUPERS, 60:110]
    marks = c.small[0:SUPERS, 120:220]
    ends = c.small[0:100, 230:231]
    line = c.small[0:1, 240:400]
    c.gcol = c.big[0:P, 3200:3860]
    c.lcol = c.big[0:P, 3900:4560]
    with ExitStack() as s:
        sem = lambda n: c.semaphore(n)
        loaded_x, loaded_e, const, dve, turned, evac, wload = map(sem, (
            "loaded_x", "loaded_e", "const", "dve", "turned", "evac", "wload"))
        block = s.enter_context(nc.Block())

        @block.sync
        def _(sp):
            sp.dma_start(codes[0:SUPERS, 0, :], src.rearrange("(s e) -> s e", s=SUPERS)).then_inc(loaded_e, 16)
            sp.dma_start(codes[0:SUPERS, 1, :], dst.rearrange("(s e) -> s e", s=SUPERS)).then_inc(loaded_e, 16)
            sp.dma_start(c.x[0:P], x.rearrange("(t p) d -> p t d", p=P)).then_inc(loaded_x, 16)
            for to, of in w_next:
                sp.dma_start(to, of).then_inc(wload, 16)
            sp.wait_ge(loaded_x, 16)
            if w_next:
                sp.wait_ge(wload, 16 * len(w_next))

        @block.gpsimd
        def _(pool):
            nc.gpsimd.memset(c.ident[:], 0.0).then_inc(const, 1)
            nc.gpsimd.memset(c.ones[:], 1.0).then_inc(const, 1)
            pool.wait_ge(const, 2)
            nc.gpsimd.affine_select(out=c.ident[:], in_=c.ident[:], compare_op=ALU.not_equal, fill=1.0, base=0,
                                    pattern=[[-1, 128]], channel_multiplier=1).then_inc(const, 1)
            nc.gpsimd.iota(wbase, [[W, WINDOWS]], base=0, channel_multiplier=0,
                           allow_small_or_imprecise_dtypes=True).then_inc(const, 1)
            nc.gpsimd.iota(rowno, [[0, 1]], base=0, channel_multiplier=1,
                           allow_small_or_imprecise_dtypes=True).then_inc(const, 1)

        @block.vector
        def _(v):
            count = [0]

            def link(ins):
                count[0] += 1
                ins.then_inc(dve, 1)
                v.wait_ge(dve, count[0])

            v.wait_ge(loaded_e, 32)
            nc.vector.tensor_copy(srcf, codes[0:SUPERS, 0, :]).then_inc(dve, 1)
            nc.vector.tensor_copy(dstf, codes[0:SUPERS, 1, :]).then_inc(dve, 1)
            count[0] += 2
            v.wait_ge(dve, count[0])
            link(nc.vector.tensor_scalar(tile, srcf, float(P), None, ALU.is_ge))
            for j in range(2, T):
                link(nc.vector.scalar_tensor_tensor(tile, srcf, float(P * j), tile, ALU.is_ge, ALU.add))
            link(nc.vector.scalar_tensor_tensor(local, tile, float(-P), srcf, ALU.mult, ALU.add))
            link(nc.vector.scalar_tensor_tensor(code, dstf, float(T), tile, ALU.mult, ALU.add))
            nc.vector.tensor_reduce(most, code, AX.X, ALU.max).then_inc(dve, 1)
            count[0] += 1
            link(nc.vector.tensor_reduce(least, code, AX.X, ALU.min))
            v.wait_ge(const, 5)
            link(nc.vector.tensor_scalar(marks[:, 0:50], wbase, most, None, ALU.is_le))
            link(nc.vector.tensor_scalar(marks[:, 50:100], wbase, float(W - 1), least, ALU.add, ALU.is_ge))
            link(nc.vector.tensor_tensor(meets, marks[:, 0:50], marks[:, 50:100], ALU.mult))
            link(nc.vector.tensor_scalar(c.small[0:SUPERS, 53:54], rowno, 1.0, None, ALU.add))
            link(nc.vector.tensor_scalar(c.small[0:SUPERS, 54:55], rowno, -1.0, float(SUPERS), ALU.mult, ALU.add))
            link(nc.vector.tensor_scalar(marks[:, 0:50], meets, c.small[0:SUPERS, 53:54], None, ALU.mult))
            link(nc.vector.tensor_scalar(marks[:, 50:100], meets, c.small[0:SUPERS, 54:55], None, ALU.mult))
            nc.vector.memset(line[:, 150:151], 0.0).then_inc(evac, 1)
            v.wait_ge(turned, 7)
            nc.vector.tensor_reduce(ends, c.ps[0:100, 6, 0:SUPERS], AX.X, ALU.max).then_inc(evac, 1)
            for k in range(6):
                to = (c.lcol if k < 3 else c.gcol)[:, 0:SUPERS * SUB].rearrange("p (s j) -> p s j", j=SUB)
                link(nc.vector.tensor_copy(to[:, :, k % 3], c.ps[0:P, k, 0:SUPERS]))
            v.wait_ge(turned, 8)
            link(nc.vector.tensor_copy(line[:, 0:100], c.ps[0:1, 7, 0:100]))
            link(nc.vector.tensor_scalar(line[:, 0:50], line[:, 0:50], 1.0, None, ALU.max))
            link(nc.vector.tensor_scalar(line[:, 50:100], line[:, 50:100], -1.0, float(SUPERS), ALU.mult, ALU.add))
            link(nc.vector.scalar_tensor_tensor(line[:, 50:100], line[:, 0:50], -1.0, line[:, 50:100], ALU.add, ALU.min))
            link(nc.vector.tensor_tensor(line[:, 100:150], line[:, 0:50], line[:, 50:100], ALU.subtract))
            v.wait_ge(evac, 1)
            for w in range(1, WINDOWS):
                link(nc.vector.tensor_tensor(line[:, 0:1] if w == 1 else line[:, w - 1:w],
                                             line[:, 100:101] if w == 1 else line[:, w - 2:w - 1],
                                             line[:, 150:151] if w == 1 else line[:, 99 + w:100 + w], ALU.add))
            link(nc.vector.tensor_copy(c.bounds[:, 0:50], line[:, 50:100]))
            link(nc.vector.tensor_copy(c.bounds[:, 50:100], line[:, 100:150]))
            link(nc.vector.memset(c.bounds[:, 100:101], 0))
            link(nc.vector.tensor_copy(c.bounds[:, 101:150], line[:, 0:49]))

        @block.tensor
        def _(pe):
            pe.wait_ge(const, 5)
            pe.wait_ge(dve, 2 + 9 + 2)
            for k in range(6):
                of = (local if k < 3 else code).rearrange("p (j e) -> p j e", j=SUB)
                nc.tensor.transpose(c.ps[0:P, k, 0:SUPERS], of[:, k % 3, :], c.ident[0:SUPERS, 0:SUPERS]).then_inc(turned, 1)
            pe.wait_ge(dve, 2 + 9 + 2 + 2 + 7)
            nc.tensor.transpose(c.ps[0:100, 6, 0:SUPERS], marks, c.ident[0:SUPERS, 0:SUPERS]).then_inc(turned, 1)
            pe.wait_ge(evac, 2)
            nc.tensor.transpose(c.ps[0:1, 7, 0:100], ends, c.ident[0:100, 0:100]).then_inc(turned, 1)


def stage_adjacency(c):
    nc = c.nc
    iota = c.big[:, 5000:11250].bitcast(I16)
    iotal = c.big[:, 11250:11320].bitcast(I16)
    hots_g = c.big[:, 12000:12000 + RING * SUB * W // 2].bitcast(BF16).rearrange("p (r j e) -> p (r j) e", r=RING, j=SUB)
    hots_l = c.big[:, 14000:14000 + RING * SUB * 64].bitcast(BF16).rearrange("p (r j e) -> p (r j) e", r=RING, j=SUB)
    zeros = c.big[:, 15000:15064].bitcast(BF16)
    with ExitStack() as s:
        sem = lambda n: c.semaphore(n)
        const, hot, used, window_done, window_free = map(sem, (
            "const", "hot", "used", "window_done", "window_free"))
        block = s.enter_context(nc.Block())

        @block.gpsimd
        def _(pool):
            nc.gpsimd.iota(iota[:, 0:N * T], [[1, N * T]], base=0, channel_multiplier=0).then_inc(const, 1)
            nc.gpsimd.iota(iotal[:, 0:P], [[1, P]], base=0, channel_multiplier=0).then_inc(const, 1)
            nc.gpsimd.memset(zeros, 0.0).then_inc(const, 1)

        @block.vector
        def _(v):
            v.wait_ge(const, 3)
            with v.Fori(0, WINDOWS) as w:
                first = v.value_load(c.bounds[0:1, bass.ds(w, 1)], min_val=0, max_val=SUPERS - 1)
                rows = v.value_load(c.bounds[0:1, bass.ds(w + WINDOWS, 1)], min_val=1, max_val=SUPERS)
                before = v.value_load(c.bounds[0:1, bass.ds(w + 2 * WINDOWS, 1)], min_val=0, max_val=SUPERS * WINDOWS)
                with v.Fori(0, rows) as i:
                    v.wait_ge(used, before + i + 1)
                    for j in range(SUB):
                        ins = nc.vector.tensor_scalar(hots_g[0:P, bass.ds(((before + i) % RING) * SUB + j, 1), 0:W],
                                                iota[0:P, bass.ds(w * W, W)], c.gcol[:, bass.ds((first + i) * SUB + j, 1)],
                                                None, ALU.is_equal)
                        ins = nc.vector.tensor_scalar(hots_l[0:P, bass.ds(((before + i) % RING) * SUB + j, 1), 0:P],
                                                iotal[0:P, 0:P], c.lcol[:, bass.ds((first + i) * SUB + j, 1)],
                                                None, ALU.is_equal)
                    ins.then_inc(hot, 1)

        @block.tensor
        def _(pe):
            pe.wait_ge(const, 3)
            pe.sem_inc(used, RING)
            with pe.Fori(0, WINDOWS // 2) as ww:
                for par in range(2):
                    w = ww * 2 + par
                    rows = pe.value_load(c.bounds[0:1, bass.ds(w + WINDOWS, 1)], min_val=1, max_val=SUPERS)
                    before = pe.value_load(c.bounds[0:1, bass.ds(w + 2 * WINDOWS, 1)], min_val=0, max_val=SUPERS * WINDOWS)
                    pe.wait_ge(window_free, w + 1)
                    out = c.ps[0:P, par, 0:W]
                    nc.tensor.matmul(out, zeros[0:P, 0:P], iota[0:P, 0:W].bitcast(BF16), start=True, stop=False)
                    with pe.Fori(0, rows) as i:
                        pe.wait_ge(hot, before + i + 1)
                        for j in range(SUB):
                            k = ((before + i) % RING) * SUB + j
                            ins = nc.tensor.matmul(out, hots_l[0:P, bass.ds(k, 1), 0:P], hots_g[0:P, bass.ds(k, 1), 0:W],
                                             start=False, stop=False)
                        ins.then_inc(used, 1)
                    nc.tensor.matmul(out, zeros[0:P, 0:P], iota[0:P, 0:W].bitcast(BF16), start=False,
                                     stop=True).then_inc(window_done, 1)

        @block.scalar
        def _(act):
            act.wait_ge(const, 3)
            act.sem_inc(window_free, 2)
            with act.Fori(0, WINDOWS // 2) as ww:
                for par in range(2):
                    w = ww * 2 + par
                    act.wait_ge(window_done, w + 1)
                    nc.scalar.activation(c.adj[0:P, :, bass.ds(w * (W // T), W // T)],
                                         c.ps[0:P, par, 0:W].rearrange("p (d t) -> p t d", t=T),
                                         ACT.Copy).then_inc(window_free, 1)



def stage_layernorm(c, of, to):
    nc = c.nc
    stats = c.small[0:P, 0:60].rearrange("p (t s) -> p t s", t=T)
    mv = c.small[0:P, 60:80].rearrange("p (t s) -> p t s", t=T)
    root = c.small[0:P, 80:90]
    inverse = c.small[0:P, 90:100]
    with ExitStack() as s:
        sem = lambda n: c.semaphore(n)
        stats_done, moments, shifted, rooted, inverted = map(sem, (
            "stats_done", "moments", "shifted", "rooted", "inverted"))
        block = s.enter_context(nc.Block())

        @block.scalar
        def _(act):
            act.wait_ge(shifted, 1)
            nc.scalar.activation(root, root, ACT.Sqrt).then_inc(rooted, 1)

        @block.vector
        def _(v):
            for t in range(T):
                nc.vector.bn_stats(stats[:, t, :], of[0:P, t, :]).then_inc(stats_done, 1)
            for t in range(T):
                v.wait_ge(stats_done, t + 1)
                nc.vector.bn_aggr(mv[:, t, :], stats[:, t, :]).then_inc(moments, 1)
            v.wait_ge(moments, T)
            nc.vector.tensor_scalar(root, mv[:, :, 1], EPS, None, ALU.add).then_inc(shifted, 1)
            v.wait_ge(rooted, 1)
            nc.vector.reciprocal(inverse, root).then_inc(inverted, 1)
            v.wait_ge(inverted, 1)
            for t in range(T):
                nc.vector.tensor_scalar(to[0:P, t, :], of[0:P, t, :], mv[:, t, 0:1], inverse[:, t:t + 1],
                                        ALU.subtract, ALU.mult)


def tiles_on_tensor(c, tiles, loads=(), only_vector=False):
    nc = c.nc
    with ExitStack() as s:
        sem = lambda n: c.semaphore(n)
        made, scalar_out, vector_out, scalar_step, vector_step, loaded = map(sem, (
            "made", "scalar_out", "vector_out", "scalar_step", "vector_step", "loaded"))
        block = s.enter_context(nc.Block())

        @block.sync
        def _(sp):
            for to, of in loads:
                sp.dma_start(to, of).then_inc(loaded, 16)
            if loads:
                sp.wait_ge(loaded, 16 * len(loads))

        @block.tensor
        def _(pe):
            for g, (rows, cols, parts, _) in enumerate(tiles):
                if g >= 8:
                    if only_vector:
                        pe.wait_ge(vector_out, g - 7)
                    else:
                        pe.wait_ge(vector_out if g % 2 else scalar_out, (g - 8) // 2 + 1)
                ps = c.ps[0:rows, g % 8, 0:cols]
                if isinstance(parts, tuple) and parts[0] == "turn":
                    for k, of in enumerate(parts[1]):
                        r, w = of.shape
                        ins = nc.tensor.transpose(ps[0:w, k * r:(k + 1) * r], of, c.ident[0:r, 0:r])
                else:
                    for k, (l, r) in enumerate(parts):
                        ins = nc.tensor.matmul(ps, l, r, start=(k == 0), stop=(k == len(parts) - 1))
                ins.then_inc(made, 1)

        def copies(engine, first, step, out):
            count = [0]

            def link(ins):
                count[0] += 1
                ins.then_inc(step, 1)
                engine.wait_ge(step, count[0])

            for g in range(first, len(tiles), 1 if only_vector else 2):
                engine.wait_ge(made, g + 1)
                rows, cols, _, copy = tiles[g]
                copy(engine, c.ps[0:rows, g % 8, 0:cols], link).then_inc(out, 1)

        if not only_vector:
            @block.scalar
            def _(act):
                copies(act, 0, scalar_step, scalar_out)

        @block.vector
        def _(v):
            copies(v, 0 if only_vector else 1, vector_step, vector_out)


def is_scalar(engine):
    return engine.engine == mybir.EngineType.Activation


def copy_to(to):
    def copy(e, ps, link):
        return e.activation(to, ps, ACT.Copy) if is_scalar(e) else e.tensor_copy(to, ps)
    return copy


def scaled_to(to, scale, bias=None):
    def copy(e, ps, link):
        if is_scalar(e):
            return e.activation(to, ps, ACT.Identity, scale=scale, bias=0.0 if bias is None else bias)
        if bias is None:
            return e.tensor_scalar(to, ps, scale, None, ALU.mult)
        return e.tensor_scalar(to, ps, scale, bias, ALU.mult, ALU.add)
    return copy


def biased_to(to, bias, relu=False):
    def copy(e, ps, link):
        if is_scalar(e):
            return e.activation(to, ps, ACT.Relu if relu else ACT.Identity, bias=bias)
        return e.tensor_scalar(to, ps, bias, 0.0 if relu else None, ALU.add, ALU.max if relu else ALU.bypass)
    return copy


def turn(of, to, post=None):
    out = []
    for k in range(KC):
        for t0 in range(0, T, 4):
            n = min(4, T - t0)
            where = to[:, k, t0 * P:(t0 + n) * P]
            out.append((128, n * P, ("turn", [of[0:P, t, 128 * k:128 * k + 128] for t in range(t0, t0 + n)]),
                        post(k, where) if post else copy_to(where)))
    return out


def turned_product(w, of, rows, copy, kc=KC):
    return [(min(128, rows - 128 * m), n, [(w[:, k, 128 * m:min(rows, 128 * m + 128)], of[:, k, c0:c0 + n]) for k in range(kc)],
             copy(m, slice(c0, c0 + n))) for m in range((rows + 127) // 128) for c0, n in COLS]


def natural_product(of, w, copy, kc=KC):
    return [(P, w.shape[2], [(of[:, k, t * P:t * P + P], w[:, k, :]) for k in range(kc)], copy(t)) for t in range(T)]


def weight(c, slot, of):
    return (c.w[:, slot], of.rearrange("(k p) n -> p k n", p=128))


def column(ap, n=KC):
    return ap.rearrange("(k p) -> p k", k=n)


def stage_degrees(c):
    nc = c.nc
    sums = c.big[0:P, 0:N]
    with ExitStack() as s:
        sem = lambda n: c.semaphore(n)
        v_done, p_done, a_done = map(sem, ("v_done", "p_done", "a_done"))
        block = s.enter_context(nc.Block())

        @block.tensor
        def _(pe):
            pe.wait_ge(v_done, 1)
            for b, (c0, n) in enumerate(COLS):
                ins = nc.tensor.matmul(c.ps[:, b, 0:n], c.ones[0:P, :], sums[:, c0:c0 + n], start=True, stop=True)
            ins.then_inc(p_done, 1)
            pe.wait_ge(v_done, 6)
            for t in range(T):
                ins = nc.tensor.transpose(c.ps[0:P, 3 + t // 4, 128 * (t % 4):128 * (t % 4) + 128],
                                          c.inv_t[:, t * P:t * P + P], c.ident[:, :])
            ins.then_inc(p_done, 1)

        @block.vector
        def _(v):
            nc.vector.tensor_reduce(sums, c.adj[0:P].rearrange("p s d -> p d s"), AX.X, ALU.add).then_inc(v_done, 1)
            nc.vector.tensor_reduce(c.out_n[0:P, :], c.adj[0:P], AX.X, ALU.add).then_inc(v_done, 1)
            v.wait_ge(p_done, 1)
            for b, (c0, n) in enumerate(COLS):
                ins = nc.vector.tensor_scalar(c.inv_t[:, c0:c0 + n], c.ps[:, b, 0:n], 1.0, None, ALU.max)
            ins.then_inc(v_done, 1)
            v.wait_ge(v_done, 3)
            nc.vector.tensor_scalar(c.out_n[0:P, :], c.out_n[0:P, :], 1.0, None, ALU.add).then_inc(v_done, 1)
            v.wait_ge(v_done, 4)
            nc.vector.reciprocal(c.inv_t[:, :], c.inv_t[:, :]).then_inc(v_done, 1)
            v.wait_ge(v_done, 5)
            nc.vector.tensor_copy(c.small[0:1, 511:512], c.inv_t[0:1, 0:1]).then_inc(v_done, 1)
            v.wait_ge(p_done, 2)
            nc.vector.tensor_copy(c.inv_n[0:P, 0:8].rearrange("p (a b) -> p a b", a=2),
                                  c.ps[0:P, 3:5, :].rearrange("p a (b q) -> p a b q", q=128)[:, :, :, 0])
            nc.vector.tensor_copy(c.inv_n[0:P, 8:10], c.ps[0:P, 5, 0:256].rearrange("p (b q) -> p b q", q=128)[:, :, 0])
            v.wait_ge(a_done, 1)
            nc.vector.reciprocal(c.out_n[0:P, :], c.out_n[0:P, :])

        @block.scalar
        def _(act):
            act.wait_ge(v_done, 4)
            nc.scalar.activation(c.out_n[0:P, :], c.out_n[0:P, :], ACT.Sqrt).then_inc(a_done, 1)


def stage_l0_mix(c, a):
    qt = c.big[:, 0:5000].rearrange("p (k n) -> p k n", k=KC)
    kn = c.nat
    vn = c.big[:, 5000:5000 + T * D].rearrange("p (t d) -> p t d", t=T)
    wt = c.big[:, 10500:10500 + 2048].rearrange("p (k d) -> p k d", k=KC)
    tmp = c.big[:, 12600:12600 + 512 * 4].rearrange("p (b d) -> p b d", b=4)
    kv = c.big[:, 14700:14700 + 4 * 130].rearrange("p (k d) -> p k d", k=4)

    def elu(to):
        return to

    def turn_w(slot):
        return [(128, 512, ("turn", [c.w[:, slot, m, 128 * k:128 * k + 128] for m in range(KC)]),
                 copy_to(wt[:, k, :])) for k in range(KC)]

    tiles_on_tensor(c, turn_w(0))
    stage_elu(c, [(128, n, [(wt[:, k, 128 * m:128 * m + 128], c.xt[:, k, c0:c0 + n]) for k in range(KC)],
                   qt[:, m, c0:c0 + n]) for m in range(KC) for c0, n in COLS], tmp)
    tiles_on_tensor(c, turn_w(1))
    stage_elu(c, [(P, D, [(c.xt[:, k, t * P:t * P + P], wt[:, k, :]) for k in range(KC)], kn[0:P, t, :])
                  for t in range(T)], tmp)
    tiles_on_tensor(c, turn_w(2))
    tiles_on_tensor(c, natural_product(c.xt, wt, lambda t: scaled_to(vn[0:P, t, :], 1.0 / N)))

    def pair(p):
        def copy(e, ps, link):
            cp = (lambda o, i: e.activation(o, i, ACT.Copy)) if is_scalar(e) else e.tensor_copy
            cp(kv[0:64, p, 0:64], ps[0:64, 0:64])
            cp(kv[64:128, p, 64:128], ps[64:128, 64:128])
            cp(kv[0:64, p, 128:129], ps[0:64, 128:129])
            return cp(kv[64:128, p, 129:130], ps[64:128, 128:129])
        return copy
    memsets(c, [kv[:]])
    vo = c.w[0:P, 2].rearrange("p a b -> p (a b)")[:, 0:T * 132].rearrange("p (t q) -> p t q", q=132)
    for p in range(4):
        stage_pool_copy(c, vo, vn[0:P, :, 128 * p:128 * p + 128], p == 0)
        tiles_on_tensor(c, [(128, 132, [(kn[0:P, t, 128 * p:128 * p + 128], vo[:, t, :]) for t in range(T)], pair(p))])

    r = c.small[0:P, 0:512]

    def out(t, h):
        def copy(e, ps, link):
            v = c.nc.vector
            num = ps.rearrange("p (a q) -> p a q", q=130)
            link(v.tensor_scalar(r[:, 16 * h:16 * h + 4].rearrange("p (a q) -> p a q", a=2), num[:, :, 128:130], 1e-6, None, ALU.add))
            link(v.reciprocal(r[:, 16 * h + 4:16 * h + 8], r[:, 16 * h:16 * h + 4]))
            m = tmp[0:P, h, 0:256]
            link(v.tensor_tensor(m.rearrange("p (a b d) -> p a b d", a=2, b=2),
                                 num[:, :, 0:128].rearrange("p a (b d) -> p a b d", b=2),
                                 r[:, 16 * h + 4:16 * h + 8].rearrange("p (a b) -> p a b", a=2).unsqueeze(3).to_broadcast([P, 2, 2, 64]),
                                 ALU.mult))
            x = c.x[0:P, t, 256 * h:256 * h + 256]
            return v.scalar_tensor_tensor(x, m, float(N), x, ALU.mult, ALU.add)
        return copy
    on_vector(c, [(P, 260, [("pairs", 2 * h, t)], out(t, h)) for t in range(T) for h in range(2)], qt, kv)


def memsets(c, aps, value=0.0):
    nc = c.nc
    with nc.Block() as block:
        @block.gpsimd
        def _(pool):
            for ap in aps:
                nc.gpsimd.memset(ap, value)


def stage_pool_copy(c, to, of, ones):
    nc = c.nc
    with nc.Block() as block:
        @block.gpsimd
        def _(pool):
            if ones:
                nc.gpsimd.memset(to[:, :, 128:132], 1.0)
            nc.gpsimd.tensor_copy(to[:, :, 0:128], of)


def on_vector(c, tiles, qt, kv):
    nc = c.nc
    with ExitStack() as s:
        sem = lambda n: c.semaphore(n)
        made, out, step = map(sem, ("made", "out", "step"))
        block = s.enter_context(nc.Block())

        @block.tensor
        def _(pe):
            for g, (rows, cols, parts, _) in enumerate(tiles):
                if g >= 8:
                    pe.wait_ge(out, g - 7)
                _, p0, t = parts[0]
                for j in range(2):
                    ins = nc.tensor.matmul(c.ps[0:P, g % 8, 130 * j:130 * j + 130], qt[:, p0 + j, t * P:t * P + P],
                                           kv[:, p0 + j, :], start=True, stop=True)
                ins.then_inc(made, 1)

        @block.vector
        def _(v):
            count = [0]

            def link(ins):
                count[0] += 1
                ins.then_inc(step, 1)
                v.wait_ge(step, count[0])

            for g, (rows, cols, parts, copy) in enumerate(tiles):
                v.wait_ge(made, g + 1)
                copy(v, c.ps[0:rows, g % 8, 0:cols], link).then_inc(out, 1)


def stage_elu(c, tiles, tmp):
    nc = c.nc
    with ExitStack() as s:
        sem = lambda n: c.semaphore(n)
        made, low, exped, out = map(sem, ("made", "low", "exped", "out"))
        block = s.enter_context(nc.Block())

        @block.tensor
        def _(pe):
            for g, (rows, cols, parts, _) in enumerate(tiles):
                if g >= 8:
                    pe.wait_ge(out, g - 7)
                for k, (l, r) in enumerate(parts):
                    ins = nc.tensor.matmul(c.ps[0:rows, g % 8, 0:cols], l, r, start=(k == 0), stop=(k == len(parts) - 1))
                ins.then_inc(made, 1)

        @block.scalar
        def _(act):
            for g, (rows, cols, _, to) in enumerate(tiles):
                act.wait_ge(low, g + 1)
                t = tmp[0:rows, g % 4, 0:cols]
                nc.scalar.activation(t, t, ACT.Exp).then_inc(exped, 1)

        @block.vector
        def _(v):
            for g in range(len(tiles) + 2):
                if g < len(tiles):
                    rows, cols, _, to = tiles[g]
                    v.wait_ge(made, g + 1)
                    if g >= 4:
                        v.wait_ge(out, g - 3)
                    nc.vector.tensor_scalar(tmp[0:rows, g % 4, 0:cols], c.ps[0:rows, g % 8, 0:cols], 0.0, None,
                                            ALU.min).then_inc(low, 1)
                if g >= 2:
                    rows, cols, _, to = tiles[g - 2]
                    v.wait_ge(exped, g - 1)
                    nc.vector.scalar_tensor_tensor(to, c.ps[0:rows, (g - 2) % 8, 0:cols], 0.0,
                                                   tmp[0:rows, (g - 2) % 4, 0:cols], ALU.max, ALU.add).then_inc(out, 1)


def stage_aggregate(c, of_t, to_t, u, b, relu):
    nc = c.nc
    tmp = c.small
    tiles = [(m, c0, n) for m in range(KC) for c0, n in COLS]
    scratch = c.big[:, 12600:12600 + 1024].rearrange("p (b d) -> p b d", b=2)
    with ExitStack() as s:
        sem = lambda n: c.semaphore(n)
        made, mult, added, out = map(sem, ("made", "mult", "added", "out"))
        block = s.enter_context(nc.Block())

        @block.tensor
        def _(pe):
            for g, (m, c0, n) in enumerate(tiles):
                if g >= 4:
                    pe.wait_ge(out, g - 3)
                for t in range(T):
                    nc.tensor.matmul(c.ps[:, 2 * (g % 4), 0:n], u[0:P, t, 128 * m:128 * m + 128],
                                     c.adj[0:P, t, c0:c0 + n], start=(t == 0), stop=(t == T - 1))
                for k in range(KC):
                    ins = nc.tensor.matmul(c.ps[:, 2 * (g % 4) + 1, 0:n], c.w[:, 0, k, 128 * m:128 * m + 128],
                                           of_t[:, k, c0:c0 + n], start=(k == 0), stop=(k == KC - 1))
                ins.then_inc(made, 1)

        @block.vector
        def _(v):
            for g, (m, c0, n) in enumerate(tiles):
                v.wait_ge(made, g + 1)
                if g >= 2:
                    v.wait_ge(out, g - 1)
                t = scratch[:, g % 2, 0:n]
                nc.vector.tensor_tensor(t, c.ps[:, 2 * (g % 4), 0:n], c.inv_t[:, c0:c0 + n], ALU.mult).then_inc(mult, 1)
                v.wait_ge(mult, g + 1)
                nc.vector.tensor_tensor(t, t, c.ps[:, 2 * (g % 4) + 1, 0:n], ALU.add).then_inc(added, 1)

        @block.scalar
        def _(act):
            for g, (m, c0, n) in enumerate(tiles):
                act.wait_ge(added, g + 1)
                nc.scalar.activation(to_t[:, m, c0:c0 + n], scratch[:, g % 2, 0:n], ACT.Relu,
                                     bias=b[:, m:m + 1]).then_inc(out, 1)


def stage_aggregate_natural(c, of_t, u, b_all):
    nc = c.nc
    with ExitStack() as s:
        sem = lambda n: c.semaphore(n)
        made, step, out = map(sem, ("made", "step", "out"))
        block = s.enter_context(nc.Block())

        @block.tensor
        def _(pe):
            for g in range(T):
                if g >= 4:
                    pe.wait_ge(out, g - 3)
                for t in range(T):
                    nc.tensor.matmul(c.ps[0:P, 2 * (g % 4), :], c.adj[0:P, t, g * P:g * P + P], u[0:P, t, :],
                                     start=(t == 0), stop=(t == T - 1))
                for k in range(KC):
                    ins = nc.tensor.matmul(c.ps[0:P, 2 * (g % 4) + 1, :], of_t[:, k, g * P:g * P + P], c.w[:, 0, k, :],
                                           start=(k == 0), stop=(k == KC - 1))
                ins.then_inc(made, 1)

        @block.vector
        def _(v):
            for g in range(T):
                v.wait_ge(made, g + 1)
                x = c.x[0:P, g, :]
                nc.vector.scalar_tensor_tensor(x, c.ps[0:P, 2 * (g % 4), :], c.inv_n[0:P, g:g + 1], x, ALU.mult,
                                               ALU.add).then_inc(step, 1)
                v.wait_ge(step, 2 * g + 1)
                nc.vector.tensor_tensor(x, x, c.ps[0:P, 2 * (g % 4) + 1, :], ALU.add).then_inc(step, 1)
                v.wait_ge(step, 2 * g + 2)
                nc.vector.tensor_tensor(x, x, b_all, ALU.add).then_inc(out, 1)



def chain(engine, sem):
    count = [0]

    def link(ins):
        count[0] += 1
        ins.then_inc(sem, 1)
        engine.wait_ge(sem, count[0])
    return link


KEYS = [(0, 512), (512, 512), (1024, N - 1024)]
QUERIES = [(0, 4), (4, 4), (8, 2)]


def stage_attention_constants(c):
    nc = c.nc
    f = c.w[:, 2, 0]
    c.blockones = f[:, 0:128]
    c.minus = c.rounded[0:P, 3 * N:3 * N + 128]
    c.mask_n = f[0:P, 256:320].bitcast(BF16)[:, 0:P]
    c.mask_t = f[0:P, 320:384].bitcast(BF16)[:, 0:P]
    c.identb = f[0:P, 384:448].bitcast(BF16)[:, 0:P]
    with ExitStack() as s:
        a, b = (c.semaphore(n) for n in ("a", "b"))
        block = s.enter_context(nc.Block())

        @block.gpsimd
        def _(pool):
            nc.gpsimd.memset(c.blockones, 0.0).then_inc(a, 1)
            nc.gpsimd.memset(c.mask_n, 0.0).then_inc(a, 1)
            nc.gpsimd.memset(c.mask_t, 0.0).then_inc(a, 1)
            pool.wait_ge(a, 3)
            nc.gpsimd.affine_select(out=c.mask_n, in_=c.mask_n, compare_op=ALU.is_ge, fill=-3e38, base=0,
                                    pattern=[[-1, P]], channel_multiplier=1)
            nc.gpsimd.affine_select(out=c.mask_t, in_=c.mask_t, compare_op=ALU.is_ge, fill=-3e38, base=0,
                                    pattern=[[1, P]], channel_multiplier=-1)

        @block.vector
        def _(v):
            nc.vector.tensor_copy(c.identb, c.ident[0:P, 0:P])
            v.wait_ge(a, 3)
            nc.vector.memset(c.blockones[0:64, 0:64], 1.0)
            nc.vector.memset(c.blockones[64:128, 64:128], 1.0)
            nc.vector.tensor_scalar(c.minus, c.ones[0:P, 0:128], -1.0, None, ALU.mult)


def stage_unit(c, raw, rounded, gain, work):
    nc = c.nc
    with ExitStack() as s:
        sem = lambda n: c.semaphore(n)
        squared, summed, shifted, rooted, step = map(sem, ("squared", "summed", "shifted", "rooted", "step"))
        block = s.enter_context(nc.Block())

        @block.scalar
        def _(act):
            for b, (c0, n) in enumerate(COLS):
                nc.scalar.activation(work[:, c0:c0 + n], raw[:, c0:c0 + n], ACT.Square).then_inc(squared, 1)
            for b, (c0, n) in enumerate(COLS):
                act.wait_ge(shifted, b + 1)
                nc.scalar.activation(work[:, c0:c0 + n], work[:, c0:c0 + n], ACT.Sqrt).then_inc(rooted, 1)

        @block.tensor
        def _(pe):
            for b, (c0, n) in enumerate(COLS):
                pe.wait_ge(squared, b + 1)
                nc.tensor.matmul(c.ps[:, b, 0:n], c.blockones, work[:, c0:c0 + n], start=True, stop=True).then_inc(summed, 1)

        @block.vector
        def _(v):
            link = chain(v, step)
            for b, (c0, n) in enumerate(COLS):
                v.wait_ge(summed, b + 1)
                nc.vector.tensor_scalar(work[:, c0:c0 + n], c.ps[:, b, 0:n], 1e-12, None, ALU.add).then_inc(shifted, 1)
            for b, (c0, n) in enumerate(COLS):
                v.wait_ge(rooted, b + 1)
                link(nc.vector.reciprocal(work[:, c0:c0 + n], work[:, c0:c0 + n]))
                link(nc.vector.scalar_tensor_tensor(raw[:, c0:c0 + n], raw[:, c0:c0 + n], gain,
                                                    work[:, c0:c0 + n], ALU.mult, ALU.mult))
                nc.vector.tensor_copy(rounded[:, c0:c0 + n], raw[:, c0:c0 + n])


def stage_head(c, h, qt, kt, qr, kr, dm, pr, va, ot, rd):
    nc = c.nc
    lo = 64 * (h % 2)
    hi = 64 - lo
    mx = c.small[0:P, 0:T]
    flat = c.ps.ap().rearrange("p b n -> p (b n)") if hasattr(c.ps, "ap") else c.ps[:].rearrange("p b n -> p (b n)")
    turns = [(q, i0, ni, j) for q, (i0, ni) in enumerate(QUERIES) for j in range(i0 + ni)]
    with ExitStack() as s:
        sem = lambda n: c.semaphore(n)
        copied, scored, maxed, diag, turned, exped, summed, divided, step = map(sem, (
            "copied", "scored", "maxed", "diag", "turned", "exped", "summed", "divided", "step"))
        block = s.enter_context(nc.Block())

        @block.gpsimd
        def _(pool):
            nc.gpsimd.memset(va[:, :, hi:hi + 64], 1.0).then_inc(copied, 1)
            nc.gpsimd.tensor_copy(va[:, :, lo:lo + 64], c.nat[0:P, :, 64 * h:64 * h + 64]).then_inc(copied, 1)

        @block.tensor
        def _(pe):
            for i in range(T):
                if i >= 2:
                    pe.wait_ge(maxed, i - 1)
                width = P * (i + 1)
                for b, (c0, n) in enumerate(KEYS):
                    if c0 >= width:
                        continue
                    w = min(n, width - c0)
                    d0, d1 = max(P * i, c0), min(width, c0 + n)
                    bank = 4 * (i % 2) + b
                    diagonal = d1 > d0
                    ins = nc.tensor.matmul(c.ps[0:P, bank, 0:w + w % 2], qr[lo:lo + 64, P * i:P * i + P],
                                           kr[lo:lo + 64, c0:c0 + w + w % 2], start=True, stop=not diagonal)
                    if diagonal:
                        ins = nc.tensor.matmul(c.ps[0:P, bank, d0 - c0:d1 - c0], c.identb, c.mask_n[:, d0 - P * i:d1 - P * i],
                                               start=False, stop=True)
                ins.then_inc(scored, 1)
            pe.wait_ge(diag, 1)
            pe.wait_ge(copied, 2)

            def weigh(g):
                q, i0, ni, j = turns[g]
                s0 = max(i0, j) * P
                w = (i0 + ni) * P - s0
                pe.wait_ge(exped, g + 1)
                if j == 0 and q >= 2:
                    pe.wait_ge(divided, q - 1)
                ins = nc.tensor.matmul(c.ps[:, 4 + q % 2, s0 - i0 * P:s0 - i0 * P + w], va[:, j, :], pr[:, g % 4, 0:w],
                                       start=(j == 0), stop=(j == i0 + ni - 1))
                ins.then_inc(summed, 1)

            for g, (q, i0, ni, j) in enumerate(turns):
                s0 = max(i0, j) * P
                w = (i0 + ni) * P - s0
                odd = w % 2
                if g >= 4:
                    pe.wait_ge(exped, g - 3)
                out = c.ps[0:P, g % 4, 0:w + odd]
                nc.tensor.matmul(out, kt[lo:lo + 64, j * P:j * P + P], qt[lo:lo + 64, s0 - odd:s0 + w], start=True, stop=False)
                ins = nc.tensor.matmul(out, c.minus[:, 0:P], dm[:, s0 - odd:s0 + w], start=False, stop=(j < i0))
                if j >= i0:
                    ins = nc.tensor.matmul(c.ps[0:P, g % 4, odd:odd + P], c.identb, c.mask_t, start=False, stop=True)
                ins.then_inc(turned, 1)
                if g >= 2:
                    weigh(g - 2)
            weigh(len(turns) - 2)
            weigh(len(turns) - 1)

        @block.scalar
        def _(act):
            for g, (q, i0, ni, j) in enumerate(turns):
                s0 = max(i0, j) * P
                w = (i0 + ni) * P - s0
                act.wait_ge(turned, g + 1)
                if g >= 4:
                    act.wait_ge(summed, g - 3)
                nc.scalar.activation(pr[:, g % 4, 0:w], c.ps[0:P, g % 4, w % 2:w % 2 + w], ACT.Exp).then_inc(exped, 1)

        @block.vector
        def _(v):
            link = chain(v, step)
            for i in range(T):
                v.wait_ge(scored, i + 1)
                nc.vector.tensor_reduce(mx[:, i:i + 1], flat[0:P, 2048 * (i % 2):2048 * (i % 2) + P * (i + 1)], AX.X,
                                        ALU.max).then_inc(maxed, 1)
            v.wait_ge(maxed, T)
            nc.vector.tensor_tensor(dm.rearrange("p (i q) -> p i q", q=P),
                                    c.ident[0:P, 0:P].unsqueeze(1).to_broadcast([P, T, P]),
                                    mx.unsqueeze(2).to_broadcast([P, T, P]), ALU.mult).then_inc(diag, 1)
            done = 0
            for q, (i0, ni) in enumerate(QUERIES):
                done += i0 + ni
                v.wait_ge(summed, done)
                cols = slice(i0 * P, (i0 + ni) * P)
                ps = c.ps[:, 4 + q % 2, 0:ni * P]
                link(nc.vector.reciprocal(rd[lo:lo + 64, 0:ni * P], ps[hi:hi + 64]))
                ins = nc.vector.tensor_tensor(ot[lo:lo + 64, cols], ps[lo:lo + 64], rd[lo:lo + 64, 0:ni * P], ALU.mult)
                ins.then_inc(divided, 1)
                v.wait_ge(divided, q + 1)


def stage_gate(c, logits, coef):
    nc = c.nc
    s8 = [P, T, 8]
    red = c.small[0:P, 200:230].rearrange("p (a t) -> p a t", a=3)
    with ExitStack() as s:
        a, b = (c.semaphore(n) for n in ("a", "b"))
        block = s.enter_context(nc.Block())

        @block.vector
        def _(v):
            link = chain(v, a)
            link(nc.vector.tensor_reduce(red[:, 0, :], logits, AX.X, ALU.max))
            link(nc.vector.tensor_tensor(coef, logits, red[:, 0, :].unsqueeze(2).to_broadcast(s8), ALU.subtract))
            v.wait_ge(b, 1)
            link(nc.vector.tensor_reduce(red[:, 1, :], coef, AX.X, ALU.add))
            link(nc.vector.reciprocal(red[:, 2, :], red[:, 1, :]))
            link(nc.vector.tensor_tensor(coef, coef, red[:, 2, :].unsqueeze(2).to_broadcast(s8), ALU.mult))

        @block.scalar
        def _(act):
            act.wait_ge(a, 2)
            nc.scalar.activation(coef, coef, ACT.Exp).then_inc(b, 1)


CAPACITY = 512


def stage_route(c, logits, coef, work):
    nc = c.nc
    s8 = [P, T, 8]
    f = work[0:P, 0:20 * 80].rearrange("p (a t e) -> p a t e", a=20, t=T)
    expert, left, same, key, one, two, both, slots, keep, spare = (f[:, k] for k in range(10))
    r = f[:, 10].rearrange("p t e -> p (t e)").rearrange("p (a t) -> p a t", t=T)
    m1, i1, m2, i2, d, e, w1, w2 = (r[:, k] for k in range(8))
    upper = work[0:P, 1700:1825]
    wide = lambda x: x.unsqueeze(2).to_broadcast(s8)
    with ExitStack() as s:
        sem = lambda n: c.semaphore(n)
        consts, step, counted, exped, step2 = map(sem, ("consts", "step", "counted", "exped", "step2"))
        block = s.enter_context(nc.Block())

        @block.gpsimd
        def _(pool):
            nc.gpsimd.iota(expert, [[0, T], [1, 8]], base=0, channel_multiplier=0,
                           allow_small_or_imprecise_dtypes=True).then_inc(consts, 1)
            nc.gpsimd.memset(upper, 1.0).then_inc(consts, 1)
            pool.wait_ge(consts, 2)
            nc.gpsimd.affine_select(out=upper, in_=upper, compare_op=ALU.is_gt, fill=0.0, base=0,
                                    pattern=[[1, P]], channel_multiplier=-1).then_inc(consts, 1)

        @block.vector
        def _(v):
            link = chain(v, step)
            v.wait_ge(consts, 3)

            def first(of, m, i, hot):
                link(nc.vector.tensor_reduce(m, of, AX.X, ALU.max))
                link(nc.vector.tensor_tensor(same, of, wide(m), ALU.is_equal))
                link(nc.vector.scalar_tensor_tensor(key, same, -100.0, expert, ALU.mult, ALU.add))
                link(nc.vector.tensor_reduce(i, key, AX.X, ALU.min))
                link(nc.vector.tensor_tensor(hot, key, wide(i), ALU.is_equal))

            first(logits, m1, i1, one)
            link(nc.vector.tensor_scalar(spare, one, -1.0, 1.0, ALU.mult, ALU.add))
            link(nc.vector.tensor_tensor(left, logits, spare, ALU.mult))
            link(nc.vector.scalar_tensor_tensor(left, one, -3e38, left, ALU.mult, ALU.add))
            first(left, m2, i2, two)
            link(nc.vector.tensor_tensor(both, one, two, ALU.add))
            link(nc.vector.tensor_tensor(d, m2, m1, ALU.subtract))
            v.wait_ge(exped, 1)
            link(nc.vector.tensor_scalar(w1, e, 1.0, None, ALU.add))
            link(nc.vector.reciprocal(w1, w1))
            link(nc.vector.tensor_tensor(w2, e, w1, ALU.mult))
            v.wait_ge(counted, 1)
            link(nc.vector.memset(spare[:, 0, :], 0.0))
            for t in range(1, T):
                link(nc.vector.tensor_tensor(spare[:, t, :], spare[:, t - 1, :], c.ps[0:P, 1, 8 * t - 8:8 * t], ALU.add))
            link(nc.vector.tensor_tensor(slots, spare, c.ps[0:P, 0, 0:80].rearrange("p (t e) -> p t e", e=8), ALU.add))
            link(nc.vector.tensor_scalar(keep, slots, float(CAPACITY), None, ALU.is_lt))
            link(nc.vector.tensor_tensor(one, one, wide(w1), ALU.mult))
            link(nc.vector.tensor_tensor(two, two, wide(w2), ALU.mult))
            link(nc.vector.tensor_tensor(one, one, two, ALU.add))
            link(nc.vector.tensor_tensor(coef, one, keep, ALU.mult))

        @block.scalar
        def _(act):
            act.wait_ge(step, 5 + 3 + 5 + 2)
            nc.scalar.activation(e, d, ACT.Exp).then_inc(exped, 1)

        @block.tensor
        def _(pe):
            pe.wait_ge(step, 5 + 3 + 5 + 1)
            flat = both.rearrange("p t e -> p (t e)")
            nc.tensor.matmul(c.ps[0:P, 0, 0:80], upper, flat, start=True, stop=True)
            nc.tensor.matmul(c.ps[0:P, 1, 0:80], c.ones[0:P, 0:P], flat, start=True, stop=True).then_inc(counted, 1)


def stage_experts(c, yt, coef, b1, w1_d, w2_d, hid):
    nc = c.nc
    w1 = [c.w[:, p].rearrange("p k d -> p (k d)")[:, 0:1024].rearrange("p (k f) -> p k f", k=KC) for p in range(2)]
    w2 = [c.w[:, p].rearrange("p k d -> p (k d)")[:, 1024:2048].rearrange("p (k f) -> p k f", k=2) for p in range(2)]
    with ExitStack() as s:
        sem = lambda n: c.semaphore(n)
        names = ("loaded0", "loaded1", "hid_made", "hid_out", "eo_made", "eo_out", "biased")
        loaded0, loaded1, hid_made, hid_out, eo_made, eo_out, biased = map(sem, names)
        loaded = (loaded0, loaded1)
        block = s.enter_context(nc.Block())

        @block.sync
        def _(sp):
            def load(e, par):
                sp.dma_start(w1[par], w1_d[bass.ds(e, 1)].rearrange("a (k p) f -> p (a k) f", p=128)).then_inc(loaded[par], 16)
                sp.dma_start(w2[par], w2_d[bass.ds(e, 1)].rearrange("a (k p) f -> p (a k) f", p=128)).then_inc(loaded[par], 16)

            load(0, 0)
            load(1, 1)
            with sp.Fori(1, 4) as i:
                for par in range(2):
                    sp.wait_ge(eo_made, i * (2 * T) + (par - 1) * T)
                    load(i * 2 + par, par)

        @block.tensor
        def _(pe):
            with pe.Fori(0, 4) as i:
                for par in range(2):
                    e = i * 2 + par
                    pe.wait_ge(loaded[par], i * 32 + 32)
                    for q, (f, (c0, n)) in enumerate((f, cols) for f in range(2) for cols in COLS):
                        pe.wait_ge(hid_out, e * 6 + (q + 1))
                        for k in range(KC):
                            ins = nc.tensor.matmul(c.ps[:, q % 3, 0:n], w1[par][:, k, 128 * f:128 * f + 128],
                                                   yt[:, k, c0:c0 + n], start=(k == 0), stop=(k == KC - 1))
                        ins.then_inc(hid_made, 1)
                    for t in range(T):
                        if t == 0:
                            pe.wait_ge(hid_out, e * 6 + 9)
                        pe.wait_ge(eo_out, e * T + (t + 1))
                        for f in range(2):
                            ins = nc.tensor.matmul(c.ps[0:P, 3 + t % 5, :], hid[par][:, f, t * P:t * P + P], w2[par][:, f, :],
                                                   start=(f == 0), stop=(f == 1))
                        ins.then_inc(eo_made, 1)

        @block.scalar
        def _(act):
            act.sem_inc(hid_out, 3)
            with act.Fori(0, 4) as i:
                for par in range(2):
                    e = i * 2 + par
                    bias = b1[:, 16 + 2 * par:18 + 2 * par]
                    nc.scalar.activation(bias, b1[:, bass.ds(e * 2, 2)], ACT.Copy).then_inc(biased, 1)
                    act.wait_ge(biased, e + 1)
                    for q, (f, (c0, n)) in enumerate((f, cols) for f in range(2) for cols in COLS):
                        act.wait_ge(hid_made, e * 6 + (q + 1))
                        nc.scalar.activation(hid[par][:, f, c0:c0 + n], c.ps[:, q % 3, 0:n], ACT.Gelu_apprx_tanh,
                                             bias=bias[:, f:f + 1]).then_inc(hid_out, 1)

        @block.vector
        def _(v):
            v.sem_inc(eo_out, 5)
            with v.Fori(0, 4) as i:
                for par in range(2):
                    e = i * 2 + par
                    for t in range(T):
                        v.wait_ge(eo_made, e * T + (t + 1))
                        x = c.x[0:P, t, :]
                        nc.vector.scalar_tensor_tensor(x, c.ps[0:P, 3 + t % 5, :], coef[:, t, bass.ds(e, 1)], x,
                                                       ALU.mult, ALU.add).then_inc(eo_out, 1)


def add_to_x(c, t, extra=None, scale=None, relu=False):
    def copy(e, ps, link):
        x = c.x[0:P, t, :]
        v = c.nc.vector
        if relu:
            m = c.big[0:P, 12600 + 512 * (t % 2):13112 + 512 * (t % 2)]
            link(v.tensor_scalar(m, ps, scale, 0.0, ALU.mult, ALU.max))
            return v.tensor_tensor(x, x, m, ALU.add)
        if extra is not None:
            link(v.tensor_tensor(x, x, extra, ALU.add))
        return v.tensor_tensor(x, x, ps, ALU.add)
    return copy


def mixture(c, a, pre, yt, gate_w, gate_b, b1_d, w1_d, w2_d, b2_d, route, base):
    big = c.big
    lt = big[0:8, base:base + N]
    coef_t = big[0:8, base + N:base + 2 * N]
    coef = big[0:P, base + 2 * N:base + 2 * N + 80].rearrange("p (t e) -> p t e", e=8)
    logits = big[0:P, base + 2 * N + 80:base + 2 * N + 160].rearrange("p (t e) -> p t e", e=8)
    b1 = big[:, base + 2 * N + 722:base + 2 * N + 742]
    b2 = big[0:8, base + 2 * N + 176:base + 2 * N + 688]
    gw = big[:, base + 2 * N + 688:base + 2 * N + 720].rearrange("p (k e) -> p k e", k=KC)
    gb = big[0:8, base + 2 * N + 720:base + 2 * N + 721]
    hid = [big[:, 5000 + 2500 * k:7500 + 2500 * k].rearrange("p (f n) -> p f n", f=2) for k in range(2)]
    c.recycle()
    loads = [(gw, gate_w.rearrange("(k p) e -> p k e", p=128)), (b1[:, 0:16], b1_d.rearrange("e (f p) -> p (e f)", p=128)), (b2, b2_d)]
    if gate_b is not None:
        loads.append((gb, gate_b.rearrange("(e o) -> e o", o=1)))
    tiles_on_tensor(c, [], loads)
    if gate_b is not None:
        copies = lambda m, cols: biased_to(lt[:, cols], gb)
    else:
        copies = lambda m, cols: copy_to(lt[:, cols])
    tiles_on_tensor(c, turned_product(gw, yt, 8, copies))
    tiles_on_tensor(c, [(P, 80, ("turn", [lt[:, t * P:t * P + P] for t in range(T)]),
                         copy_to(logits.rearrange("p t e -> p (t e)")))])
    if route:
        stage_route(c, logits, coef, big[:, 5000:7500])
    else:
        stage_gate(c, logits, coef)
    tiles_on_tensor(c, [(8, n * P, ("turn", [coef[:, t, :] for t in range(t0, t0 + n)]),
                         copy_to(coef_t[:, t0 * P:(t0 + n) * P])) for t0, n in QUERIES])
    tiles_on_tensor(c, [(P, D, [(coef_t[:, t * P:t * P + P], b2)], add_to_x(c, t)) for t in range(T)], only_vector=True)
    stage_experts(c, yt, coef, b1, w1_d, w2_d, hid)


def stage_loop_add_identity(c, b):
    nc = c.nc
    with nc.Block() as block:
        @block.vector
        def _(v):
            for i in range(T):
                d = b[:, i, P * i:P * i + P]
                nc.vector.tensor_tensor(d, d, c.ident[0:P, 0:P], ALU.add)


def stage_key_softmax(c, ke):
    nc = c.nc
    r = c.small[:, 0:8]
    with ExitStack() as s:
        a, b = (c.semaphore(n) for n in ("a", "b"))
        block = s.enter_context(nc.Block())

        @block.vector
        def _(v):
            link = chain(v, a)
            link(nc.vector.tensor_reduce(r[:, 0:2], ke, AX.X, ALU.max))
            link(nc.vector.tensor_scalar(r[:, 2:4], r[:, 0:2], -1.0, None, ALU.mult))
            v.wait_ge(b, 2)
            link(nc.vector.reciprocal(r[:, 6:8], r[:, 4:6]))
            for g in range(2):
                nc.vector.tensor_scalar(ke[:, g, :], ke[:, g, :], r[:, 6 + g:7 + g], None, ALU.mult)

        @block.scalar
        def _(act):
            act.wait_ge(a, 2)
            for g in range(2):
                nc.scalar.activation(ke[:, g, :], ke[:, g, :], ACT.Exp, bias=r[:, 2 + g:3 + g],
                                     accum_out=r[:, 4 + g:5 + g]).then_inc(b, 1)


def stage_query_softmax(c, q):
    nc = c.nc
    g = q.rearrange("p t (h s) -> p (t h) s", s=32)
    r = c.small[0:P, 0:240].rearrange("p (a k) -> p a k", a=3)
    wide = lambda x: x.unsqueeze(2).to_broadcast([P, 80, 32])
    with ExitStack() as s:
        a, b = (c.semaphore(n) for n in ("a", "b"))
        block = s.enter_context(nc.Block())

        @block.vector
        def _(v):
            link = chain(v, a)
            link(nc.vector.tensor_reduce(r[:, 0, :], g, AX.X, ALU.max))
            link(nc.vector.tensor_tensor(g, g, wide(r[:, 0, :]), ALU.subtract))
            v.wait_ge(b, 1)
            link(nc.vector.tensor_reduce(r[:, 1, :], g, AX.X, ALU.add))
            link(nc.vector.reciprocal(r[:, 2, :], r[:, 1, :]))
            link(nc.vector.tensor_tensor(g, g, wide(r[:, 2, :]), ALU.mult))

        @block.scalar
        def _(act):
            act.wait_ge(a, 2)
            nc.scalar.activation(q, q, ACT.Exp).then_inc(b, 1)


def stage_l1_mix(c, a):
    big = c.big
    adj = c.adj[:].rearrange("p s d -> p (s d)")
    xm = big[:, 0:5000].rearrange("p (k n) -> p k n", k=KC)
    ke = big[:, 5000:7500].rearrange("p (g n) -> p g n", g=2)
    wk = big[:, 7500:7756].rearrange("p (a s) -> p a s", a=2)
    wqv = big[:, 7756:7948]
    kvb = big[:, 7948:8460].rearrange("p (g d) -> p g d", g=2)
    b_in = big[:, 8460:8464]
    b_out = big[0:P, 8470:8982]
    out_t = big[:, 9000:14000].rearrange("p (k n) -> p k n", k=KC)
    qn = adj[0:P, 0:2560].rearrange("p (t s) -> p t s", t=T)
    kn = adj[0:P, 2560:5120].rearrange("p (t s) -> p t s", t=T)
    qt = adj[:, 5200:7700].rearrange("p (g n) -> p g n", g=2)
    vn = c.nat
    memsets(c, [wk, wqv, kvb])
    loads = [weight(c, 0, a["L1_mix_W_in"]), weight(c, 1, a["L1_mix_W_out"]), (b_in, column(a["L1_mix_b_in"])),
             (b_out, a["L1_mix_b_out"].partition_broadcast(P))]
    for h in range(2):
        rows = slice(64 * h, 64 * h + 64)
        for k in range(2):
            loads.append((wk[rows, k, 64 * k + 32 * h:64 * k + 32 * h + 32], a["L1_mix_Wk"]))
        loads.append((wqv[rows, 32 * h:32 * h + 32], a["L1_mix_Wq"]))
        loads.append((wqv[rows, 64 + 64 * h:128 + 64 * h], a["L1_mix_Wv"]))
    tiles_on_tensor(c, [], loads)
    tiles_on_tensor(c, turned_product(c.w[:, 0], c.xt, D, lambda m, cols: biased_to(xm[:, m, cols], b_in[:, m:m + 1])))
    tiles_on_tensor(c, [(128, n, [(wk[:, k, :], xm[:, 2 * g + k, c0:c0 + n]) for k in range(2)],
                         copy_to(ke[:, g, c0:c0 + n])) for g in range(2) for c0, n in COLS])

    def qv(t, m):
        def copy(e, ps, link):
            cp = (lambda o, i: e.activation(o, i, ACT.Copy)) if is_scalar(e) else e.tensor_copy
            cp(qn[:, t, 64 * m:64 * m + 64], ps[:, 0:64])
            return cp(vn[0:P, t, 128 * m:128 * m + 128], ps[:, 64:192])
        return copy
    tiles_on_tensor(c, [(P, 192, [(xm[:, m, t * P:t * P + P], wqv)], qv(t, m)) for t in range(T) for m in range(KC)])
    c.recycle()
    stage_key_softmax(c, ke)
    stage_query_softmax(c, qn)
    tiles_on_tensor(c, [(P, 256, ("turn", [ke[:, g, t * P:t * P + P] for g in range(2)]), copy_to(kn[:, t, :]))
                        for t in range(T)])

    def blocks(g):
        def copy(e, ps, link):
            cp = (lambda o, i: e.activation(o, i, ACT.Copy)) if is_scalar(e) else e.tensor_copy
            for h in range(4):
                ins = cp(kvb[32 * h:32 * h + 32, g, 64 * h:64 * h + 64], ps[32 * h:32 * h + 32, 64 * h:64 * h + 64])
            return ins
        return copy
    tiles_on_tensor(c, [(128, 256, [(kn[:, t, 128 * g:128 * g + 128], vn[0:P, t, 256 * g:256 * g + 256]) for t in range(T)],
                         blocks(g)) for g in range(2)])
    tiles_on_tensor(c, [(128, n * P, ("turn", [qn[:, t, 128 * g:128 * g + 128] for t in range(t0, t0 + n)]),
                         copy_to(qt[:, g, t0 * P:(t0 + n) * P])) for g in range(2) for t0, n in QUERIES])
    tiles_on_tensor(c, [(128, n, [(kvb[:, m // 2, 128 * (m % 2):128 * (m % 2) + 128], qt[:, m // 2, c0:c0 + n])],
                         copy_to(out_t[:, m, c0:c0 + n])) for m in range(KC) for c0, n in COLS])
    tiles_on_tensor(c, natural_product(out_t, c.w[:, 1], lambda t: add_to_x(c, t, extra=b_out)), only_vector=True)


STOP = 9


def build(nc, a, out):
    with ExitStack() as ctx:
        ctx.enter_context(nc.allow_non_contiguous_dma(reason="bias and gain vectors of 512 values, by feature"))
        c = Chip(nc, ctx)
        layer0_graph(c, a)
        layer0_attention(c, a)
        layer1(c, a)
        finish(c, out)


def layer0_graph(c, a):
    with ExitStack() as ctx:
        big = c.work(ctx, "big_graph", 17500)
        c.inv_t = big[:, 16250:17500]
        wq, wkv = a["L0_mix_Wq"], a["L0_mix_Wkv"]
        stage_prepare(c, a["x"], a["src"], a["dst"], [weight(c, 0, wq), weight(c, 1, wkv[0:D]), weight(c, 2, wkv[D:2 * D])])
        stage_adjacency(c)
        stage_degrees(c)
        c.recycle()
        stage_layernorm(c, c.x, c.nat)
        tiles_on_tensor(c, turn(c.nat, c.xt))
        stage_l0_mix(c, a)
        c.recycle()
        ha = big[:, 0:5000].rearrange("p (k n) -> p k n", k=KC)
        hb = big[:, 5000:10000].rearrange("p (k n) -> p k n", k=KC)
        b_all = big[0:P, 14700:15212]
        h = c.xt
        for layer in range(3):
            loads = [weight(c, 0, a["L0_gnn_Ws_self"][layer]), weight(c, 1, a["L0_gnn_Ws_neigh"][layer])]
            loads.append((b_all, a["L0_gnn_bs"][2].partition_broadcast(P)) if layer == 2 else
                         (c.gain[:, 0:KC], column(a["L0_gnn_bs"][layer])))
            tiles_on_tensor(c, [], loads)
            tiles_on_tensor(c, natural_product(h, c.w[:, 1], lambda t: copy_to(c.nat[0:P, t, :])))
            if layer < 2:
                to = (ha, hb)[layer]
                stage_aggregate(c, h, to, c.nat, c.gain, True)
                h = to
            else:
                stage_aggregate_natural(c, h, c.nat, b_all)


def layer0_attention(c, a):
    with ExitStack() as ctx:
        big = c.work(ctx, "big_attention", 13550, 3 * N + 128)
        c.recycle()
        g, b, qg, kg = c.gain[:, 0:4], c.gain[:, 4:8], c.gain[:, 8:9], c.gain[:, 9:10]
        loads = [(g, column(a["L0_ffn_ln_g"])), (b, column(a["L0_ffn_ln_b"])), weight(c, 0, a["L0_ffn_Wv"]), weight(c, 1, a["L0_ffn_Wk"])]
        for k in range(2):
            loads.append((qg[64 * k:64 * k + 64], a["L0_ffn_qn_g"].rearrange("(p o) -> p o", o=1)))
            loads.append((kg[64 * k:64 * k + 64], a["L0_ffn_kn_g"].rearrange("(p o) -> p o", o=1)))
        tiles_on_tensor(c, [], loads)
        stage_layernorm(c, c.x, c.nat)
        stage_layernorm(c, c.nat, c.nat)
        tiles_on_tensor(c, turn(c.nat, c.xt, lambda k, to: scaled_to(to, g[:, k:k + 1], b[:, k:k + 1])))
        tiles_on_tensor(c, natural_product(c.xt, c.w[:, 0], lambda t: copy_to(c.nat[0:P, t, :])))
        tiles_on_tensor(c, [], [weight(c, 0, a["L0_ffn_Wq"])])
        stage_attention_constants(c)
        stage_scale8(c, kg)
        ot = big[:, 0:5000].rearrange("p (k n) -> p k n", k=KC)
        qt, kt, work = big[:, 5000:6250], big[:, 6250:7500], big[:, 7500:8750]
        qr, kr, dm = c.rounded[:, 0:N], c.rounded[:, N:2 * N], c.rounded[0:P, 2 * N:3 * N]
        pr = big[0:P, 8750:10750].rearrange("p (b n) -> p b n", b=4)
        va = big[0:P, 10750:12030].rearrange("p (t d) -> p t d", t=T)
        rd = big[:, 12050:12550]
        for p in range(4):
            tiles_on_tensor(c, [(128, n, [(c.w[:, 1 - z, k, 128 * p:128 * p + 128], c.xt[:, k, c0:c0 + n]) for k in range(KC)],
                                 copy_to((kt if z == 0 else qt)[:, c0:c0 + n])) for z in range(2) for c0, n in COLS])
            c.recycle()
            stage_unit(c, qt, qr, qg, work)
            stage_unit(c, kt, kr, kg, work)
            for par in range(2):
                stage_head(c, 2 * p + par, qt, kt, qr, kr, dm, pr, va, ot[:, p], rd)
        tiles_on_tensor(c, [], [weight(c, 0, a["L0_ffn_Wo"])])
        tiles_on_tensor(c, turned_product(c.w[:, 0], ot, D, lambda m, cols: copy_to(c.xt[:, m, cols])))
        mixture(c, a, "L0_ffn", c.xt, a["L0_ffn_gate_W"], a["L0_ffn_gate_b"], a["L0_ffn_b1"], a["L0_ffn_W1"],
                a["L0_ffn_W2"], a["L0_ffn_b2"], False, 10000)


def layer1(c, a):
    with ExitStack() as ctx:
        big = c.work(ctx, "big_layer1", 17500)
        c.recycle()
        stage_layernorm(c, c.x, c.nat)
        tiles_on_tensor(c, turn(c.nat, c.xt), [weight(c, 0, a["L1_gnn_weight"])])
        tiles_on_tensor(c, natural_product(c.xt, c.w[:, 0], lambda t: scaled_to(c.nat[0:P, t, :], c.out_n[0:P, t:t + 1])))
        rev = big[0:P, 0:12500].rearrange("p (i n) -> p i n", i=T)
        tiles_on_tensor(c, [(P, n * P, ("turn", [c.adj[0:P, t, P * i:P * i + P] for t in range(t0, t0 + n)]),
                             copy_to(rev[:, i, t0 * P:(t0 + n) * P])) for i in range(T) for t0, n in QUERIES])
        c.recycle()
        stage_loop_add_identity(c, rev)
        tiles_on_tensor(c, [(P, D, [(rev[:, i, t * P:t * P + P], c.nat[0:P, i, :]) for i in range(T)],
                             add_to_x(c, t, relu=True, scale=c.out_n[0:P, t:t + 1])) for t in range(T)], only_vector=True)
        stage_l1_mix(c, a)
        c.recycle()
        stage_layernorm(c, c.x, c.nat)
        tiles_on_tensor(c, turn(c.nat, c.xt))
        mixture(c, a, "L1_ffn", c.xt, a["L1_ffn_router_w"], None, a["L1_ffn_b1"], a["L1_ffn_w1"], a["L1_ffn_w2"],
                a["L1_ffn_b2"], True, 10000)


def stage_scale8(c, kg):
    nc = c.nc
    with nc.Block() as block:
        @block.vector
        def _(v):
            nc.vector.tensor_scalar(kg, kg, 8.0, None, ALU.mult)


def finish(c, out):
    nc = c.nc
    with ExitStack() as s:
        stored = c.semaphore("stored")
        block = s.enter_context(nc.Block())

        @block.sync
        def _(sp):
            sp.dma_start(out.rearrange("(t p) d -> p t d", p=P), c.x[0:P]).then_inc(stored, 16)
            sp.wait_ge(stored, 16)


def kernel(**inputs):
    import concourse.bacc as bacc
    from concourse.bass_utils import run_bass_kernel_spmd

    nc = bacc.Bacc("TRN2", target_bir_lowering=False, num_devices=1)
    arrays, aps = {}, {}
    for name, value in inputs.items():
        a = np.ascontiguousarray(value)
        arrays["in_" + name] = a
        aps[name] = nc.dram_tensor("in_" + name, a.shape, mybir.dt.from_np(a.dtype), kind="ExternalInput").ap()
    out = nc.dram_tensor("out", (N, D), F32, kind="ExternalOutput").ap()
    build(nc, aps, out)
    return run_bass_kernel_spmd(nc, [arrays], core_ids=[0]).results[0]["out"]
```

```python
from contextlib import ExitStack

import numpy as np
import concourse.bass as bass
from concourse import mybir

F32 = mybir.dt.float32
F32R = mybir.dt.float32r
BF16 = mybir.dt.bfloat16
I32 = mybir.dt.int32
I16 = mybir.dt.int16
ALU = mybir.AluOpType
ACT = mybir.ActivationFunctionType
AX = mybir.AxisListType

N = 1250
D = 512
P = 125
T = N // P
KC = D // 128
EDGES = 41250
SUPERS = 110
SUB = 3
CHUNKS = SUPERS * SUB
W = 500
WINDOWS = N * T // W
COLS = [(0, 418), (418, 416), (834, 416)]
EPS = 1e-5


class Chip:

    def __init__(self, nc, ctx):
        def sb(name, shape, dt):
            return ctx.enter_context(nc.sbuf_tensor(name, shape, dt))

        self.nc = nc
        self.in_use = []
        self.named = 0
        self.adj = sb("adj", [128, T, N], F32)
        self.x = sb("x", [128, T, D], F32)
        self.ident = sb("ident", [128, 128], F32)
        self.ones = sb("ones", [128, 128], F32)
        self.inv_n = sb("inv_n", [128, T], F32)
        self.out_n = sb("out_n", [128, T], F32)
        self.gain = sb("gain", [128, 16], F32)
        self.small = sb("small", [128, 512], F32)
        self.ps = ctx.enter_context(nc.psum_tensor("ps", [128, 8, 512], F32))

    def semaphore(self, name):
        self.named += 1
        handle = self.nc.alloc_semaphore(name=f"{name}_{self.named}")
        self.in_use.append(handle)
        return handle

    def recycle(self):
        self.nc.clear_and_free_semaphores(self.in_use)
        self.nc.all_engine_barrier()
        self.in_use = []

    def work(self, ctx, name, columns, weights=3, rounded=0):
        def sb(part, shape, dt=F32):
            return ctx.enter_context(self.nc.sbuf_tensor(f"{name}_{part}", shape, dt))

        self.big = sb("big", [128, columns])
        self.w = sb("w", [128, weights, KC, D])
        self.xt = sb("xt", [128, KC, N])
        self.nat = sb("nat", [128, T, D])
        if rounded:
            self.rounded = sb("rounded", [128, rounded], F32R)
        return self.big


class Edges:

    def __init__(self, nc, ctx):
        def sb(name, shape, dt):
            return ctx.enter_context(nc.sbuf_tensor(name, shape, dt))

        self.ends = sb("ends", [SUPERS, 2, SUB * P], I32)
        self.f = sb("codes", [SUPERS, 4, SUB * P], F32)
        self.gcol = sb("gcol", [P, CHUNKS + SUB], F32)
        self.lcol = sb("lcol", [P, CHUNKS], F32)
        self.iota = sb("iota", [P, N * T], I16)
        self.local_hot = sb("local_hot", [P, CHUNKS + SUB, P], BF16)
        self.code_hot = sb("code_hot", [P, SUB, W], BF16)
        self.zeros = sb("zeros", [P, P], BF16)
        self.marks = sb("marks", [SUPERS, 6, WINDOWS], F32)
        self.few = sb("few", [128, 8], F32)
        self.line = sb("line", [1, 6, WINDOWS], F32)
        self.bounds = sb("bounds", [1, 2, WINDOWS], I32)


def stage_codes(c, m, x, src, dst):
    nc = c.nc
    srcf, dstf, tile, local = (m.f[:, k, :] for k in range(4))
    code = dstf
    least, most, rowno, up, down = (m.few[0:SUPERS, k:k + 1] for k in range(5))
    wbase, low, high, meets = (m.marks[:, k, :] for k in range(4))
    marks = m.marks[:, 4:6, :].rearrange("p a w -> p (a w)")
    ends = m.few[0:2 * WINDOWS, 5:6]
    last, first, rows, before, bases, ones = (m.line[:, k, :] for k in range(6))
    loaded_x, loaded_e, const, iota, step, turned, maxed = map(c.semaphore, (
        "loaded_x", "loaded_e", "const", "iota", "step", "turned", "maxed"))
    LOCAL, CODE = 2 + (T - 1) + 1, 2 + (T - 1) + 2
    MARKS = CODE + 2 + 7
    CHUNKED = MARKS + 6
    with nc.Block() as block:
        @block.sync
        def _(sp):
            sp.dma_start(m.ends[:, 0, :], src.rearrange("(s e) -> s e", s=SUPERS)).then_inc(loaded_e, 16)
            sp.dma_start(m.ends[:, 1, :], dst.rearrange("(s e) -> s e", s=SUPERS)).then_inc(loaded_e, 16)
            sp.dma_start(c.x[0:P], x.rearrange("(t p) d -> p t d", p=P)).then_inc(loaded_x, 16)
            sp.wait_ge(loaded_x, 16)

        @block.gpsimd
        def _(pool):
            nc.gpsimd.memset(c.ident[:], 0.0).then_inc(const, 1)
            nc.gpsimd.memset(c.ones[:], 1.0).then_inc(const, 1)
            nc.gpsimd.iota(wbase, [[W, WINDOWS]], base=0, channel_multiplier=0,
                           allow_small_or_imprecise_dtypes=True).then_inc(const, 1)
            nc.gpsimd.iota(rowno, [[0, 1]], base=0, channel_multiplier=1,
                           allow_small_or_imprecise_dtypes=True).then_inc(const, 1)
            pool.wait_ge(const, 4)
            nc.gpsimd.affine_select(out=c.ident[:], in_=c.ident[:], compare_op=ALU.not_equal, fill=1.0, base=0,
                                    pattern=[[-1, 128]], channel_multiplier=1).then_inc(const, 1)
            nc.gpsimd.memset(m.zeros[:], 0.0).then_inc(iota, 1)
            nc.gpsimd.iota(m.iota[:], [[1, N * T]], base=0, channel_multiplier=0).then_inc(iota, 1)

        @block.vector
        def _(v):
            link = chain(v, step)
            v.wait_ge(loaded_e, 32)
            link(nc.vector.tensor_copy(srcf, m.ends[:, 0, :]))
            link(nc.vector.tensor_copy(dstf, m.ends[:, 1, :]))
            link(nc.vector.tensor_scalar(tile, srcf, float(P), None, ALU.is_ge))
            for j in range(2, T):
                link(nc.vector.scalar_tensor_tensor(tile, srcf, float(P * j), tile, ALU.is_ge, ALU.add))
            link(nc.vector.scalar_tensor_tensor(local, tile, float(-P), srcf, ALU.mult, ALU.add))
            link(nc.vector.scalar_tensor_tensor(code, dstf, float(T), tile, ALU.mult, ALU.add))
            link(nc.vector.tensor_reduce(most, code, AX.X, ALU.max))
            link(nc.vector.tensor_reduce(least, code, AX.X, ALU.min))
            v.wait_ge(const, 5)
            link(nc.vector.tensor_scalar(low, wbase, most, None, ALU.is_le))
            link(nc.vector.tensor_scalar(high, wbase, float(W - 1), least, ALU.add, ALU.is_ge))
            link(nc.vector.tensor_tensor(meets, low, high, ALU.mult))
            link(nc.vector.tensor_scalar(up, rowno, 1.0, None, ALU.add))
            link(nc.vector.tensor_scalar(down, rowno, -1.0, float(SUPERS), ALU.mult, ALU.add))
            link(nc.vector.tensor_scalar(marks[:, 0:WINDOWS], meets, up, None, ALU.mult))
            link(nc.vector.tensor_scalar(marks[:, WINDOWS:], meets, down, None, ALU.mult))
            v.wait_ge(turned, 6)
            for k in range(6):
                to = (m.lcol if k < 3 else m.gcol)[:, 0:CHUNKS].rearrange("p (s j) -> p s j", j=SUB)
                link(nc.vector.tensor_copy(to[:, :, k % 3], c.ps[0:P, k, 0:SUPERS]))
            v.wait_ge(turned, 7)
            nc.vector.tensor_reduce(ends, c.ps[0:2 * WINDOWS, 6, 0:SUPERS], AX.X, ALU.max).then_inc(maxed, 1)
            link(nc.vector.memset(ones, 1.0))
            v.wait_ge(turned, 8)
            link(nc.vector.tensor_copy(m.line[:, 0:2, :].rearrange("p a w -> p (a w)"), c.ps[0:1, 7, 0:2 * WINDOWS]))
            link(nc.vector.tensor_scalar(last, last, 1.0, None, ALU.max))
            link(nc.vector.tensor_scalar(first, first, -1.0, float(SUPERS), ALU.mult, ALU.add))
            link(nc.vector.scalar_tensor_tensor(first, last, -1.0, first, ALU.add, ALU.min))
            link(nc.vector.tensor_tensor(rows, last, first, ALU.subtract))
            link(nc.vector.tensor_tensor_scan(before, ones, rows, 0.0, ALU.mult, ALU.add))
            link(nc.vector.tensor_tensor(before, before, last, ALU.subtract))
            link(nc.vector.tensor_scalar(m.bounds[:, 1, :], before, float(SUB), float(CHUNKS), ALU.mult, ALU.add))
            link(nc.vector.scalar_tensor_tensor(bases, first, 512.0, last, ALU.mult, ALU.add))
            link(nc.vector.tensor_scalar(m.bounds[:, 0, :], bases, float(SUB), None, ALU.mult))

        @block.tensor
        def _(pe):
            pe.wait_ge(const, 5)
            for k in range(6):
                pe.wait_ge(step, LOCAL if k < 3 else CODE)
                of = (local if k < 3 else code).rearrange("p (j e) -> p j e", j=SUB)
                nc.tensor.transpose(c.ps[0:P, k, 0:SUPERS], of[:, k % 3, :], c.ident[0:SUPERS, 0:SUPERS]).then_inc(turned, 1)
            pe.wait_ge(step, MARKS)
            nc.tensor.transpose(c.ps[0:2 * WINDOWS, 6, 0:SUPERS], marks, c.ident[0:SUPERS, 0:SUPERS]).then_inc(turned, 1)
            pe.wait_ge(maxed, 1)
            nc.tensor.transpose(c.ps[0:1, 7, 0:2 * WINDOWS], ends, c.ident[0:2 * WINDOWS, 0:2 * WINDOWS]).then_inc(turned, 1)


def stage_adjacency(c, m):
    nc = c.nc
    hot, used, window_done, window_free, local = map(c.semaphore, (
        "hot", "used", "window_done", "window_free", "local"))

    def bounds(engine, w):
        both = engine.value_load(m.bounds[0:1, 0, w:w + 1], min_val=0, max_val=512 * CHUNKS - 1)
        made = engine.value_load(m.bounds[0:1, 1, w:w + 1], min_val=0, max_val=CHUNKS * (WINDOWS + 1))
        return (engine.snap(both >> 9).with_bounds(min_val=0, max_val=CHUNKS - SUB), engine.snap(both & 511).with_bounds(min_val=SUB, max_val=CHUNKS), made)

    with nc.Block() as block:
        @block.gpsimd
        def _(pool):
            for k in range(CHUNKS):
                nc.gpsimd.tensor_scalar(m.local_hot[:, k, :], m.iota[:, 0:P], m.lcol[:, k:k + 1], None,
                                        ALU.is_equal).then_inc(local, 1)

        @block.vector
        def _(v):
            for w in range(WINDOWS):
                first, end, made = bounds(v, w)
                with v.Fori(first, end, SUB) as r:
                    for j in range(SUB):
                        v.wait_ge(used, made + r + (j + 1))
                        nc.vector.tensor_scalar(m.code_hot[:, j, :], m.iota[:, w * W:w * W + W],
                                                m.gcol[:, bass.ds(r + j, 1)], None, ALU.is_equal).then_inc(hot, 1)

        @block.tensor
        def _(pe):
            pe.sem_inc(used, SUB + CHUNKS)
            pe.sem_inc(hot, CHUNKS)
            for w in range(WINDOWS):
                first, end, made = bounds(pe, w)
                if w >= 2:
                    pe.wait_ge(window_free, w - 1)
                if w == 0:
                    pe.wait_ge(local, W // P)
                pe.wait_ge(local, end)
                out = c.ps[0:P, w % 2, 0:W]
                nc.tensor.matmul(out, m.zeros[:], m.local_hot[:, 0:W // P, :], start=True, stop=False)
                with pe.Fori(first, end, SUB) as r:
                    for j in range(SUB):
                        pe.wait_ge(hot, made + r + (j + 1))
                        nc.tensor.matmul(out, m.local_hot[:, bass.ds(r + j, 1), :], m.code_hot[:, j, :], start=False,
                                         stop=False).then_inc(used, 1)
                nc.tensor.matmul(out, m.zeros[:], m.local_hot[:, 0:W // P, :], start=False,
                                 stop=True).then_inc(window_done, 1)

        @block.scalar
        def _(act):
            for w in range(WINDOWS):
                act.wait_ge(window_done, w + 1)
                nc.scalar.activation(c.adj[0:P, :, w * (W // T):(w + 1) * (W // T)],
                                     c.ps[0:P, w % 2, 0:W].rearrange("p (d t) -> p t d", t=T),
                                     ACT.Copy).then_inc(window_free, 1)


def stage_layernorm(c, of, to):
    nc = c.nc
    stats = c.small[0:P, 0:60].rearrange("p (t s) -> p t s", t=T)
    mv = c.small[0:P, 60:80].rearrange("p (t s) -> p t s", t=T)
    root = c.small[0:P, 80:90]
    inverse = c.small[0:P, 90:100]
    with ExitStack() as s:
        sem = lambda n: c.semaphore(n)
        stats_done, moments, shifted, rooted, inverted = map(sem, (
            "stats_done", "moments", "shifted", "rooted", "inverted"))
        block = s.enter_context(nc.Block())

        @block.scalar
        def _(act):
            act.wait_ge(shifted, 1)
            nc.scalar.activation(root, root, ACT.Sqrt).then_inc(rooted, 1)

        @block.vector
        def _(v):
            for t in range(T):
                nc.vector.bn_stats(stats[:, t, :], of[0:P, t, :]).then_inc(stats_done, 1)
            for t in range(T):
                v.wait_ge(stats_done, t + 1)
                nc.vector.bn_aggr(mv[:, t, :], stats[:, t, :]).then_inc(moments, 1)
            v.wait_ge(moments, T)
            nc.vector.tensor_scalar(root, mv[:, :, 1], EPS, None, ALU.add).then_inc(shifted, 1)
            v.wait_ge(rooted, 1)
            nc.vector.reciprocal(inverse, root).then_inc(inverted, 1)
            v.wait_ge(inverted, 1)
            for t in range(T):
                nc.vector.tensor_scalar(to[0:P, t, :], of[0:P, t, :], mv[:, t, 0:1], inverse[:, t:t + 1],
                                        ALU.subtract, ALU.mult)


def tiles_on_tensor(c, tiles, loads=(), only_vector=False):
    nc = c.nc
    with ExitStack() as s:
        sem = lambda n: c.semaphore(n)
        made, scalar_out, vector_out, scalar_step, vector_step, loaded = map(sem, (
            "made", "scalar_out", "vector_out", "scalar_step", "vector_step", "loaded"))
        block = s.enter_context(nc.Block())

        @block.sync
        def _(sp):
            for to, of in loads:
                sp.dma_start(to, of).then_inc(loaded, 16)
            if loads:
                sp.wait_ge(loaded, 16 * len(loads))

        @block.tensor
        def _(pe):
            for g, (rows, cols, parts, _) in enumerate(tiles):
                if g >= 8:
                    if only_vector:
                        pe.wait_ge(vector_out, g - 7)
                    else:
                        pe.wait_ge(vector_out if g % 2 else scalar_out, (g - 8) // 2 + 1)
                ps = c.ps[0:rows, g % 8, 0:cols]
                if isinstance(parts, tuple) and parts[0] == "turn":
                    for k, of in enumerate(parts[1]):
                        r, w = of.shape
                        ins = nc.tensor.transpose(ps[0:w, k * r:(k + 1) * r], of, c.ident[0:r, 0:r])
                else:
                    for k, (l, r) in enumerate(parts):
                        ins = nc.tensor.matmul(ps, l, r, start=(k == 0), stop=(k == len(parts) - 1))
                ins.then_inc(made, 1)

        def copies(engine, first, step, out):
            count = [0]

            def link(ins):
                count[0] += 1
                ins.then_inc(step, 1)
                engine.wait_ge(step, count[0])

            for g in range(first, len(tiles), 1 if only_vector else 2):
                engine.wait_ge(made, g + 1)
                rows, cols, _, copy = tiles[g]
                copy(engine, c.ps[0:rows, g % 8, 0:cols], link).then_inc(out, 1)

        if not only_vector:
            @block.scalar
            def _(act):
                copies(act, 0, scalar_step, scalar_out)

        @block.vector
        def _(v):
            copies(v, 0 if only_vector else 1, vector_step, vector_out)


def is_scalar(engine):
    return engine.engine == mybir.EngineType.Activation


def copy_to(to):
    def copy(e, ps, link):
        return e.activation(to, ps, ACT.Copy) if is_scalar(e) else e.tensor_copy(to, ps)
    return copy


def scaled_to(to, scale, bias=None):
    def copy(e, ps, link):
        if is_scalar(e):
            return e.activation(to, ps, ACT.Identity, scale=scale, bias=0.0 if bias is None else bias)
        if bias is None:
            return e.tensor_scalar(to, ps, scale, None, ALU.mult)
        return e.tensor_scalar(to, ps, scale, bias, ALU.mult, ALU.add)
    return copy


def biased_to(to, bias, relu=False):
    def copy(e, ps, link):
        if is_scalar(e):
            return e.activation(to, ps, ACT.Relu if relu else ACT.Identity, bias=bias)
        return e.tensor_scalar(to, ps, bias, 0.0 if relu else None, ALU.add, ALU.max if relu else ALU.bypass)
    return copy


def turn(of, to, post=None):
    out = []
    for k in range(KC):
        for t0 in range(0, T, 4):
            n = min(4, T - t0)
            where = to[:, k, t0 * P:(t0 + n) * P]
            out.append((128, n * P, ("turn", [of[0:P, t, 128 * k:128 * k + 128] for t in range(t0, t0 + n)]),
                        post(k, where) if post else copy_to(where)))
    return out


def turned_product(w, of, rows, copy, kc=KC):
    return [(min(128, rows - 128 * m), n, [(w[:, k, 128 * m:min(rows, 128 * m + 128)], of[:, k, c0:c0 + n]) for k in range(kc)],
             copy(m, slice(c0, c0 + n))) for m in range((rows + 127) // 128) for c0, n in COLS]


def natural_product(of, w, copy, kc=KC):
    return [(P, w.shape[2], [(of[:, k, t * P:t * P + P], w[:, k, :]) for k in range(kc)], copy(t)) for t in range(T)]


def weight(c, slot, of):
    return (c.w[:, slot], of.rearrange("(k p) n -> p k n", p=128))


def column(ap, n=KC):
    return ap.rearrange("(k p) -> p k", k=n)


def stage_degrees(c):
    nc = c.nc
    sums = c.big[0:P, 0:N]
    with ExitStack() as s:
        sem = lambda n: c.semaphore(n)
        v_done, p_done, a_done = map(sem, ("v_done", "p_done", "a_done"))
        block = s.enter_context(nc.Block())

        @block.tensor
        def _(pe):
            pe.wait_ge(v_done, 1)
            for b, (c0, n) in enumerate(COLS):
                ins = nc.tensor.matmul(c.ps[:, b, 0:n], c.ones[0:P, :], sums[:, c0:c0 + n], start=True, stop=True)
            ins.then_inc(p_done, 1)
            pe.wait_ge(v_done, 6)
            for t in range(T):
                ins = nc.tensor.transpose(c.ps[0:P, 3 + t // 4, 128 * (t % 4):128 * (t % 4) + 128],
                                          c.inv_t[:, t * P:t * P + P], c.ident[:, :])
            ins.then_inc(p_done, 1)

        @block.vector
        def _(v):
            nc.vector.tensor_reduce(sums, c.adj[0:P].rearrange("p s d -> p d s"), AX.X, ALU.add).then_inc(v_done, 1)
            nc.vector.tensor_reduce(c.out_n[0:P, :], c.adj[0:P], AX.X, ALU.add).then_inc(v_done, 1)
            v.wait_ge(p_done, 1)
            for b, (c0, n) in enumerate(COLS):
                ins = nc.vector.tensor_scalar(c.inv_t[:, c0:c0 + n], c.ps[:, b, 0:n], 1.0, None, ALU.max)
            ins.then_inc(v_done, 1)
            v.wait_ge(v_done, 3)
            nc.vector.tensor_scalar(c.out_n[0:P, :], c.out_n[0:P, :], 1.0, None, ALU.add).then_inc(v_done, 1)
            v.wait_ge(v_done, 4)
            nc.vector.reciprocal(c.inv_t[:, :], c.inv_t[:, :]).then_inc(v_done, 1)
            v.wait_ge(v_done, 5)
            nc.vector.tensor_copy(c.small[0:1, 511:512], c.inv_t[0:1, 0:1]).then_inc(v_done, 1)
            v.wait_ge(p_done, 2)
            nc.vector.tensor_copy(c.inv_n[0:P, 0:8].rearrange("p (a b) -> p a b", a=2),
                                  c.ps[0:P, 3:5, :].rearrange("p a (b q) -> p a b q", q=128)[:, :, :, 0])
            nc.vector.tensor_copy(c.inv_n[0:P, 8:10], c.ps[0:P, 5, 0:256].rearrange("p (b q) -> p b q", q=128)[:, :, 0])
            v.wait_ge(a_done, 1)
            nc.vector.reciprocal(c.out_n[0:P, :], c.out_n[0:P, :])

        @block.scalar
        def _(act):
            act.wait_ge(v_done, 4)
            nc.scalar.activation(c.out_n[0:P, :], c.out_n[0:P, :], ACT.Sqrt).then_inc(a_done, 1)


def stage_l0_mix(c, a):
    qt = c.big[:, 0:5000].rearrange("p (k n) -> p k n", k=KC)
    kn = c.nat
    vn = c.big[:, 5000:5000 + T * D].rearrange("p (t d) -> p t d", t=T)
    wt = c.big[:, 10500:10500 + 2048].rearrange("p (k d) -> p k d", k=KC)
    tmp = c.big[:, 12600:12600 + 512 * 4].rearrange("p (b d) -> p b d", b=4)
    kv = c.big[:, 14700:14700 + 4 * 130].rearrange("p (k d) -> p k d", k=4)

    def elu(to):
        return to

    def turn_w(slot):
        return [(128, 512, ("turn", [c.w[:, slot, m, 128 * k:128 * k + 128] for m in range(KC)]),
                 copy_to(wt[:, k, :])) for k in range(KC)]

    tiles_on_tensor(c, turn_w(0))
    stage_elu(c, [(128, n, [(wt[:, k, 128 * m:128 * m + 128], c.xt[:, k, c0:c0 + n]) for k in range(KC)],
                   qt[:, m, c0:c0 + n]) for m in range(KC) for c0, n in COLS], tmp)
    tiles_on_tensor(c, turn_w(1))
    stage_elu(c, [(P, D, [(c.xt[:, k, t * P:t * P + P], wt[:, k, :]) for k in range(KC)], kn[0:P, t, :])
                  for t in range(T)], tmp)
    tiles_on_tensor(c, turn_w(2))
    tiles_on_tensor(c, natural_product(c.xt, wt, lambda t: scaled_to(vn[0:P, t, :], 1.0 / N)))

    def pair(p):
        def copy(e, ps, link):
            cp = (lambda o, i: e.activation(o, i, ACT.Copy)) if is_scalar(e) else e.tensor_copy
            cp(kv[0:64, p, 0:64], ps[0:64, 0:64])
            cp(kv[64:128, p, 64:128], ps[64:128, 64:128])
            cp(kv[0:64, p, 128:129], ps[0:64, 128:129])
            return cp(kv[64:128, p, 129:130], ps[64:128, 128:129])
        return copy
    memsets(c, [kv[:]])
    vo = c.w[0:P, 2].rearrange("p a b -> p (a b)")[:, 0:T * 132].rearrange("p (t q) -> p t q", q=132)
    for p in range(4):
        stage_pool_copy(c, vo, vn[0:P, :, 128 * p:128 * p + 128], p == 0)
        tiles_on_tensor(c, [(128, 132, [(kn[0:P, t, 128 * p:128 * p + 128], vo[:, t, :]) for t in range(T)], pair(p))])

    r = c.small[0:P, 0:512]

    def out(t, h):
        def copy(e, ps, link):
            v = c.nc.vector
            num = ps.rearrange("p (a q) -> p a q", q=130)
            link(v.tensor_scalar(r[:, 16 * h:16 * h + 4].rearrange("p (a q) -> p a q", a=2), num[:, :, 128:130], 1e-6, None, ALU.add))
            link(v.reciprocal(r[:, 16 * h + 4:16 * h + 8], r[:, 16 * h:16 * h + 4]))
            m = tmp[0:P, h, 0:256]
            link(v.tensor_tensor(m.rearrange("p (a b d) -> p a b d", a=2, b=2),
                                 num[:, :, 0:128].rearrange("p a (b d) -> p a b d", b=2),
                                 r[:, 16 * h + 4:16 * h + 8].rearrange("p (a b) -> p a b", a=2).unsqueeze(3).to_broadcast([P, 2, 2, 64]),
                                 ALU.mult))
            x = c.x[0:P, t, 256 * h:256 * h + 256]
            return v.scalar_tensor_tensor(x, m, float(N), x, ALU.mult, ALU.add)
        return copy
    on_vector(c, [(P, 260, [("pairs", 2 * h, t)], out(t, h)) for t in range(T) for h in range(2)], qt, kv)


def memsets(c, aps, value=0.0):
    nc = c.nc
    with nc.Block() as block:
        @block.gpsimd
        def _(pool):
            for ap in aps:
                nc.gpsimd.memset(ap, value)


def stage_pool_copy(c, to, of, ones):
    nc = c.nc
    with nc.Block() as block:
        @block.gpsimd
        def _(pool):
            if ones:
                nc.gpsimd.memset(to[:, :, 128:132], 1.0)
            nc.gpsimd.tensor_copy(to[:, :, 0:128], of)


def on_vector(c, tiles, qt, kv):
    nc = c.nc
    with ExitStack() as s:
        sem = lambda n: c.semaphore(n)
        made, out, step = map(sem, ("made", "out", "step"))
        block = s.enter_context(nc.Block())

        @block.tensor
        def _(pe):
            for g, (rows, cols, parts, _) in enumerate(tiles):
                if g >= 8:
                    pe.wait_ge(out, g - 7)
                _, p0, t = parts[0]
                for j in range(2):
                    ins = nc.tensor.matmul(c.ps[0:P, g % 8, 130 * j:130 * j + 130], qt[:, p0 + j, t * P:t * P + P],
                                           kv[:, p0 + j, :], start=True, stop=True)
                ins.then_inc(made, 1)

        @block.vector
        def _(v):
            count = [0]

            def link(ins):
                count[0] += 1
                ins.then_inc(step, 1)
                v.wait_ge(step, count[0])

            for g, (rows, cols, parts, copy) in enumerate(tiles):
                v.wait_ge(made, g + 1)
                copy(v, c.ps[0:rows, g % 8, 0:cols], link).then_inc(out, 1)


def stage_elu(c, tiles, tmp):
    nc = c.nc
    with ExitStack() as s:
        sem = lambda n: c.semaphore(n)
        made, low, exped, out = map(sem, ("made", "low", "exped", "out"))
        block = s.enter_context(nc.Block())

        @block.tensor
        def _(pe):
            for g, (rows, cols, parts, _) in enumerate(tiles):
                if g >= 8:
                    pe.wait_ge(out, g - 7)
                for k, (l, r) in enumerate(parts):
                    ins = nc.tensor.matmul(c.ps[0:rows, g % 8, 0:cols], l, r, start=(k == 0), stop=(k == len(parts) - 1))
                ins.then_inc(made, 1)

        @block.scalar
        def _(act):
            for g, (rows, cols, _, to) in enumerate(tiles):
                act.wait_ge(low, g + 1)
                t = tmp[0:rows, g % 4, 0:cols]
                nc.scalar.activation(t, t, ACT.Exp).then_inc(exped, 1)

        @block.vector
        def _(v):
            for g in range(len(tiles) + 2):
                if g < len(tiles):
                    rows, cols, _, to = tiles[g]
                    v.wait_ge(made, g + 1)
                    if g >= 4:
                        v.wait_ge(out, g - 3)
                    nc.vector.tensor_scalar(tmp[0:rows, g % 4, 0:cols], c.ps[0:rows, g % 8, 0:cols], 0.0, None,
                                            ALU.min).then_inc(low, 1)
                if g >= 2:
                    rows, cols, _, to = tiles[g - 2]
                    v.wait_ge(exped, g - 1)
                    nc.vector.scalar_tensor_tensor(to, c.ps[0:rows, (g - 2) % 8, 0:cols], 0.0,
                                                   tmp[0:rows, (g - 2) % 4, 0:cols], ALU.max, ALU.add).then_inc(out, 1)


def stage_aggregate(c, of_t, to_t, u, b, relu):
    nc = c.nc
    tmp = c.small
    tiles = [(m, c0, n) for m in range(KC) for c0, n in COLS]
    scratch = c.big[:, 12600:12600 + 1024].rearrange("p (b d) -> p b d", b=2)
    with ExitStack() as s:
        sem = lambda n: c.semaphore(n)
        made, mult, added, out = map(sem, ("made", "mult", "added", "out"))
        block = s.enter_context(nc.Block())

        @block.tensor
        def _(pe):
            for g, (m, c0, n) in enumerate(tiles):
                if g >= 4:
                    pe.wait_ge(out, g - 3)
                for t in range(T):
                    nc.tensor.matmul(c.ps[:, 2 * (g % 4), 0:n], u[0:P, t, 128 * m:128 * m + 128],
                                     c.adj[0:P, t, c0:c0 + n], start=(t == 0), stop=(t == T - 1))
                for k in range(KC):
                    ins = nc.tensor.matmul(c.ps[:, 2 * (g % 4) + 1, 0:n], c.w[:, 0, k, 128 * m:128 * m + 128],
                                           of_t[:, k, c0:c0 + n], start=(k == 0), stop=(k == KC - 1))
                ins.then_inc(made, 1)

        @block.vector
        def _(v):
            for g, (m, c0, n) in enumerate(tiles):
                v.wait_ge(made, g + 1)
                if g >= 2:
                    v.wait_ge(out, g - 1)
                t = scratch[:, g % 2, 0:n]
                nc.vector.tensor_tensor(t, c.ps[:, 2 * (g % 4), 0:n], c.inv_t[:, c0:c0 + n], ALU.mult).then_inc(mult, 1)
                v.wait_ge(mult, g + 1)
                nc.vector.tensor_tensor(t, t, c.ps[:, 2 * (g % 4) + 1, 0:n], ALU.add).then_inc(added, 1)

        @block.scalar
        def _(act):
            for g, (m, c0, n) in enumerate(tiles):
                act.wait_ge(added, g + 1)
                nc.scalar.activation(to_t[:, m, c0:c0 + n], scratch[:, g % 2, 0:n], ACT.Relu,
                                     bias=b[:, m:m + 1]).then_inc(out, 1)


def stage_aggregate_natural(c, of_t, u, b_all):
    nc = c.nc
    with ExitStack() as s:
        sem = lambda n: c.semaphore(n)
        made, step, out = map(sem, ("made", "step", "out"))
        block = s.enter_context(nc.Block())

        @block.tensor
        def _(pe):
            for g in range(T):
                if g >= 4:
                    pe.wait_ge(out, g - 3)
                for t in range(T):
                    nc.tensor.matmul(c.ps[0:P, 2 * (g % 4), :], c.adj[0:P, t, g * P:g * P + P], u[0:P, t, :],
                                     start=(t == 0), stop=(t == T - 1))
                for k in range(KC):
                    ins = nc.tensor.matmul(c.ps[0:P, 2 * (g % 4) + 1, :], of_t[:, k, g * P:g * P + P], c.w[:, 0, k, :],
                                           start=(k == 0), stop=(k == KC - 1))
                ins.then_inc(made, 1)

        @block.vector
        def _(v):
            for g in range(T):
                v.wait_ge(made, g + 1)
                x = c.x[0:P, g, :]
                nc.vector.scalar_tensor_tensor(x, c.ps[0:P, 2 * (g % 4), :], c.inv_n[0:P, g:g + 1], x, ALU.mult,
                                               ALU.add).then_inc(step, 1)
                v.wait_ge(step, 2 * g + 1)
                nc.vector.tensor_tensor(x, x, c.ps[0:P, 2 * (g % 4) + 1, :], ALU.add).then_inc(step, 1)
                v.wait_ge(step, 2 * g + 2)
                nc.vector.tensor_tensor(x, x, b_all, ALU.add).then_inc(out, 1)



def chain(engine, sem):
    count = [0]

    def link(ins):
        count[0] += 1
        ins.then_inc(sem, 1)
        engine.wait_ge(sem, count[0])
    return link


KEYS = [(0, 512), (512, 512), (1024, N - 1024)]
QUERIES = [(0, 4), (4, 4), (8, 2)]


def stage_attention_constants(c):
    nc = c.nc
    f = c.w[:, 2, 0]
    c.blockones = f[:, 0:128]
    c.minus = c.rounded[0:P, 3 * N:3 * N + 128]
    c.mask_n = f[0:P, 256:320].bitcast(BF16)[:, 0:P]
    c.mask_t = f[0:P, 320:384].bitcast(BF16)[:, 0:P]
    c.identb = f[0:P, 384:448].bitcast(BF16)[:, 0:P]
    with ExitStack() as s:
        a, b = (c.semaphore(n) for n in ("a", "b"))
        block = s.enter_context(nc.Block())

        @block.gpsimd
        def _(pool):
            nc.gpsimd.memset(c.blockones, 0.0).then_inc(a, 1)
            nc.gpsimd.memset(c.mask_n, 0.0).then_inc(a, 1)
            nc.gpsimd.memset(c.mask_t, 0.0).then_inc(a, 1)
            pool.wait_ge(a, 3)
            nc.gpsimd.affine_select(out=c.mask_n, in_=c.mask_n, compare_op=ALU.is_ge, fill=-3e38, base=0,
                                    pattern=[[-1, P]], channel_multiplier=1)
            nc.gpsimd.affine_select(out=c.mask_t, in_=c.mask_t, compare_op=ALU.is_ge, fill=-3e38, base=0,
                                    pattern=[[1, P]], channel_multiplier=-1)

        @block.vector
        def _(v):
            nc.vector.tensor_copy(c.identb, c.ident[0:P, 0:P])
            v.wait_ge(a, 3)
            nc.vector.memset(c.blockones[0:64, 0:64], 1.0)
            nc.vector.memset(c.blockones[64:128, 64:128], 1.0)
            nc.vector.tensor_scalar(c.minus, c.ones[0:P, 0:128], -1.0, None, ALU.mult)


def stage_unit(c, raw, rounded, gain, work):
    nc = c.nc
    with ExitStack() as s:
        sem = lambda n: c.semaphore(n)
        squared, summed, shifted, rooted, step = map(sem, ("squared", "summed", "shifted", "rooted", "step"))
        block = s.enter_context(nc.Block())

        @block.scalar
        def _(act):
            for b, (c0, n) in enumerate(COLS):
                nc.scalar.activation(work[:, c0:c0 + n], raw[:, c0:c0 + n], ACT.Square).then_inc(squared, 1)
            for b, (c0, n) in enumerate(COLS):
                act.wait_ge(shifted, b + 1)
                nc.scalar.activation(work[:, c0:c0 + n], work[:, c0:c0 + n], ACT.Sqrt).then_inc(rooted, 1)

        @block.tensor
        def _(pe):
            for b, (c0, n) in enumerate(COLS):
                pe.wait_ge(squared, b + 1)
                nc.tensor.matmul(c.ps[:, b, 0:n], c.blockones, work[:, c0:c0 + n], start=True, stop=True).then_inc(summed, 1)

        @block.vector
        def _(v):
            link = chain(v, step)
            for b, (c0, n) in enumerate(COLS):
                v.wait_ge(summed, b + 1)
                nc.vector.tensor_scalar(work[:, c0:c0 + n], c.ps[:, b, 0:n], 1e-12, None, ALU.add).then_inc(shifted, 1)
            for b, (c0, n) in enumerate(COLS):
                v.wait_ge(rooted, b + 1)
                link(nc.vector.reciprocal(work[:, c0:c0 + n], work[:, c0:c0 + n]))
                link(nc.vector.scalar_tensor_tensor(raw[:, c0:c0 + n], raw[:, c0:c0 + n], gain,
                                                    work[:, c0:c0 + n], ALU.mult, ALU.mult))
                nc.vector.tensor_copy(rounded[:, c0:c0 + n], raw[:, c0:c0 + n])


def stage_head(c, h, qt, kt, qr, kr, dm, pr, va, ot, rd):
    nc = c.nc
    lo = 64 * (h % 2)
    hi = 64 - lo
    mx = c.small[0:P, 0:T]
    flat = c.ps.ap().rearrange("p b n -> p (b n)") if hasattr(c.ps, "ap") else c.ps[:].rearrange("p b n -> p (b n)")
    turns = [(q, i0, ni, j) for q, (i0, ni) in enumerate(QUERIES) for j in range(i0 + ni)]
    with ExitStack() as s:
        sem = lambda n: c.semaphore(n)
        copied, scored, maxed, diag, turned, exped, summed, divided, step = map(sem, (
            "copied", "scored", "maxed", "diag", "turned", "exped", "summed", "divided", "step"))
        block = s.enter_context(nc.Block())

        @block.gpsimd
        def _(pool):
            nc.gpsimd.memset(va[:, :, hi:hi + 64], 1.0).then_inc(copied, 1)
            nc.gpsimd.tensor_copy(va[:, :, lo:lo + 64], c.nat[0:P, :, 64 * h:64 * h + 64]).then_inc(copied, 1)

        @block.tensor
        def _(pe):
            for i in range(T):
                if i >= 2:
                    pe.wait_ge(maxed, i - 1)
                width = P * (i + 1)
                for b, (c0, n) in enumerate(KEYS):
                    if c0 >= width:
                        continue
                    w = min(n, width - c0)
                    d0, d1 = max(P * i, c0), min(width, c0 + n)
                    bank = 4 * (i % 2) + b
                    diagonal = d1 > d0
                    ins = nc.tensor.matmul(c.ps[0:P, bank, 0:w + w % 2], qr[lo:lo + 64, P * i:P * i + P],
                                           kr[lo:lo + 64, c0:c0 + w + w % 2], start=True, stop=not diagonal)
                    if diagonal:
                        ins = nc.tensor.matmul(c.ps[0:P, bank, d0 - c0:d1 - c0], c.identb, c.mask_n[:, d0 - P * i:d1 - P * i],
                                               start=False, stop=True)
                ins.then_inc(scored, 1)
            pe.wait_ge(diag, 1)
            pe.wait_ge(copied, 2)

            def weigh(g):
                q, i0, ni, j = turns[g]
                s0 = max(i0, j) * P
                w = (i0 + ni) * P - s0
                pe.wait_ge(exped, g + 1)
                if j == 0 and q >= 2:
                    pe.wait_ge(divided, q - 1)
                ins = nc.tensor.matmul(c.ps[:, 4 + q % 2, s0 - i0 * P:s0 - i0 * P + w], va[:, j, :], pr[:, g % 4, 0:w],
                                       start=(j == 0), stop=(j == i0 + ni - 1))
                ins.then_inc(summed, 1)

            for g, (q, i0, ni, j) in enumerate(turns):
                s0 = max(i0, j) * P
                w = (i0 + ni) * P - s0
                odd = w % 2
                if g >= 4:
                    pe.wait_ge(exped, g - 3)
                out = c.ps[0:P, g % 4, 0:w + odd]
                nc.tensor.matmul(out, kt[lo:lo + 64, j * P:j * P + P], qt[lo:lo + 64, s0 - odd:s0 + w], start=True, stop=False)
                ins = nc.tensor.matmul(out, c.minus[:, 0:P], dm[:, s0 - odd:s0 + w], start=False, stop=(j < i0))
                if j >= i0:
                    ins = nc.tensor.matmul(c.ps[0:P, g % 4, odd:odd + P], c.identb, c.mask_t, start=False, stop=True)
                ins.then_inc(turned, 1)
                if g >= 2:
                    weigh(g - 2)
            weigh(len(turns) - 2)
            weigh(len(turns) - 1)

        @block.scalar
        def _(act):
            for g, (q, i0, ni, j) in enumerate(turns):
                s0 = max(i0, j) * P
                w = (i0 + ni) * P - s0
                act.wait_ge(turned, g + 1)
                if g >= 4:
                    act.wait_ge(summed, g - 3)
                nc.scalar.activation(pr[:, g % 4, 0:w], c.ps[0:P, g % 4, w % 2:w % 2 + w], ACT.Exp).then_inc(exped, 1)

        @block.vector
        def _(v):
            link = chain(v, step)
            for i in range(T):
                v.wait_ge(scored, i + 1)
                nc.vector.tensor_reduce(mx[:, i:i + 1], flat[0:P, 2048 * (i % 2):2048 * (i % 2) + P * (i + 1)], AX.X,
                                        ALU.max).then_inc(maxed, 1)
            v.wait_ge(maxed, T)
            nc.vector.tensor_tensor(dm.rearrange("p (i q) -> p i q", q=P),
                                    c.ident[0:P, 0:P].unsqueeze(1).to_broadcast([P, T, P]),
                                    mx.unsqueeze(2).to_broadcast([P, T, P]), ALU.mult).then_inc(diag, 1)
            done = 0
            for q, (i0, ni) in enumerate(QUERIES):
                done += i0 + ni
                v.wait_ge(summed, done)
                cols = slice(i0 * P, (i0 + ni) * P)
                ps = c.ps[:, 4 + q % 2, 0:ni * P]
                link(nc.vector.reciprocal(rd[lo:lo + 64, 0:ni * P], ps[hi:hi + 64]))
                ins = nc.vector.tensor_tensor(ot[lo:lo + 64, cols], ps[lo:lo + 64], rd[lo:lo + 64, 0:ni * P], ALU.mult)
                ins.then_inc(divided, 1)
                v.wait_ge(divided, q + 1)


def stage_gate(c, logits, coef):
    nc = c.nc
    s8 = [P, T, 8]
    red = c.small[0:P, 200:230].rearrange("p (a t) -> p a t", a=3)
    with ExitStack() as s:
        a, b = (c.semaphore(n) for n in ("a", "b"))
        block = s.enter_context(nc.Block())

        @block.vector
        def _(v):
            link = chain(v, a)
            link(nc.vector.tensor_reduce(red[:, 0, :], logits, AX.X, ALU.max))
            link(nc.vector.tensor_tensor(coef, logits, red[:, 0, :].unsqueeze(2).to_broadcast(s8), ALU.subtract))
            v.wait_ge(b, 1)
            link(nc.vector.tensor_reduce(red[:, 1, :], coef, AX.X, ALU.add))
            link(nc.vector.reciprocal(red[:, 2, :], red[:, 1, :]))
            link(nc.vector.tensor_tensor(coef, coef, red[:, 2, :].unsqueeze(2).to_broadcast(s8), ALU.mult))

        @block.scalar
        def _(act):
            act.wait_ge(a, 2)
            nc.scalar.activation(coef, coef, ACT.Exp).then_inc(b, 1)


CAPACITY = 512


def stage_route(c, logits, coef, work):
    nc = c.nc
    s8 = [P, T, 8]
    f = work[0:P, 0:20 * 80].rearrange("p (a t e) -> p a t e", a=20, t=T)
    expert, left, same, key, one, two, both, slots, keep, spare = (f[:, k] for k in range(10))
    r = f[:, 10].rearrange("p t e -> p (t e)").rearrange("p (a t) -> p a t", t=T)
    m1, i1, m2, i2, d, e, w1, w2 = (r[:, k] for k in range(8))
    upper = work[0:P, 1700:1825]
    wide = lambda x: x.unsqueeze(2).to_broadcast(s8)
    with ExitStack() as s:
        sem = lambda n: c.semaphore(n)
        consts, step, counted, exped, step2 = map(sem, ("consts", "step", "counted", "exped", "step2"))
        block = s.enter_context(nc.Block())

        @block.gpsimd
        def _(pool):
            nc.gpsimd.iota(expert, [[0, T], [1, 8]], base=0, channel_multiplier=0,
                           allow_small_or_imprecise_dtypes=True).then_inc(consts, 1)
            nc.gpsimd.memset(upper, 1.0).then_inc(consts, 1)
            pool.wait_ge(consts, 2)
            nc.gpsimd.affine_select(out=upper, in_=upper, compare_op=ALU.is_gt, fill=0.0, base=0,
                                    pattern=[[1, P]], channel_multiplier=-1).then_inc(consts, 1)

        @block.vector
        def _(v):
            link = chain(v, step)
            v.wait_ge(consts, 3)

            def first(of, m, i, hot):
                link(nc.vector.tensor_reduce(m, of, AX.X, ALU.max))
                link(nc.vector.tensor_tensor(same, of, wide(m), ALU.is_equal))
                link(nc.vector.scalar_tensor_tensor(key, same, -100.0, expert, ALU.mult, ALU.add))
                link(nc.vector.tensor_reduce(i, key, AX.X, ALU.min))
                link(nc.vector.tensor_tensor(hot, key, wide(i), ALU.is_equal))

            first(logits, m1, i1, one)
            link(nc.vector.tensor_scalar(spare, one, -1.0, 1.0, ALU.mult, ALU.add))
            link(nc.vector.tensor_tensor(left, logits, spare, ALU.mult))
            link(nc.vector.scalar_tensor_tensor(left, one, -3e38, left, ALU.mult, ALU.add))
            first(left, m2, i2, two)
            link(nc.vector.tensor_tensor(both, one, two, ALU.add))
            link(nc.vector.tensor_tensor(d, m2, m1, ALU.subtract))
            v.wait_ge(exped, 1)
            link(nc.vector.tensor_scalar(w1, e, 1.0, None, ALU.add))
            link(nc.vector.reciprocal(w1, w1))
            link(nc.vector.tensor_tensor(w2, e, w1, ALU.mult))
            v.wait_ge(counted, 1)
            link(nc.vector.memset(spare[:, 0, :], 0.0))
            for t in range(1, T):
                link(nc.vector.tensor_tensor(spare[:, t, :], spare[:, t - 1, :], c.ps[0:P, 1, 8 * t - 8:8 * t], ALU.add))
            link(nc.vector.tensor_tensor(slots, spare, c.ps[0:P, 0, 0:80].rearrange("p (t e) -> p t e", e=8), ALU.add))
            link(nc.vector.tensor_scalar(keep, slots, float(CAPACITY), None, ALU.is_lt))
            link(nc.vector.tensor_tensor(one, one, wide(w1), ALU.mult))
            link(nc.vector.tensor_tensor(two, two, wide(w2), ALU.mult))
            link(nc.vector.tensor_tensor(one, one, two, ALU.add))
            link(nc.vector.tensor_tensor(coef, one, keep, ALU.mult))

        @block.scalar
        def _(act):
            act.wait_ge(step, 5 + 3 + 5 + 2)
            nc.scalar.activation(e, d, ACT.Exp).then_inc(exped, 1)

        @block.tensor
        def _(pe):
            pe.wait_ge(step, 5 + 3 + 5 + 1)
            flat = both.rearrange("p t e -> p (t e)")
            nc.tensor.matmul(c.ps[0:P, 0, 0:80], upper, flat, start=True, stop=True)
            nc.tensor.matmul(c.ps[0:P, 1, 0:80], c.ones[0:P, 0:P], flat, start=True, stop=True).then_inc(counted, 1)


def stage_experts(c, yt, coef, b1, w1_d, w2_d, hid):
    nc = c.nc
    w1 = [c.w[:, p].rearrange("p k d -> p (k d)")[:, 0:1024].rearrange("p (k f) -> p k f", k=KC) for p in range(2)]
    w2 = [c.w[:, p].rearrange("p k d -> p (k d)")[:, 1024:2048].rearrange("p (k f) -> p k f", k=2) for p in range(2)]
    with ExitStack() as s:
        sem = lambda n: c.semaphore(n)
        names = ("loaded0", "loaded1", "hid_made", "hid_out", "eo_made", "eo_out", "biased")
        loaded0, loaded1, hid_made, hid_out, eo_made, eo_out, biased = map(sem, names)
        loaded = (loaded0, loaded1)
        block = s.enter_context(nc.Block())

        @block.sync
        def _(sp):
            def load(e, par):
                sp.dma_start(w1[par], w1_d[bass.ds(e, 1)].rearrange("a (k p) f -> p (a k) f", p=128)).then_inc(loaded[par], 16)
                sp.dma_start(w2[par], w2_d[bass.ds(e, 1)].rearrange("a (k p) f -> p (a k) f", p=128)).then_inc(loaded[par], 16)

            load(0, 0)
            load(1, 1)
            with sp.Fori(1, 4) as i:
                for par in range(2):
                    sp.wait_ge(eo_made, i * (2 * T) + (par - 1) * T)
                    load(i * 2 + par, par)

        @block.tensor
        def _(pe):
            with pe.Fori(0, 4) as i:
                for par in range(2):
                    e = i * 2 + par
                    pe.wait_ge(loaded[par], i * 32 + 32)
                    for q, (f, (c0, n)) in enumerate((f, cols) for f in range(2) for cols in COLS):
                        pe.wait_ge(hid_out, e * 6 + (q + 1))
                        for k in range(KC):
                            ins = nc.tensor.matmul(c.ps[:, q % 3, 0:n], w1[par][:, k, 128 * f:128 * f + 128],
                                                   yt[:, k, c0:c0 + n], start=(k == 0), stop=(k == KC - 1))
                        ins.then_inc(hid_made, 1)
                    for t in range(T):
                        if t == 0:
                            pe.wait_ge(hid_out, e * 6 + 9)
                        pe.wait_ge(eo_out, e * T + (t + 1))
                        for f in range(2):
                            ins = nc.tensor.matmul(c.ps[0:P, 3 + t % 5, :], hid[par][:, f, t * P:t * P + P], w2[par][:, f, :],
                                                   start=(f == 0), stop=(f == 1))
                        ins.then_inc(eo_made, 1)

        @block.scalar
        def _(act):
            act.sem_inc(hid_out, 3)
            with act.Fori(0, 4) as i:
                for par in range(2):
                    e = i * 2 + par
                    bias = b1[:, 16 + 2 * par:18 + 2 * par]
                    nc.scalar.activation(bias, b1[:, bass.ds(e * 2, 2)], ACT.Copy).then_inc(biased, 1)
                    act.wait_ge(biased, e + 1)
                    for q, (f, (c0, n)) in enumerate((f, cols) for f in range(2) for cols in COLS):
                        act.wait_ge(hid_made, e * 6 + (q + 1))
                        nc.scalar.activation(hid[par][:, f, c0:c0 + n], c.ps[:, q % 3, 0:n], ACT.Gelu_apprx_tanh,
                                             bias=bias[:, f:f + 1]).then_inc(hid_out, 1)

        @block.vector
        def _(v):
            v.sem_inc(eo_out, 5)
            with v.Fori(0, 4) as i:
                for par in range(2):
                    e = i * 2 + par
                    for t in range(T):
                        v.wait_ge(eo_made, e * T + (t + 1))
                        x = c.x[0:P, t, :]
                        nc.vector.scalar_tensor_tensor(x, c.ps[0:P, 3 + t % 5, :], coef[:, t, bass.ds(e, 1)], x,
                                                       ALU.mult, ALU.add).then_inc(eo_out, 1)


def add_to_x(c, t, extra=None, scale=None, relu=False):
    def copy(e, ps, link):
        x = c.x[0:P, t, :]
        v = c.nc.vector
        if relu:
            m = c.big[0:P, 12600 + 512 * (t % 2):13112 + 512 * (t % 2)]
            link(v.tensor_scalar(m, ps, scale, 0.0, ALU.mult, ALU.max))
            return v.tensor_tensor(x, x, m, ALU.add)
        if extra is not None:
            link(v.tensor_tensor(x, x, extra, ALU.add))
        return v.tensor_tensor(x, x, ps, ALU.add)
    return copy


def mixture(c, a, pre, yt, gate_w, gate_b, b1_d, w1_d, w2_d, b2_d, route, base):
    big = c.big
    lt = big[0:8, base:base + N]
    coef_t = big[0:8, base + N:base + 2 * N]
    coef = big[0:P, base + 2 * N:base + 2 * N + 80].rearrange("p (t e) -> p t e", e=8)
    logits = big[0:P, base + 2 * N + 80:base + 2 * N + 160].rearrange("p (t e) -> p t e", e=8)
    b1 = big[:, base + 2 * N + 722:base + 2 * N + 742]
    b2 = big[0:8, base + 2 * N + 176:base + 2 * N + 688]
    gw = big[:, base + 2 * N + 688:base + 2 * N + 720].rearrange("p (k e) -> p k e", k=KC)
    gb = big[0:8, base + 2 * N + 720:base + 2 * N + 721]
    hid = [big[:, 5000 + 2500 * k:7500 + 2500 * k].rearrange("p (f n) -> p f n", f=2) for k in range(2)]
    c.recycle()
    loads = [(gw, gate_w.rearrange("(k p) e -> p k e", p=128)), (b1[:, 0:16], b1_d.rearrange("e (f p) -> p (e f)", p=128)), (b2, b2_d)]
    if gate_b is not None:
        loads.append((gb, gate_b.rearrange("(e o) -> e o", o=1)))
    tiles_on_tensor(c, [], loads)
    if gate_b is not None:
        copies = lambda m, cols: biased_to(lt[:, cols], gb)
    else:
        copies = lambda m, cols: copy_to(lt[:, cols])
    tiles_on_tensor(c, turned_product(gw, yt, 8, copies))
    tiles_on_tensor(c, [(P, 80, ("turn", [lt[:, t * P:t * P + P] for t in range(T)]),
                         copy_to(logits.rearrange("p t e -> p (t e)")))])
    if route:
        stage_route(c, logits, coef, big[:, 5000:7500])
    else:
        stage_gate(c, logits, coef)
    tiles_on_tensor(c, [(8, n * P, ("turn", [coef[:, t, :] for t in range(t0, t0 + n)]),
                         copy_to(coef_t[:, t0 * P:(t0 + n) * P])) for t0, n in QUERIES])
    tiles_on_tensor(c, [(P, D, [(coef_t[:, t * P:t * P + P], b2)], add_to_x(c, t)) for t in range(T)], only_vector=True)
    stage_experts(c, yt, coef, b1, w1_d, w2_d, hid)


def stage_loop_add_identity(c, b):
    nc = c.nc
    with nc.Block() as block:
        @block.vector
        def _(v):
            for i in range(T):
                d = b[:, i, P * i:P * i + P]
                nc.vector.tensor_tensor(d, d, c.ident[0:P, 0:P], ALU.add)


def stage_key_softmax(c, ke):
    nc = c.nc
    r = c.small[:, 0:8]
    with ExitStack() as s:
        a, b = (c.semaphore(n) for n in ("a", "b"))
        block = s.enter_context(nc.Block())

        @block.vector
        def _(v):
            link = chain(v, a)
            link(nc.vector.tensor_reduce(r[:, 0:2], ke, AX.X, ALU.max))
            link(nc.vector.tensor_scalar(r[:, 2:4], r[:, 0:2], -1.0, None, ALU.mult))
            v.wait_ge(b, 2)
            link(nc.vector.reciprocal(r[:, 6:8], r[:, 4:6]))
            for g in range(2):
                nc.vector.tensor_scalar(ke[:, g, :], ke[:, g, :], r[:, 6 + g:7 + g], None, ALU.mult)

        @block.scalar
        def _(act):
            act.wait_ge(a, 2)
            for g in range(2):
                nc.scalar.activation(ke[:, g, :], ke[:, g, :], ACT.Exp, bias=r[:, 2 + g:3 + g],
                                     accum_out=r[:, 4 + g:5 + g]).then_inc(b, 1)


def stage_query_softmax(c, q):
    nc = c.nc
    g = q.rearrange("p t (h s) -> p (t h) s", s=32)
    r = c.small[0:P, 0:240].rearrange("p (a k) -> p a k", a=3)
    wide = lambda x: x.unsqueeze(2).to_broadcast([P, 80, 32])
    with ExitStack() as s:
        a, b = (c.semaphore(n) for n in ("a", "b"))
        block = s.enter_context(nc.Block())

        @block.vector
        def _(v):
            link = chain(v, a)
            link(nc.vector.tensor_reduce(r[:, 0, :], g, AX.X, ALU.max))
            link(nc.vector.tensor_tensor(g, g, wide(r[:, 0, :]), ALU.subtract))
            v.wait_ge(b, 1)
            link(nc.vector.tensor_reduce(r[:, 1, :], g, AX.X, ALU.add))
            link(nc.vector.reciprocal(r[:, 2, :], r[:, 1, :]))
            link(nc.vector.tensor_tensor(g, g, wide(r[:, 2, :]), ALU.mult))

        @block.scalar
        def _(act):
            act.wait_ge(a, 2)
            nc.scalar.activation(q, q, ACT.Exp).then_inc(b, 1)


def stage_l1_mix(c, a):
    big = c.big
    adj = c.adj[:].rearrange("p s d -> p (s d)")
    xm = big[:, 0:5000].rearrange("p (k n) -> p k n", k=KC)
    ke = big[:, 5000:7500].rearrange("p (g n) -> p g n", g=2)
    wk = big[:, 7500:7756].rearrange("p (a s) -> p a s", a=2)
    wqv = big[:, 7756:7948]
    kvb = big[:, 7948:8460].rearrange("p (g d) -> p g d", g=2)
    b_in = big[:, 8460:8464]
    b_out = big[0:P, 8470:8982]
    out_t = big[:, 9000:14000].rearrange("p (k n) -> p k n", k=KC)
    qn = adj[0:P, 0:2560].rearrange("p (t s) -> p t s", t=T)
    kn = adj[0:P, 2560:5120].rearrange("p (t s) -> p t s", t=T)
    qt = adj[:, 5200:7700].rearrange("p (g n) -> p g n", g=2)
    vn = c.nat
    memsets(c, [wk, wqv, kvb])
    loads = [weight(c, 0, a["L1_mix_W_in"]), weight(c, 1, a["L1_mix_W_out"]), (b_in, column(a["L1_mix_b_in"])),
             (b_out, a["L1_mix_b_out"].partition_broadcast(P))]
    for h in range(2):
        rows = slice(64 * h, 64 * h + 64)
        for k in range(2):
            loads.append((wk[rows, k, 64 * k + 32 * h:64 * k + 32 * h + 32], a["L1_mix_Wk"]))
        loads.append((wqv[rows, 32 * h:32 * h + 32], a["L1_mix_Wq"]))
        loads.append((wqv[rows, 64 + 64 * h:128 + 64 * h], a["L1_mix_Wv"]))
    tiles_on_tensor(c, [], loads)
    tiles_on_tensor(c, turned_product(c.w[:, 0], c.xt, D, lambda m, cols: biased_to(xm[:, m, cols], b_in[:, m:m + 1])))
    tiles_on_tensor(c, [(128, n, [(wk[:, k, :], xm[:, 2 * g + k, c0:c0 + n]) for k in range(2)],
                         copy_to(ke[:, g, c0:c0 + n])) for g in range(2) for c0, n in COLS])

    def qv(t, m):
        def copy(e, ps, link):
            cp = (lambda o, i: e.activation(o, i, ACT.Copy)) if is_scalar(e) else e.tensor_copy
            cp(qn[:, t, 64 * m:64 * m + 64], ps[:, 0:64])
            return cp(vn[0:P, t, 128 * m:128 * m + 128], ps[:, 64:192])
        return copy
    tiles_on_tensor(c, [(P, 192, [(xm[:, m, t * P:t * P + P], wqv)], qv(t, m)) for t in range(T) for m in range(KC)])
    c.recycle()
    stage_key_softmax(c, ke)
    stage_query_softmax(c, qn)
    tiles_on_tensor(c, [(P, 256, ("turn", [ke[:, g, t * P:t * P + P] for g in range(2)]), copy_to(kn[:, t, :]))
                        for t in range(T)])

    def blocks(g):
        def copy(e, ps, link):
            cp = (lambda o, i: e.activation(o, i, ACT.Copy)) if is_scalar(e) else e.tensor_copy
            for h in range(4):
                ins = cp(kvb[32 * h:32 * h + 32, g, 64 * h:64 * h + 64], ps[32 * h:32 * h + 32, 64 * h:64 * h + 64])
            return ins
        return copy
    tiles_on_tensor(c, [(128, 256, [(kn[:, t, 128 * g:128 * g + 128], vn[0:P, t, 256 * g:256 * g + 256]) for t in range(T)],
                         blocks(g)) for g in range(2)])
    tiles_on_tensor(c, [(128, n * P, ("turn", [qn[:, t, 128 * g:128 * g + 128] for t in range(t0, t0 + n)]),
                         copy_to(qt[:, g, t0 * P:(t0 + n) * P])) for g in range(2) for t0, n in QUERIES])
    tiles_on_tensor(c, [(128, n, [(kvb[:, m // 2, 128 * (m % 2):128 * (m % 2) + 128], qt[:, m // 2, c0:c0 + n])],
                         copy_to(out_t[:, m, c0:c0 + n])) for m in range(KC) for c0, n in COLS])
    tiles_on_tensor(c, natural_product(out_t, c.w[:, 1], lambda t: add_to_x(c, t, extra=b_out)), only_vector=True)


STOP = 9


def build(nc, a, out):
    with ExitStack() as ctx:
        ctx.enter_context(nc.allow_non_contiguous_dma(reason="bias and gain vectors of 512 values, by feature"))
        c = Chip(nc, ctx)
        with ExitStack() as edges:
            m = Edges(nc, edges)
            stage_codes(c, m, a["x"], a["src"], a["dst"])
            stage_adjacency(c, m)
        layer0_graph(c, a)
        layer0_attention(c, a)
        layer1(c, a)
        finish(c, out)


def layer0_graph(c, a):
    with ExitStack() as ctx:
        big = c.work(ctx, "graph", 17500)
        c.inv_t = big[:, 16250:17500]
        wq, wkv = a["L0_mix_Wq"], a["L0_mix_Wkv"]
        tiles_on_tensor(c, [], [weight(c, 0, wq), weight(c, 1, wkv[0:D]), weight(c, 2, wkv[D:2 * D])])
        stage_degrees(c)
        c.recycle()
        stage_layernorm(c, c.x, c.nat)
        tiles_on_tensor(c, turn(c.nat, c.xt))
        stage_l0_mix(c, a)
        c.recycle()
        ha = big[:, 0:5000].rearrange("p (k n) -> p k n", k=KC)
        hb = big[:, 5000:10000].rearrange("p (k n) -> p k n", k=KC)
        b_all = big[0:P, 14700:15212]
        h = c.xt
        for layer in range(3):
            loads = [weight(c, 0, a["L0_gnn_Ws_self"][layer]), weight(c, 1, a["L0_gnn_Ws_neigh"][layer])]
            loads.append((b_all, a["L0_gnn_bs"][2].partition_broadcast(P)) if layer == 2 else
                         (c.gain[:, 0:KC], column(a["L0_gnn_bs"][layer])))
            tiles_on_tensor(c, [], loads)
            tiles_on_tensor(c, natural_product(h, c.w[:, 1], lambda t: copy_to(c.nat[0:P, t, :])))
            if layer < 2:
                to = (ha, hb)[layer]
                stage_aggregate(c, h, to, c.nat, c.gain, True)
                h = to
            else:
                stage_aggregate_natural(c, h, c.nat, b_all)


def layer0_attention(c, a):
    with ExitStack() as ctx:
        big = c.work(ctx, "attention", 13550, rounded=3 * N + 128)
        c.recycle()
        g, b, qg, kg = c.gain[:, 0:4], c.gain[:, 4:8], c.gain[:, 8:9], c.gain[:, 9:10]
        loads = [(g, column(a["L0_ffn_ln_g"])), (b, column(a["L0_ffn_ln_b"])), weight(c, 0, a["L0_ffn_Wv"]), weight(c, 1, a["L0_ffn_Wk"])]
        for k in range(2):
            loads.append((qg[64 * k:64 * k + 64], a["L0_ffn_qn_g"].rearrange("(p o) -> p o", o=1)))
            loads.append((kg[64 * k:64 * k + 64], a["L0_ffn_kn_g"].rearrange("(p o) -> p o", o=1)))
        tiles_on_tensor(c, [], loads)
        stage_layernorm(c, c.x, c.nat)
        stage_layernorm(c, c.nat, c.nat)
        tiles_on_tensor(c, turn(c.nat, c.xt, lambda k, to: scaled_to(to, g[:, k:k + 1], b[:, k:k + 1])))
        tiles_on_tensor(c, natural_product(c.xt, c.w[:, 0], lambda t: copy_to(c.nat[0:P, t, :])))
        tiles_on_tensor(c, [], [weight(c, 0, a["L0_ffn_Wq"])])
        stage_attention_constants(c)
        stage_scale8(c, kg)
        ot = big[:, 0:5000].rearrange("p (k n) -> p k n", k=KC)
        qt, kt, work = big[:, 5000:6250], big[:, 6250:7500], big[:, 7500:8750]
        qr, kr, dm = c.rounded[:, 0:N], c.rounded[:, N:2 * N], c.rounded[0:P, 2 * N:3 * N]
        pr = big[0:P, 8750:10750].rearrange("p (b n) -> p b n", b=4)
        va = big[0:P, 10750:12030].rearrange("p (t d) -> p t d", t=T)
        rd = big[:, 12050:12550]
        for p in range(4):
            tiles_on_tensor(c, [(128, n, [(c.w[:, 1 - z, k, 128 * p:128 * p + 128], c.xt[:, k, c0:c0 + n]) for k in range(KC)],
                                 copy_to((kt if z == 0 else qt)[:, c0:c0 + n])) for z in range(2) for c0, n in COLS])
            c.recycle()
            stage_unit(c, qt, qr, qg, work)
            stage_unit(c, kt, kr, kg, work)
            for par in range(2):
                stage_head(c, 2 * p + par, qt, kt, qr, kr, dm, pr, va, ot[:, p], rd)
        tiles_on_tensor(c, [], [weight(c, 0, a["L0_ffn_Wo"])])
        tiles_on_tensor(c, turned_product(c.w[:, 0], ot, D, lambda m, cols: copy_to(c.xt[:, m, cols])))
        mixture(c, a, "L0_ffn", c.xt, a["L0_ffn_gate_W"], a["L0_ffn_gate_b"], a["L0_ffn_b1"], a["L0_ffn_W1"],
                a["L0_ffn_W2"], a["L0_ffn_b2"], False, 10000)


def layer1(c, a):
    with ExitStack() as ctx:
        big = c.work(ctx, "layer1", 17500)
        c.recycle()
        stage_layernorm(c, c.x, c.nat)
        tiles_on_tensor(c, turn(c.nat, c.xt), [weight(c, 0, a["L1_gnn_weight"])])
        tiles_on_tensor(c, natural_product(c.xt, c.w[:, 0], lambda t: scaled_to(c.nat[0:P, t, :], c.out_n[0:P, t:t + 1])))
        rev = big[0:P, 0:12500].rearrange("p (i n) -> p i n", i=T)
        tiles_on_tensor(c, [(P, n * P, ("turn", [c.adj[0:P, t, P * i:P * i + P] for t in range(t0, t0 + n)]),
                             copy_to(rev[:, i, t0 * P:(t0 + n) * P])) for i in range(T) for t0, n in QUERIES])
        c.recycle()
        stage_loop_add_identity(c, rev)
        tiles_on_tensor(c, [(P, D, [(rev[:, i, t * P:t * P + P], c.nat[0:P, i, :]) for i in range(T)],
                             add_to_x(c, t, relu=True, scale=c.out_n[0:P, t:t + 1])) for t in range(T)], only_vector=True)
        stage_l1_mix(c, a)
        c.recycle()
        stage_layernorm(c, c.x, c.nat)
        tiles_on_tensor(c, turn(c.nat, c.xt))
        mixture(c, a, "L1_ffn", c.xt, a["L1_ffn_router_w"], None, a["L1_ffn_b1"], a["L1_ffn_w1"], a["L1_ffn_w2"],
                a["L1_ffn_b2"], True, 10000)


def stage_scale8(c, kg):
    nc = c.nc
    with nc.Block() as block:
        @block.vector
        def _(v):
            nc.vector.tensor_scalar(kg, kg, 8.0, None, ALU.mult)


def finish(c, out):
    nc = c.nc
    with ExitStack() as s:
        stored = c.semaphore("stored")
        block = s.enter_context(nc.Block())

        @block.sync
        def _(sp):
            sp.dma_start(out.rearrange("(t p) d -> p t d", p=P), c.x[0:P]).then_inc(stored, 16)
            sp.wait_ge(stored, 16)


def kernel(**inputs):
    import concourse.bacc as bacc
    from concourse.bass_utils import run_bass_kernel_spmd

    nc = bacc.Bacc("TRN2", target_bir_lowering=False, num_devices=1)
    arrays, aps = {}, {}
    for name, value in inputs.items():
        a = np.ascontiguousarray(value)
        arrays["in_" + name] = a
        aps[name] = nc.dram_tensor("in_" + name, a.shape, mybir.dt.from_np(a.dtype), kind="ExternalInput").ap()
    out = nc.dram_tensor("out", (N, D), F32, kind="ExternalOutput").ap()
    build(nc, aps, out)
    return run_bass_kernel_spmd(nc, [arrays], core_ids=[0]).results[0]["out"]
```

```python
from contextlib import ExitStack

import numpy as np
import concourse.bass as bass
from concourse import mybir

F32 = mybir.dt.float32
F32R = mybir.dt.float32r
BF16 = mybir.dt.bfloat16
I32 = mybir.dt.int32
I16 = mybir.dt.int16
ALU = mybir.AluOpType
ACT = mybir.ActivationFunctionType
AX = mybir.AxisListType

N = 1250
D = 512
P = 125
T = N // P
KC = D // 128
EDGES = 41250
SUPERS = 110
SUB = 3
CHUNKS = SUPERS * SUB
STRIDE = 3
PAD = (STRIDE - 1) * SUB
SPARE = STRIDE * SUB
W = 500
WINDOWS = N * T // W
COLS = [(0, 418), (418, 416), (834, 416)]
EPS = 1e-5
EXACT_COUNT = 4000.0


class Chip:

    def __init__(self, nc, ctx):
        def sb(name, shape, dt):
            return ctx.enter_context(nc.sbuf_tensor(name, shape, dt))

        self.nc = nc
        self.in_use = []
        self.named = 0
        self.adj = sb("adj", [128, T, N], F32R)
        self.x = sb("x", [128, T, D], F32)
        self.ident = sb("ident", [128, 128], F32)
        self.ones = sb("ones", [128, 128], F32)
        self.inv_n = sb("inv_n", [128, T], F32)
        self.out_n = sb("out_n", [128, T], F32)
        self.gain = sb("gain", [128, 16], F32)
        self.small = sb("small", [128, 512], F32)
        self.ident_r = sb("ident_r", [P, 126], F32R)
        self.eps = sb("eps", [128, 1], F32)
        self.many = sb("many", [1, 2], I32)
        self.ps = ctx.enter_context(nc.psum_tensor("ps", [128, 8, 512], F32))

    def semaphore(self, name):
        self.named += 1
        handle = self.nc.alloc_semaphore(name=f"{name}_{self.named}")
        self.in_use.append(handle)
        return handle

    def recycle(self):
        self.nc.clear_and_free_semaphores(self.in_use)
        self.nc.all_engine_barrier()
        self.in_use = []


class Edges:

    def __init__(self, nc, ctx):
        def sb(name, shape, dt):
            return ctx.enter_context(nc.sbuf_tensor(name, shape, dt))

        self.ends = sb("ends", [SUPERS, 2, SUB * P], I32)
        self.f = sb("codes", [SUPERS, 4, SUB * P], F32)
        self.gcol = sb("gcol", [P, CHUNKS + PAD + SPARE], F32)
        self.lcol = sb("lcol", [P, CHUNKS + PAD + SPARE], F32)
        self.iota = sb("iota", [P, W], I16)
        self.local_hot = sb("local_hot", [P, CHUNKS + PAD + SPARE, P], BF16)
        self.counts = sb("counts", [P, 3, T, W // T], F32)
        self.square = sb("square", [P, 2, P], F32)
        self.code_hot = sb("code_hot", [P, STRIDE * SUB, W], BF16)
        self.zeros = sb("zeros", [P, P], BF16)
        self.marks = sb("marks", [SUPERS, 6, WINDOWS], F32)
        self.few = sb("few", [128, 8], F32)
        self.line = sb("line", [1, 6, WINDOWS], F32)
        self.bounds = sb("bounds", [1, 2, WINDOWS], I32)


def stage_codes(c, m, x, src, dst):
    nc = c.nc
    srcf, dstf, tile, local = (m.f[:, k, :] for k in range(4))
    code = dstf
    least, most, rowno, up, down = (m.few[0:SUPERS, k:k + 1] for k in range(5))
    wbase, low, high, meets = (m.marks[:, k, :] for k in range(4))
    marks = m.marks[:, 4:6, :].rearrange("p a w -> p (a w)")
    ends = m.few[0:2 * WINDOWS, 5:6]
    last, first, rows, before, bases, ones = (m.line[:, k, :] for k in range(6))
    loaded_x, loaded_e, const, iota, step, turned, maxed = map(c.semaphore, (
        "loaded_x", "loaded_e", "const", "iota", "step", "turned", "maxed"))
    LOCAL, CODE = 2 + (T - 1) + 1, 2 + (T - 1) + 2
    MARKS = CODE + 2 + 7
    CHUNKED = MARKS + 6
    with nc.Block() as block:
        @block.sync
        def _(sp):
            sp.dma_start(m.ends[:, 0, :], src.rearrange("(s e) -> s e", s=SUPERS)).then_inc(loaded_e, 16)
            sp.dma_start(m.ends[:, 1, :], dst.rearrange("(s e) -> s e", s=SUPERS)).then_inc(loaded_e, 16)
            sp.dma_start(c.x[0:P], x.rearrange("(t p) d -> p t d", p=P)).then_inc(loaded_x, 16)
            sp.wait_ge(loaded_x, 16)

        @block.gpsimd
        def _(pool):
            nc.gpsimd.memset(c.ident[:], 0.0).then_inc(const, 1)
            nc.gpsimd.memset(c.ones[:], 1.0).then_inc(const, 1)
            nc.gpsimd.iota(wbase, [[W, WINDOWS]], base=0, channel_multiplier=0,
                           allow_small_or_imprecise_dtypes=True).then_inc(const, 1)
            nc.gpsimd.iota(rowno, [[0, 1]], base=0, channel_multiplier=1,
                           allow_small_or_imprecise_dtypes=True).then_inc(const, 1)
            pool.wait_ge(const, 4)
            nc.gpsimd.affine_select(out=c.ident[:], in_=c.ident[:], compare_op=ALU.not_equal, fill=1.0, base=0,
                                    pattern=[[-1, 128]], channel_multiplier=1).then_inc(const, 1)
            nc.gpsimd.memset(m.zeros[:], 0.0).then_inc(iota, 1)
            nc.gpsimd.memset(c.eps[:], EPS).then_inc(iota, 1)
            nc.gpsimd.iota(m.iota[:], [[1, W]], base=0, channel_multiplier=0).then_inc(iota, 1)
            nc.gpsimd.memset(m.gcol[:, CHUNKS:], -1.0).then_inc(iota, 1)
            nc.gpsimd.memset(m.lcol[:, CHUNKS:], -1.0).then_inc(iota, 1)

        @block.vector
        def _(v):
            link = chain(v, step)
            v.wait_ge(loaded_e, 32)
            link(nc.vector.tensor_copy(srcf, m.ends[:, 0, :]))
            link(nc.vector.tensor_copy(dstf, m.ends[:, 1, :]))
            link(nc.vector.tensor_scalar(tile, srcf, float(P), None, ALU.is_ge))
            for j in range(2, T):
                link(nc.vector.scalar_tensor_tensor(tile, srcf, float(P * j), tile, ALU.is_ge, ALU.add))
            link(nc.vector.scalar_tensor_tensor(local, tile, float(-P), srcf, ALU.mult, ALU.add))
            link(nc.vector.scalar_tensor_tensor(code, dstf, float(T), tile, ALU.mult, ALU.add))
            link(nc.vector.tensor_reduce(most, code, AX.X, ALU.max))
            link(nc.vector.tensor_reduce(least, code, AX.X, ALU.min))
            v.wait_ge(const, 5)
            link(nc.vector.tensor_scalar(low, wbase, most, None, ALU.is_le))
            link(nc.vector.tensor_scalar(high, wbase, float(W - 1), least, ALU.add, ALU.is_ge))
            link(nc.vector.tensor_tensor(meets, low, high, ALU.mult))
            link(nc.vector.tensor_scalar(up, rowno, 1.0, None, ALU.add))
            link(nc.vector.tensor_scalar(down, rowno, -1.0, float(SUPERS), ALU.mult, ALU.add))
            link(nc.vector.tensor_scalar(marks[:, 0:WINDOWS], meets, up, None, ALU.mult))
            link(nc.vector.tensor_scalar(marks[:, WINDOWS:], meets, down, None, ALU.mult))
            v.wait_ge(turned, 6)
            for k in range(6):
                to = (m.lcol if k < 3 else m.gcol)[:, 0:CHUNKS].rearrange("p (s j) -> p s j", j=SUB)
                link(nc.vector.tensor_copy(to[:, :, k % 3], c.ps[0:P, k, 0:SUPERS]))
            v.wait_ge(turned, 7)
            nc.vector.tensor_reduce(ends, c.ps[0:2 * WINDOWS, 6, 0:SUPERS], AX.X, ALU.max).then_inc(maxed, 1)
            link(nc.vector.memset(ones, 1.0))
            v.wait_ge(turned, 8)
            link(nc.vector.tensor_copy(m.line[:, 0:2, :].rearrange("p a w -> p (a w)"), c.ps[0:1, 7, 0:2 * WINDOWS]))
            link(nc.vector.tensor_scalar(last, last, 1.0, None, ALU.max))
            link(nc.vector.tensor_scalar(first, first, -1.0, float(SUPERS), ALU.mult, ALU.add))
            link(nc.vector.scalar_tensor_tensor(first, last, -1.0, first, ALU.add, ALU.min))
            link(nc.vector.tensor_tensor(rows, last, first, ALU.subtract))
            link(nc.vector.tensor_scalar(rows, rows, 1.0, 1.0 / STRIDE, ALU.add, ALU.mult))
            link(nc.vector.tensor_scalar(rows, rows, float(2 ** 23), float(-2 ** 23), ALU.add, ALU.add))
            link(nc.vector.tensor_scalar(rows, rows, float(STRIDE), None, ALU.mult))
            link(nc.vector.tensor_tensor(last, first, rows, ALU.add))
            link(nc.vector.tensor_tensor_scan(before, ones, rows, 0.0, ALU.mult, ALU.add))
            link(nc.vector.tensor_tensor(before, before, last, ALU.subtract))
            link(nc.vector.tensor_scalar(m.bounds[:, 1, :], before, float(SUB), float(CHUNKS), ALU.mult, ALU.add))
            link(nc.vector.scalar_tensor_tensor(bases, first, 512.0, last, ALU.mult, ALU.add))
            link(nc.vector.tensor_scalar(m.bounds[:, 0, :], bases, float(SUB), None, ALU.mult))

        @block.tensor
        def _(pe):
            pe.wait_ge(const, 5)
            for k in range(6):
                pe.wait_ge(step, LOCAL if k < 3 else CODE)
                of = (local if k < 3 else code).rearrange("p (j e) -> p j e", j=SUB)
                nc.tensor.transpose(c.ps[0:P, k, 0:SUPERS], of[:, k % 3, :], c.ident[0:SUPERS, 0:SUPERS]).then_inc(turned, 1)
            pe.wait_ge(step, MARKS)
            nc.tensor.transpose(c.ps[0:2 * WINDOWS, 6, 0:SUPERS], marks, c.ident[0:SUPERS, 0:SUPERS]).then_inc(turned, 1)
            pe.wait_ge(maxed, 1)
            nc.tensor.transpose(c.ps[0:1, 7, 0:2 * WINDOWS], ends, c.ident[0:2 * WINDOWS, 0:2 * WINDOWS]).then_inc(turned, 1)


NORMAL_AT = 12


def stage_adjacency(c, m, nat):
    nc = c.nc
    minus_mean, squares, inverse, shift = (c.small[0:P, k:k + T] for k in range(0, 4 * T, T))
    hot, used, window_done, window_free, local_pool, local_act, squared, kept, moments, inverted = map(c.semaphore, (
        "hot", "used", "window_done", "window_free", "local_pool", "local_act", "squared", "kept", "moments", "inverted"))

    def bounds(engine, w):
        both = engine.value_load(m.bounds[0:1, 0, w:w + 1], min_val=0, max_val=512 * CHUNKS - 1)
        made = engine.value_load(m.bounds[0:1, 1, w:w + 1], min_val=0, max_val=(CHUNKS + PAD) * (WINDOWS + 1))
        return (engine.snap(both >> 9).with_bounds(min_val=0, max_val=CHUNKS - SUB), engine.snap(both & 511).with_bounds(min_val=SUB, max_val=CHUNKS + PAD), made)

    with nc.Block() as block:
        @block.gpsimd
        def _(pool):
            for k in range(CHUNKS + PAD):
                if k % 6:
                    nc.gpsimd.tensor_scalar(m.local_hot[:, k, :], m.iota[:, 0:P], m.lcol[:, k:k + 1], None,
                                            ALU.is_equal).then_inc(local_pool, 2 if k % 6 == 1 else 1)

        @block.vector
        def _(v):
            for w in range(WINDOWS):
                first, end, made = bounds(v, w)
                with v.Fori(first, end, STRIDE * SUB) as r:
                    for j in range(STRIDE * SUB):
                        v.wait_ge(used, made + r + (j + 1))
                        nc.vector.tensor_scalar(m.code_hot[:, j, :], m.iota[:], m.gcol[:, bass.ds(r + j, 1)],
                                                float(-W * w), ALU.subtract, ALU.is_equal).then_inc(hot, 1)
                if w == NORMAL_AT:
                    v.wait_ge(moments, 2 * T + 2)
                    nc.vector.reciprocal(inverse, squares).then_inc(inverted, 1)
                    v.wait_ge(inverted, 1)
                    nc.vector.tensor_tensor(shift, minus_mean, inverse, ALU.mult).then_inc(inverted, 1)

        @block.tensor
        def _(pe):
            pe.sem_inc(used, STRIDE * SUB + CHUNKS)
            pe.sem_inc(hot, CHUNKS)
            for w in range(WINDOWS):
                first, end, made = bounds(pe, w)
                if w >= 8:
                    pe.wait_ge(window_free, w - 7)
                for local in (local_pool, local_act):
                    if w == 0:
                        pe.wait_ge(local, 6)
                    pe.wait_ge(local, end)
                out = c.ps[0:P, w % 8, 0:W]
                nc.tensor.matmul(out, m.zeros[:], m.local_hot[:, 0:W // P, :], start=True, stop=False)
                with pe.Fori(first, end, STRIDE * SUB) as r:
                    for j in range(STRIDE * SUB):
                        pe.wait_ge(hot, made + r + (j + 1))
                        nc.tensor.matmul(out, m.local_hot[:, bass.ds(r + j, 1), :], m.code_hot[:, j, :], start=False,
                                         stop=False).then_inc(used, 1)
                nc.tensor.matmul(out, m.zeros[:], m.local_hot[:, 0:W // P, :], start=False,
                                 stop=True).then_inc(window_done, 1)

        @block.scalar
        def _(act):
            for i, k in enumerate(range(0, CHUNKS + PAD, 6)):
                square = m.square[:, i % 2, :]
                if i >= 2:
                    act.wait_ge(local_act, 6 * (i - 1))
                nc.scalar.activation(square, m.iota[:, 0:P], ACT.Square, scale=-1.0, bias=m.lcol[:, k:k + 1]).then_inc(squared, 1)
                act.wait_ge(squared, i + 1)
                nc.scalar.activation(m.local_hot[:, k, :], square, ACT.Relu, scale=-1.0,
                                     bias=c.ones[0:P, 0:1]).then_inc(local_act, 6)
            for t in range(T):
                nc.scalar.activation(nat[0:P, t, :], c.x[0:P, t, :], ACT.Copy, scale=-1.0 / D,
                                     accum_out=minus_mean[:, t:t + 1]).then_inc(moments, 1)
            act.wait_ge(moments, T)
            for t in range(T):
                nc.scalar.activation(nat[0:P, t, :], c.x[0:P, t, :], ACT.Square, bias=minus_mean[:, t:t + 1],
                                     accum_out=squares[:, t:t + 1]).then_inc(moments, 1)
            act.wait_ge(moments, 2 * T)
            nc.scalar.activation(squares, squares, ACT.Sqrt, scale=1.0 / D, bias=c.eps[0:P, :]).then_inc(moments, 2)
            for w in range(WINDOWS):
                act.wait_ge(window_done, w + 1)
                if w >= 3:
                    act.wait_ge(kept, 16 * (w - 2))
                nc.scalar.activation(m.counts[:, w % 3],
                                     c.ps[0:P, w % 8, 0:W].rearrange("p (d t) -> p t d", t=T),
                                     ACT.Copy).then_inc(window_free, 1)
                if w == NORMAL_AT:
                    act.wait_ge(inverted, 2)
                    for t in range(T):
                        nc.scalar.activation(nat[0:P, t, :], c.x[0:P, t, :], ACT.Identity, scale=inverse[:, t:t + 1],
                                             bias=shift[:, t:t + 1])

        @block.sync
        def _(sp):
            for w in range(WINDOWS):
                sp.wait_ge(window_free, w + 1)
                if w:
                    sp.wait_ge(kept, 16 * w)
                sp.dma_start(c.adj[0:P, :, w * (W // T):(w + 1) * (W // T)].bitcast(F32), m.counts[:, w % 3]).then_inc(kept, 16)
            sp.wait_ge(kept, 16 * WINDOWS)


def load_all(block, loads, loaded):
    @block.sync
    def _(sp):
        for to, of in loads:
            sp.dma_start(to, of).then_inc(loaded, 16)
        if loads:
            sp.wait_ge(loaded, 16 * len(loads))


def moments_of(c):
    return (c.small[0:P, 60:80].rearrange("p (t s) -> p t s", t=T), c.small[0:P, 0:60].rearrange("p (t s) -> p t s", t=T))


def take_moments(c, v, t, link):
    mv, stats = moments_of(c)
    link(v.bn_stats(stats[:, t, :], c.x[0:P, t, :]))
    return v.bn_aggr(mv[:, t, :], stats[:, t, :])


def stage_layernorm(c, nat, to, gains=None, loads=(), twice=False, taken=False):
    nc = c.nc
    of = c.x
    mv, stats = moments_of(c)
    root, inverse, second = (c.small[0:P, a:a + 10] for a in (80, 90, 100))
    tiles = [(t0, n, k) for t0, n in QUERIES for k in range(KC)]
    with ExitStack() as s:
        stats_done, moments, shifted, rooted, inverted, loaded, normal, made, copied, low_done, scaled = map(c.semaphore, (
            "stats_done", "moments", "shifted", "rooted", "inverted", "loaded", "normal", "made", "copied", "low_done", "scaled"))
        block = s.enter_context(nc.Block())
        if loads:
            load_all(block, loads, loaded)

        @block.scalar
        def _(act):
            for k in range(2 if twice else 1):
                act.wait_ge(shifted, k + 1)
                nc.scalar.activation(root, root, ACT.Sqrt).then_inc(rooted, 1)
            if gains is not None:
                act.wait_ge(loaded, 16 * len(loads))
            for g, (t0, n, k) in enumerate(tiles):
                act.wait_ge(made, g + 1)
                here, ps = to[0][:, k, t0 * P:(t0 + n) * P], c.ps[:, g % 8, 0:n * P]
                if gains is None:
                    nc.scalar.activation(here, ps, ACT.Copy).then_inc(copied, 1)
                else:
                    nc.scalar.activation(here, ps, ACT.Identity, scale=gains[0][:, k:k + 1], bias=gains[1][:, k:k + 1]).then_inc(copied, 1)

        @block.tensor
        def _(pe):
            for g, (t0, n, k) in enumerate(tiles):
                pe.wait_ge(normal, t0 + n)
                if g >= 8:
                    pe.wait_ge(copied if len(to) == 1 else low_done, g - 7)
                for j in range(n):
                    ins = nc.tensor.transpose(c.ps[:, g % 8, j * P:(j + 1) * P], nat[0:P, t0 + j, 128 * k:128 * k + 128],
                                              c.ident[0:P, 0:P])
                ins.then_inc(made, 1)

        @block.vector
        def _(v):
            if not taken:
                for t in range(T):
                    nc.vector.bn_stats(stats[:, t, :], of[0:P, t, :]).then_inc(stats_done, 1)
                for t in range(T):
                    v.wait_ge(stats_done, t + 1)
                    nc.vector.bn_aggr(mv[:, t, :], stats[:, t, :]).then_inc(moments, 1)
                v.wait_ge(moments, T)
            nc.vector.tensor_scalar(root, mv[:, :, 1], EPS, None, ALU.add).then_inc(shifted, 1)
            v.wait_ge(rooted, 1)
            nc.vector.reciprocal(inverse, root).then_inc(inverted, 1)
            v.wait_ge(inverted, 1)
            if twice:
                nc.vector.tensor_tensor(second, inverse, inverse, ALU.mult).then_inc(scaled, 1)
                v.wait_ge(scaled, 1)
                nc.vector.tensor_tensor(second, second, mv[:, :, 1], ALU.mult).then_inc(scaled, 1)
                v.wait_ge(scaled, 2)
                nc.vector.tensor_scalar(root, second, EPS, None, ALU.add).then_inc(shifted, 1)
                v.wait_ge(rooted, 2)
                nc.vector.reciprocal(second, root).then_inc(scaled, 1)
                v.wait_ge(scaled, 3)
                nc.vector.tensor_tensor(inverse, inverse, second, ALU.mult).then_inc(scaled, 1)
                v.wait_ge(scaled, 4)
            for t in range(T):
                nc.vector.tensor_scalar(nat[0:P, t, :], of[0:P, t, :], mv[:, t, 0:1], inverse[:, t:t + 1],
                                        ALU.subtract, ALU.mult).then_inc(normal, 1)
            if len(to) == 2:
                for g, (t0, n, k) in enumerate(tiles):
                    v.wait_ge(copied, g + 1)
                    cols = slice(t0 * P, (t0 + n) * P)
                    nc.vector.tensor_tensor(to[1][:, k, cols], c.ps[:, g % 8, 0:n * P], to[0][:, k, cols].bitcast(F32),
                                            ALU.subtract).then_inc(low_done, 1)


def tiles_on_tensor(c, tiles, loads=(), only_vector=False):
    nc = c.nc
    with ExitStack() as s:
        made, scalar_out, vector_out, scalar_step, vector_step, loaded = map(c.semaphore, (
            "made", "scalar_out", "vector_out", "scalar_step", "vector_step", "loaded"))
        block = s.enter_context(nc.Block())

        @block.sync
        def _(sp):
            for to, of in loads:
                sp.dma_start(to, of).then_inc(loaded, 16)
            if loads:
                sp.wait_ge(loaded, 16 * len(loads))

        @block.tensor
        def _(pe):
            for g, (rows, cols, parts, _) in enumerate(tiles):
                if g >= 8:
                    if only_vector:
                        pe.wait_ge(vector_out, g - 7)
                    else:
                        pe.wait_ge(vector_out if g % 2 else scalar_out, (g - 8) // 2 + 1)
                ps = c.ps[0:rows, g % 8, 0:cols]
                if isinstance(parts, tuple) and parts[0] == "turn":
                    for k, of in enumerate(parts[1]):
                        r, w = of.shape
                        ins = nc.tensor.transpose(ps[0:w, k * r:(k + 1) * r], of, c.ident[0:r, 0:r])
                else:
                    for k, (l, r) in enumerate(parts):
                        ins = nc.tensor.matmul(ps, l, r, start=(k == 0), stop=(k == len(parts) - 1))
                ins.then_inc(made, 1)

        def copies(engine, first, step, out):
            count = [0]

            def link(ins):
                count[0] += 1
                ins.then_inc(step, 1)
                engine.wait_ge(step, count[0])

            for g in range(first, len(tiles), 1 if only_vector else 2):
                engine.wait_ge(made, g + 1)
                rows, cols, _, copy = tiles[g]
                copy(engine, c.ps[0:rows, g % 8, 0:cols], link).then_inc(out, 1)

        if not only_vector:
            @block.scalar
            def _(act):
                copies(act, 0, scalar_step, scalar_out)

        @block.vector
        def _(v):
            copies(v, 0 if only_vector else 1, vector_step, vector_out)


def is_scalar(engine):
    return engine.engine == mybir.EngineType.Activation


def copy_to(to):
    def copy(e, ps, link):
        return e.activation(to, ps, ACT.Copy) if is_scalar(e) else e.tensor_copy(to, ps)
    return copy


def biased_to(to, bias, relu=False):
    def copy(e, ps, link):
        if is_scalar(e):
            return e.activation(to, ps, ACT.Relu if relu else ACT.Identity, bias=bias)
        return e.tensor_scalar(to, ps, bias, 0.0 if relu else None, ALU.add, ALU.max if relu else ALU.bypass)
    return copy


def turned_product(w, of, rows, copy, kc=KC):
    return [(min(128, rows - 128 * m), n, [(w[:, k, 128 * m:min(rows, 128 * m + 128)], of[:, k, c0:c0 + n]) for k in range(kc)],
             copy(m, slice(c0, c0 + n))) for m in range((rows + 127) // 128) for c0, n in COLS]


def natural_product(of, w, copy, kc=KC):
    return [(P, w.shape[2], [(of[:, k, t * P:t * P + P], w[:, k, :]) for k in range(kc)], copy(t)) for t in range(T)]


def weight(c, slot, of):
    return (c.w[:, slot], of.rearrange("(k p) n -> p k n", p=128))


def column(ap, n=KC):
    return ap.rearrange("(k p) -> p k", k=n)


def stage_degrees(c, nat, loads):
    nc = c.nc
    sums = c.big[0:P, 0:N]
    most = c.small[0:1, 500:503]
    with ExitStack() as s:
        v_done, p_done, most_done, loaded, made, copied = map(c.semaphore, ("v_done", "p_done", "most_done", "loaded", "made", "copied"))
        tiles = [(t0, n, k) for t0, n in QUERIES for k in range(KC)]
        block = s.enter_context(nc.Block())
        load_all(block, loads, loaded)

        @block.scalar
        def _(act):
            for g, (t0, n, k) in enumerate(tiles):
                act.wait_ge(made, g + 1)
                nc.scalar.activation(c.xt[:, k, t0 * P:(t0 + n) * P], c.ps[:, 6 + g % 2, 0:n * P], ACT.Copy).then_inc(copied, 1)

        @block.tensor
        def _(pe):
            for g, (t0, n, k) in enumerate(tiles):
                if g >= 2:
                    pe.wait_ge(copied, g - 1)
                for j in range(n):
                    ins = nc.tensor.transpose(c.ps[:, 6 + g % 2, j * P:(j + 1) * P], nat[0:P, t0 + j, 128 * k:128 * k + 128],
                                              c.ident[0:P, 0:P])
                ins.then_inc(made, 1)
            pe.wait_ge(v_done, 1)
            for b, (c0, n) in enumerate(COLS):
                ins = nc.tensor.matmul(c.ps[:, b, 0:n], c.ones[0:P, :], sums[:, c0:c0 + n], start=True, stop=True)
            ins.then_inc(p_done, 1)
            pe.wait_ge(v_done, 2)
            for t in range(T):
                ins = nc.tensor.transpose(c.ps[0:P, 3 + t // 4, 128 * (t % 4):128 * (t % 4) + 128],
                                          c.inv_t[:, t * P:t * P + P], c.ident[:, :])
            ins.then_inc(p_done, 1)

        @block.vector
        def _(v):
            nc.vector.tensor_reduce(sums, c.adj[0:P].bitcast(F32).rearrange("p s d -> p d s"), AX.X, ALU.add).then_inc(v_done, 1)
            v.wait_ge(p_done, 1)
            for b, (c0, n) in enumerate(COLS):
                ins = nc.vector.tensor_scalar(c.inv_t[:, c0:c0 + n], c.ps[:, b, 0:n], 1.0, None, ALU.max)
            ins.then_inc(v_done, 1)
            v.wait_ge(v_done, 2)
            nc.vector.tensor_reduce(most[:, 0:1], c.inv_t[0:1, :], AX.X, ALU.max).then_inc(most_done, 1)
            nc.vector.tensor_copy(c.ident_r[:, 0:P], c.ident[0:P, 0:P])
            v.wait_ge(most_done, 1)
            nc.vector.tensor_scalar(c.many[:, 0:1], most[:, 0:1], EXACT_COUNT, None, ALU.is_gt)
            v.wait_ge(p_done, 2)
            nc.vector.tensor_copy(c.inv_n[0:P, 0:8].rearrange("p (a b) -> p a b", a=2),
                                  c.ps[0:P, 3:5, :].rearrange("p a (b q) -> p a b q", q=128)[:, :, :, 0]).then_inc(v_done, 1)
            nc.vector.tensor_copy(c.inv_n[0:P, 8:10], c.ps[0:P, 5, 0:256].rearrange("p (b q) -> p b q", q=128)[:, :, 0]).then_inc(v_done, 1)
            v.wait_ge(v_done, 4)
            nc.vector.reciprocal(c.inv_n[0:P, :], c.inv_n[0:P, :])


def stage_l0_mix(c, a, loads):
    qt = c.big[:, 0:5000].rearrange("p (k n) -> p k n", k=KC)
    kn = c.nat
    vo = c.big[0:P, 5000:5000 + T * 4 * 132].rearrange("p (t a q) -> p t a q", t=T, a=4)
    wt = c.big[:, 10500:10500 + 2048].rearrange("p (k d) -> p k d", k=KC)
    tmp = c.big[:, 12600:12600 + 512 * 4].rearrange("p (b d) -> p b d", b=4)
    kv = c.big[:, 14700:14700 + 4 * 130].rearrange("p (k d) -> p k d", k=4)

    def turn_w(slot):
        return [(128, 512, ("turn", [c.w[:, slot, m, 128 * k:128 * k + 128] for m in range(KC)]),
                 copy_to(wt[:, k, :])) for k in range(KC)]

    tiles_on_tensor(c, turn_w(0))
    stage_elu(c, [(128, n, [(wt[:, k, 128 * m:128 * m + 128], c.xt[:, k, c0:c0 + n]) for k in range(KC)],
                   qt[:, m, c0:c0 + n]) for m in range(KC) for c0, n in COLS], tmp)
    tiles_on_tensor(c, turn_w(1))
    stage_elu(c, [(P, D, [(c.xt[:, k, t * P:t * P + P], wt[:, k, :]) for k in range(KC)], kn[0:P, t, :])
                  for t in range(T)], tmp)
    tiles_on_tensor(c, turn_w(2))

    def to_v(t):
        def copy(e, ps, link):
            of, to = ps.rearrange("p (a q) -> p a q", a=4), vo[:, t, :, 0:128]
            return e.activation(to, of, ACT.Copy, scale=1.0 / N) if is_scalar(e) else e.tensor_scalar(to, of, 1.0 / N, None, ALU.mult)
        return copy
    tiles_on_tensor(c, natural_product(c.xt, wt, to_v), loads)

    def pair(p):
        def copy(e, ps, link):
            cp = (lambda o, i: e.activation(o, i, ACT.Copy)) if is_scalar(e) else e.tensor_copy
            cp(kv[0:64, p, 0:64], ps[0:64, 0:64])
            cp(kv[64:128, p, 64:128], ps[64:128, 64:128])
            cp(kv[0:64, p, 128:129], ps[0:64, 128:129])
            return cp(kv[64:128, p, 129:130], ps[64:128, 128:129])
        return copy
    memsets(c, [kv[:]])
    memsets(c, [vo[:, :, :, 128:132]], 1.0)
    tiles_on_tensor(c, [(128, 132, [(kn[0:P, t, 128 * p:128 * p + 128], vo[:, t, p, :]) for t in range(T)], pair(p))
                        for p in range(4)])

    stage_linear_quotients(c, qt, kv, tmp)


def memsets(c, aps, value=0.0):
    nc = c.nc
    with nc.Block() as block:
        @block.gpsimd
        def _(pool):
            for ap in aps:
                nc.gpsimd.memset(ap, value)


def stage_linear_quotients(c, qt, kv, tmp):
    nc = c.nc
    banks = [c.ps[0:P, 2 * k:2 * k + 2, 0:260].rearrange("p h (a q) -> p h a q", a=2) for k in range(4)]
    r = [[c.small[0:P, 16 * k + 8 * j:16 * k + 8 * j + 8].rearrange("p (h a b) -> p h a b", h=2, a=2) for j in range(2)] for k in range(2)]
    with ExitStack() as s:
        made, step, quotient, added = map(c.semaphore, ("made", "step", "quotient", "added"))
        block = s.enter_context(nc.Block())

        @block.tensor
        def _(pe):
            for t in range(T):
                if t >= 4:
                    pe.wait_ge(quotient, t - 3)
                for p in range(4):
                    ins = nc.tensor.matmul(banks[t % 4][:, p // 2, p % 2, :], qt[:, p, t * P:t * P + P], kv[:, p, :],
                                           start=True, stop=True)
                ins.then_inc(made, 1)

        @block.vector
        def _(v):
            link = chain(v, step)
            for t in range(T):
                v.wait_ge(made, t + 1)
                ps, (low, inverse) = banks[t % 4], r[t % 2]
                link(nc.vector.tensor_scalar(low, ps[:, :, :, 128:130], 1e-6, 1.0 / N, ALU.add, ALU.mult))
                link(nc.vector.reciprocal(inverse, low))
                if t >= 4:
                    v.wait_ge(added, t - 3)
                for h in range(2):
                    ins = nc.vector.tensor_tensor(tmp[0:P, t % 4, 256 * h:256 * h + 256].rearrange("p (a b d) -> p a b d", a=2, b=2),
                                                  ps[:, h, :, 0:128].rearrange("p a (b d) -> p a b d", b=2),
                                                  inverse[:, h].unsqueeze(3).to_broadcast([P, 2, 2, 64]), ALU.mult)
                ins.then_inc(quotient, 1)

        @block.gpsimd
        def _(pool):
            for t in range(T):
                pool.wait_ge(quotient, t + 1)
                x = c.x[0:P, t, :]
                nc.gpsimd.tensor_tensor(x, x, tmp[0:P, t % 4, :], ALU.add).then_inc(added, 1)


def stage_elu(c, tiles, tmp):
    nc = c.nc
    with ExitStack() as s:
        made, low, exped, out = map(c.semaphore, ("made", "low", "exped", "out"))
        block = s.enter_context(nc.Block())

        @block.tensor
        def _(pe):
            for g, (rows, cols, parts, _) in enumerate(tiles):
                if g >= 8:
                    pe.wait_ge(out, g - 7)
                for k, (l, r) in enumerate(parts):
                    ins = nc.tensor.matmul(c.ps[0:rows, g % 8, 0:cols], l, r, start=(k == 0), stop=(k == len(parts) - 1))
                ins.then_inc(made, 1)

        @block.scalar
        def _(act):
            for g, (rows, cols, _, to) in enumerate(tiles):
                act.wait_ge(low, g + 1)
                t = tmp[0:rows, g % 4, 0:cols]
                nc.scalar.activation(t, t, ACT.Exp).then_inc(exped, 1)

        @block.vector
        def _(v):
            for g in range(len(tiles) + 2):
                if g < len(tiles):
                    rows, cols, _, to = tiles[g]
                    v.wait_ge(made, g + 1)
                    if g >= 4:
                        v.wait_ge(out, g - 3)
                    nc.vector.tensor_scalar(tmp[0:rows, g % 4, 0:cols], c.ps[0:rows, g % 8, 0:cols], 0.0, None,
                                            ALU.min).then_inc(low, 1)
                if g >= 2:
                    rows, cols, _, to = tiles[g - 2]
                    v.wait_ge(exped, g - 1)
                    nc.vector.scalar_tensor_tensor(to, c.ps[0:rows, (g - 2) % 8, 0:cols], 0.0,
                                                   tmp[0:rows, (g - 2) % 4, 0:cols], ALU.max, ALU.add).then_inc(out, 1)


def counted_sum(nc, ps, counts, parts, flip, exact, before=()):
    as_type = (lambda ap: ap.bitcast(F32)) if exact else (lambda ap: ap)
    pairs = list(before) + [(counts[t], part[t]) for t in range(T) for part in parts]
    for k, (count, part) in enumerate(pairs):
        l, r = (part, count) if flip else (count, part)
        ins = nc.tensor.matmul(ps, as_type(l), as_type(r), start=(k == 0), stop=(k == len(pairs) - 1))
    return ins


def by_counts(c, pe, program):
    many = pe.value_load(c.many[0:1, 0:1], min_val=0, max_val=1)
    with pe.If(many > 0):
        program(True)
    with pe.Else():
        program(False)


def stage_aggregate(c, of_t, to_t, u, b, w, loads, first):
    nc = c.nc
    tiles = [(m, c0, n) for m in range(KC) for c0, n in COLS]
    scratch = c.scratch
    with ExitStack() as s:
        made, mult, added, out, loaded, degrees = map(c.semaphore, ("made", "mult", "added", "out", "loaded", "degrees"))
        block = s.enter_context(nc.Block())
        load_all(block, loads, loaded)

        @block.tensor
        def _(pe):
            def program(exact):
                for g, (m, c0, n) in enumerate(tiles):
                    if g >= 4:
                        pe.wait_ge(out, g - 3)
                    counted_sum(nc, c.ps[:, 2 * (g % 4), 0:n], [c.adj[0:P, t, c0:c0 + n] for t in range(T)],
                                [[u[0:P, part, t, 128 * m:128 * m + 128] for t in range(T)] for part in range(2)], True, exact)
                    for k in range(KC):
                        ins = nc.tensor.matmul(c.ps[:, 2 * (g % 4) + 1, 0:n], w[:, k, 128 * m:128 * m + 128],
                                               of_t[:, k, c0:c0 + n], start=(k == 0), stop=(k == KC - 1))
                    ins.then_inc(made, 1)
            by_counts(c, pe, program)

        @block.vector
        def _(v):
            if first:
                nc.vector.reciprocal(c.inv_t, c.inv_t).then_inc(degrees, 1)
                out_n = c.out_n[0:P, :]
                nc.vector.tensor_reduce(out_n, c.adj[0:P].bitcast(F32), AX.X, ALU.add).then_inc(degrees, 1)
                v.wait_ge(degrees, 2)
                nc.vector.tensor_scalar(out_n, out_n, 1.0, None, ALU.add).then_inc(degrees, 1)
            for g, (m, c0, n) in enumerate(tiles):
                v.wait_ge(made, g + 1)
                if g >= 2:
                    v.wait_ge(out, g - 1)
                if first and g == 2:
                    v.wait_ge(degrees, 4)
                    nc.vector.reciprocal(c.out_n[0:P, :], c.out_n[0:P, :])
                t = scratch[:, g % 2, 0:n]
                nc.vector.tensor_tensor(t, c.ps[:, 2 * (g % 4), 0:n], c.inv_t[:, c0:c0 + n], ALU.mult).then_inc(mult, 1)
                v.wait_ge(mult, g + 1)
                nc.vector.tensor_tensor(t, t, c.ps[:, 2 * (g % 4) + 1, 0:n], ALU.add).then_inc(added, 1)

        @block.scalar
        def _(act):
            if first:
                act.wait_ge(degrees, 3)
                nc.scalar.activation(c.out_n[0:P, :], c.out_n[0:P, :], ACT.Sqrt).then_inc(degrees, 1)
            for g, (m, c0, n) in enumerate(tiles):
                act.wait_ge(added, g + 1)
                nc.scalar.activation(to_t[:, m, c0:c0 + n], scratch[:, g % 2, 0:n], ACT.Relu,
                                     bias=b[:, m:m + 1]).then_inc(out, 1)


def stage_aggregate_natural(c, of_t, u, b_all, w):
    nc = c.nc
    with ExitStack() as s:
        made, step, out, taken = map(c.semaphore, ("made", "step", "out", "taken"))
        block = s.enter_context(nc.Block())

        @block.tensor
        def _(pe):
            def program(exact):
                for g in range(T):
                    if g >= 4:
                        pe.wait_ge(out, g - 3)
                    counted_sum(nc, c.ps[0:P, 2 * (g % 4), :], [c.adj[0:P, t, g * P:g * P + P] for t in range(T)],
                                [[u[0:P, part, t, :] for t in range(T)] for part in range(2)], False, exact)
                    for k in range(KC):
                        ins = nc.tensor.matmul(c.ps[0:P, 2 * (g % 4) + 1, :], of_t[:, k, g * P:g * P + P], w[:, k, :],
                                               start=(k == 0), stop=(k == KC - 1))
                    ins.then_inc(made, 1)
            by_counts(c, pe, program)

        @block.vector
        def _(v):
            link = chain(v, taken)
            for g in range(T):
                v.wait_ge(made, g + 1)
                x = c.x[0:P, g, :]
                nc.vector.scalar_tensor_tensor(x, c.ps[0:P, 2 * (g % 4), :], c.inv_n[0:P, g:g + 1], x, ALU.mult,
                                               ALU.add).then_inc(step, 1)
                v.wait_ge(step, 2 * g + 1)
                nc.vector.tensor_tensor(x, x, c.ps[0:P, 2 * (g % 4) + 1, :], ALU.add).then_inc(step, 1)
                v.wait_ge(step, 2 * g + 2)
                nc.vector.tensor_tensor(x, x, b_all, ALU.add).then_inc(out, 1)
                v.wait_ge(out, g + 1)
                take_moments(c, nc.vector, g, link)


def stage_split_product(c, of_t, w, u, scale=None, loads=()):
    nc = c.nc
    with ExitStack() as s:
        made, high, low, scaled, loaded = map(c.semaphore, ("made", "high", "low", "scaled", "loaded"))
        block = s.enter_context(nc.Block())
        load_all(block, loads, loaded)

        @block.tensor
        def _(pe):
            for t in range(T):
                if t >= 8:
                    pe.wait_ge(low, t - 7)
                for k in range(KC):
                    ins = nc.tensor.matmul(c.ps[0:P, t % 8, :], of_t[:, k, t * P:t * P + P], w[:, k, :], start=(k == 0),
                                           stop=(k == KC - 1))
                ins.then_inc(made, 1)

        @block.scalar
        def _(act):
            for t in range(T):
                act.wait_ge(made, t + 1)
                if scale is None:
                    nc.scalar.activation(u[0:P, 0, t, :], c.ps[0:P, t % 8, :], ACT.Copy).then_inc(high, 1)
                else:
                    value = c.scratch[0:P, t % 2, :]
                    if t >= 2:
                        act.wait_ge(low, t - 1)
                    nc.scalar.activation(value, c.ps[0:P, t % 8, :], ACT.Copy, scale=scale[:, t:t + 1]).then_inc(scaled, 1)
                    act.wait_ge(scaled, t + 1)
                    nc.scalar.activation(u[0:P, 0, t, :], value, ACT.Copy).then_inc(high, 1)

        @block.vector
        def _(v):
            for t in range(T):
                v.wait_ge(high, t + 1)
                value = c.ps[0:P, t % 8, :] if scale is None else c.scratch[0:P, t % 2, :]
                nc.vector.tensor_tensor(u[0:P, 1, t, :], value, u[0:P, 0, t, :].bitcast(F32), ALU.subtract).then_inc(low, 1)


def stage_turn_counts(c, rev, staged):
    nc = c.nc
    adj = c.adj[0:P].bitcast(F32)
    tiles = [(i, t0, n) for i in range(T) for t0, n in QUERIES]
    uses = [(len(tiles) + 3 - k) // 4 for k in range(4)]
    with ExitStack() as s:
        made, scalar_out, vector_out, placed0, placed1, placed2, placed3 = map(c.semaphore, (
            "made", "scalar_out", "vector_out", "placed0", "placed1", "placed2", "placed3"))
        placed = (placed0, placed1, placed2, placed3)
        block = s.enter_context(nc.Block())

        @block.tensor
        def _(pe):
            for g, (i, t0, n) in enumerate(tiles):
                if g >= 8:
                    pe.wait_ge(vector_out if g % 2 else scalar_out, (g - 8) // 2 + 1)
                for k in range(n):
                    ins = nc.tensor.transpose(c.ps[0:P, g % 8, k * P:(k + 1) * P], adj[:, t0 + k, P * i:P * i + P],
                                              c.ident[0:P, 0:P])
                ins.then_inc(made, 1)

        @block.scalar
        def _(act):
            for g in range(0, len(tiles), 2):
                n = tiles[g][2] * P
                act.wait_ge(made, g + 1)
                if g >= 4:
                    act.wait_ge(placed[g % 4], 16 * (g // 4))
                nc.scalar.activation(staged[:, g % 4, 0:n], c.ps[0:P, g % 8, 0:n], ACT.Copy).then_inc(scalar_out, 1)

        @block.vector
        def _(v):
            for g in range(1, len(tiles), 2):
                n = tiles[g][2] * P
                v.wait_ge(made, g + 1)
                if g >= 4:
                    v.wait_ge(placed[g % 4], 16 * (g // 4))
                nc.vector.tensor_copy(staged[:, g % 4, 0:n], c.ps[0:P, g % 8, 0:n]).then_inc(vector_out, 1)

        @block.sync
        def _(sp):
            for g, (i, t0, n) in enumerate(tiles):
                sp.wait_ge(vector_out if g % 2 else scalar_out, g // 2 + 1)
                sp.dma_start(rev[:, i, t0 * P:(t0 + n) * P].bitcast(F32), staged[:, g % 4, 0:n * P]).then_inc(placed[g % 4], 16)
            for k in range(4):
                sp.wait_ge(placed[k], 16 * uses[k])


def stage_graph_product(c, rev, u):
    nc = c.nc
    with ExitStack() as s:
        made, step, out = map(c.semaphore, ("made", "step", "out"))
        block = s.enter_context(nc.Block())

        @block.tensor
        def _(pe):
            def program(exact):
                for g in range(T):
                    if g >= 8:
                        pe.wait_ge(out, g - 7)
                    own = [(c.ident_r[:, 0:P], u[0:P, part, g, :]) for part in range(2)]
                    counted_sum(nc, c.ps[0:P, g % 8, :], [rev[:, t, g * P:g * P + P] for t in range(T)],
                                [[u[0:P, part, t, :] for t in range(T)] for part in range(2)], False, exact, own).then_inc(made, 1)
            by_counts(c, pe, program)

        @block.vector
        def _(v):
            for g in range(T):
                v.wait_ge(made, g + 1)
                if g >= 2:
                    v.wait_ge(out, g - 1)
                value = c.scratch[0:P, g % 2, :]
                nc.vector.tensor_scalar(value, c.ps[0:P, g % 8, :], c.out_n[0:P, g:g + 1], 0.0, ALU.mult,
                                        ALU.max).then_inc(step, 1)
                v.wait_ge(step, g + 1)
                x = c.x[0:P, g, :]
                nc.vector.tensor_tensor(x, x, value, ALU.add).then_inc(out, 1)


def chain(engine, sem):
    count = [0]

    def link(ins):
        count[0] += 1
        ins.then_inc(sem, 1)
        engine.wait_ge(sem, count[0])
    return link


KEYS = [(0, 512), (512, 512), (1024, N - 1024)]
QUERIES = [(0, 4), (4, 4), (8, 2)]


def stage_attention_constants(c, m, kg, loads):
    nc = c.nc
    with ExitStack() as s:
        zeroed, loaded = (c.semaphore(n) for n in ("zeroed", "loaded"))
        block = s.enter_context(nc.Block())
        load_all(block, loads, loaded)

        @block.gpsimd
        def _(pool):
            nc.gpsimd.memset(m.blockones, 0.0).then_inc(zeroed, 1)
            nc.gpsimd.memset(m.mask_n, 0.0).then_inc(zeroed, 1)
            nc.gpsimd.memset(m.mask_t, 0.0).then_inc(zeroed, 1)
            pool.wait_ge(zeroed, 3)
            nc.gpsimd.affine_select(out=m.mask_n, in_=m.mask_n, compare_op=ALU.is_ge, fill=-3e38, base=0,
                                    pattern=[[-1, P]], channel_multiplier=1)
            nc.gpsimd.affine_select(out=m.mask_t, in_=m.mask_t, compare_op=ALU.is_ge, fill=-3e38, base=0,
                                    pattern=[[1, P]], channel_multiplier=-1)
            nc.gpsimd.memset(m.peaks, -3e38)
            nc.gpsimd.memset(m.tiny, 1e-12)

        @block.vector
        def _(v):
            nc.vector.tensor_copy(m.identb, c.ident[0:P, 0:P])
            v.wait_ge(zeroed, 3)
            nc.vector.memset(m.blockones[0:64, 0:64], 1.0)
            nc.vector.memset(m.blockones[64:128, 64:128], 1.0)
            nc.vector.tensor_copy(m.one, c.ones[0:P, 0:2])
            nc.vector.tensor_scalar(kg, kg, 8.0, None, ALU.mult)
            for par in range(2):
                nc.vector.tensor_scalar(m.ops[64:65, par, 3, :], c.ones[64:65, 0:1].to_broadcast([1, N]), -1.0, None,
                                        ALU.mult)


class Attention:

    def __init__(self, nc, ctx):
        def sb(name, shape, dt=F32):
            return ctx.enter_context(nc.sbuf_tensor("attention_" + name, shape, dt))

        self.ops = sb("ops", [128, 2, 4, N], F32R)
        self.split = sb("split", [128, 2, 2, N], F32R)
        self.dm = sb("diagonal", [P, N], F32R)
        self.one = sb("one", [P, 2], F32R)[:, :]
        self.w = sb("weights", [128, 2, 2, KC, 128])
        self.root = sb("root", [128, 2, 418])
        self.unit = sb("unit", [128, 418])
        self.probs = sb("probs", [P, 3, 500])
        self.rd = sb("quotients", [128, 500])
        self.consts = sb("constants", [128, 128 + 192 + 1])
        self.blockones = self.consts[:, 0:128]
        half = lambda k: self.consts[0:P, 128 + 64 * k:192 + 64 * k].bitcast(BF16)[:, 0:P]
        self.mask_n, self.mask_t, self.identb = half(0), half(1), half(2)
        self.tiny = self.consts[:, 320:321]

    def loads(self, p, wk, wq):
        return [(self.w[:, p % 2, z], w.rearrange("(k p) n -> p k n", p=128)[:, :, 128 * p:128 * p + 128])
                for z, w in enumerate((wk, wq))]


TURNS = [(q, i0, ni, j) for q, (i0, ni) in enumerate(QUERIES) for j in range(i0 + ni)]
STEPS = len(TURNS)
PIECES = [(i, b) for i in range(T) for b, (c0, _) in enumerate(KEYS) if c0 < P * (i + 1)]
HEADS = 8
PROJECT_AT = (1, 4, 7, 10, 13, 16)
SQUARES_AT = (2, 5, 8, 11, 14, 17)
UNIT_AT = (2, 5, 8, 11, 14, 17)
HIGH_AT = (4, 7, 10, 13, 16, 19)
LOW_AT = (4, 7, 10, 13, 16, 19)
DIAGONAL_AT = 13
ROWS_AT = 17
DIVIDE_AT = (6, 14, 1)


PAIRS = HEADS // 2
PIECES_AT = {2: (0, 1), 3: (2, 3), 4: (4, 5), 5: (6, 7), 6: (8, 9), 7: (10, 11), 8: (12, 13), 9: (14,), 10: (15,), 11: (16,), 12: (17,)}


def stage_attention(c, m, vh, gains, wq, wk, ot):
    nc = c.nc
    with ExitStack() as s:
        (loaded, projected, taken, squared, summed, rooted, inverted, united, high, low, placed0, placed1, scored, maxed,
         peaked, diag, rowed, levelled, turned, exped, weighed, divided, sides, high0, high1) = map(c.semaphore, (
             "loaded", "projected", "taken", "squared", "summed", "rooted", "inverted", "united", "high", "low", "placed0", "placed1",
             "scored", "maxed", "peaked", "diag", "rowed", "levelled", "turned", "exped", "weighed", "divided", "sides", "high0", "high1"))
        placed, high_placed = (placed0, placed1), (high0, high1)
        tiles = [(z, c0, n) for z in range(2) for c0, n in COLS]
        block = s.enter_context(nc.Block())

        def rows(h):
            return slice(64 * (h % 2), 64 * (h % 2) + 64)

        def piece(k):
            i, b = PIECES[k]
            c0, n = KEYS[b]
            return i, c0, min(n, P * (i + 1) - c0)

        def raw_bank(p, j):
            return j if p == 0 else 6

        def sum_bank(p, j):
            return 6 + j % 2 if p == 0 else 7

        @block.sync
        def _(sp):
            def load(p):
                for to, of in m.loads(p, wk, wq):
                    sp.dma_start(to, of).then_inc(loaded, 16)

            def place(h):
                if h >= 2:
                    sp.wait_ge(weighed, STEPS * (h - 1))
                r, o = rows(h), m.ops[:, h % 2]
                for to, z in ((o[0:64, 1], 0), (o[0:64, 2], 1)):
                    sp.wait_ge(high, 6 * (h // 2) + 3 * (z + 1))
                    sp.dma_start(to.bitcast(F32), m.split[r, z, 0, :].bitcast(F32)).then_inc(high_placed[h % 2], 16)
                sp.wait_ge(low, 6 * (h // 2 + 1))
                for to, z, part in ((o[0:64, 0], 1, 0), (o[64:128, 0], 1, 1), (o[64:128, 1], 0, 0), (o[0:64, 3], 0, 1)):
                    sp.dma_start(to.bitcast(F32), m.split[r, z, part, :].bitcast(F32)).then_inc(placed[h % 2], 16)

            load(1)
            for h in range(HEADS):
                place(h)
                if h % 2 == 0 and 2 <= h // 2 + 1 < PAIRS:
                    sp.wait_ge(projected, 6 * (h // 2))
                    load(h // 2 + 1)
            for par in range(2):
                sp.wait_ge(placed[par], 64 * PAIRS)
                sp.wait_ge(high_placed[par], 32 * PAIRS)

        @block.tensor
        def _(pe):
            def project(p, j):
                z, c0, n = tiles[j]
                if p and j == 0:
                    pe.wait_ge(loaded, 32 * p)
                if p:
                    pe.wait_ge(taken, 6 * p + j)
                    pe.wait_ge(squared, 6 * p + j)
                for k in range(KC):
                    ins = nc.tensor.matmul(c.ps[:, raw_bank(p, j), 0:n], m.w[:, p % 2, z, k], c.xt[:, k, c0:c0 + n],
                                           start=(k == 0), stop=(k == KC - 1))
                ins.then_inc(projected, 1)

            def sum_squares(p, j):
                z, c0, n = tiles[j]
                pe.wait_ge(squared, 6 * p + j + 1)
                if p == 0 and j >= 2:
                    pe.wait_ge(rooted, j - 1)
                elif p:
                    pe.wait_ge(rooted, 6 * p + j)
                nc.tensor.matmul(c.ps[:, sum_bank(p, j), 0:n], m.blockones, m.root[:, j % 2, 0:n], start=True,
                                 stop=True).then_inc(summed, 1)

            def score(h, k):
                i, c0, w = piece(k)
                if k == 0:
                    pe.wait_ge(high_placed[h % 2], 32 * (h // 2 + 1))
                if k >= 2:
                    pe.wait_ge(maxed, 18 * h + k - 1)
                elif h:
                    pe.wait_ge(levelled, 3 * h - 1 + k)
                else:
                    pe.wait_ge(taken, 6)
                    pe.wait_ge(squared, 6)
                d0, d1 = max(P * i, c0), min(P * (i + 1), c0 + w)
                bank = 4 + (h + k) % 2
                even = w + w % 2
                ins = nc.tensor.matmul(c.ps[0:P, bank, 0:even], m.ops[0:64, h % 2, 2, P * i:P * i + P],
                                       m.ops[0:64, h % 2, 1, c0:c0 + even], start=True, stop=(d1 <= d0))
                if d1 > d0:
                    ins = nc.tensor.matmul(c.ps[0:P, bank, d0 - c0:d1 - c0], m.identb, m.mask_n[:, d0 - P * i:d1 - P * i],
                                           start=False, stop=True)
                ins.then_inc(scored, 1)

            def peaks_row(h, b):
                c0, n = COLS[b]
                if b == 0:
                    pe.wait_ge(diag, h + 1)
                if b == 2:
                    pe.wait_ge(levelled, 3 * h + 1)
                nc.tensor.matmul(c.ps[0:1, 4 + (h + b) % 2, 0:n], m.one[:, 0:1], m.dm[:, c0:c0 + n], start=True,
                                 stop=True).then_inc(rowed, 1)

            def turned_scores(at):
                h, g = at // STEPS, at % STEPS
                q, i0, ni, j = TURNS[g]
                s0 = max(i0, j) * P
                w = (i0 + ni) * P - s0
                odd = w % 2
                if g == 0:
                    pe.wait_ge(placed[h % 2], 64 * (h // 2 + 1))
                    pe.wait_ge(levelled, 3 * h + 3)
                if at >= 2:
                    pe.wait_ge(exped, at - 1)
                o = m.ops[:, h % 2]
                out = c.ps[0:P, at % 2, 0:w + odd]
                nc.tensor.matmul(out, o[:, 1, j * P:j * P + P], o[:, 0, s0 - odd:s0 + w], start=True, stop=False)
                ins = nc.tensor.matmul(out, o[0:65, 3, j * P:j * P + P], o[0:65, 2, s0 - odd:s0 + w], start=False, stop=(j < i0))
                if j >= i0:
                    ins = nc.tensor.matmul(c.ps[0:P, at % 2, odd:odd + P], m.identb, m.mask_t, start=False, stop=True)
                ins.then_inc(turned, 1)

            def weigh(at):
                h, g = at // STEPS, at % STEPS
                q, i0, ni, j = TURNS[g]
                s0 = max(i0, j) * P
                w = (i0 + ni) * P - s0
                pe.wait_ge(exped, at + 1)
                if j == 0 and 3 * h + q >= 2:
                    pe.wait_ge(divided, 3 * h + q - 1)
                nc.tensor.matmul(c.ps[:, 2 + (3 * h + q) % 2, s0 - i0 * P:s0 - i0 * P + w],
                                 vh[0:P, j, 192 * (h // 2) + 64 * (h % 2):192 * (h // 2) + 64 * (h % 2) + 128],
                                 m.probs[:, at % 3, 0:w], start=(j == 0), stop=(j == i0 + ni - 1)).then_inc(weighed, 1)

            for j in range(6):
                project(0, j)
                if j >= 1:
                    sum_squares(0, j - 1)
            sum_squares(0, 5)
            for k in range(len(PIECES)):
                score(0, k)
            for b in range(3):
                peaks_row(0, b)
            turned_scores(0)
            for h in range(HEADS):
                for g in range(STEPS):
                    if STEPS * h + g + 1 < STEPS * HEADS:
                        turned_scores(STEPS * h + g + 1)
                    if h + 1 < HEADS and g == ROWS_AT:
                        for b in range(3):
                            peaks_row(h + 1, b)
                    if h % 2 == 0 and h // 2 + 1 < PAIRS:
                        if g in SQUARES_AT:
                            sum_squares(h // 2 + 1, SQUARES_AT.index(g))
                        if g in PROJECT_AT:
                            project(h // 2 + 1, PROJECT_AT.index(g))
                    if h + 1 < HEADS:
                        for k in PIECES_AT.get(g, ()):
                            score(h + 1, k)
                    weigh(STEPS * h + g)

        @block.scalar
        def _(act):
            def square(p, j):
                z, c0, n = tiles[j]
                act.wait_ge(projected, 6 * p + j + 1)
                if 6 * p + j >= 2:
                    act.wait_ge(united, 6 * p + j - 1)
                nc.scalar.activation(m.root[:, j % 2, 0:n], c.ps[:, raw_bank(p, j), 0:n], ACT.Square).then_inc(squared, 1)
                if 6 * p + j >= 2:
                    act.wait_ge(low, 6 * p + j - 1)
                nc.scalar.activation(m.unit[j % 2][:, 0:n], c.ps[:, raw_bank(p, j), 0:n], ACT.Copy).then_inc(taken, 1)

            def take_root(p, j):
                z, c0, n = tiles[j]
                act.wait_ge(summed, 6 * p + j + 1)
                nc.scalar.activation(m.root[:, j % 2, 0:n], c.ps[:, sum_bank(p, j), 0:n], ACT.Sqrt,
                                     bias=m.tiny).then_inc(rooted, 1)

            def take_high(p, j):
                z, c0, n = tiles[j]
                act.wait_ge(united, 6 * p + j + 1)
                if p and j == 0:
                    for par in range(2):
                        act.wait_ge(placed[par], 64 * p)
                        act.wait_ge(high_placed[par], 32 * p)
                nc.scalar.activation(m.split[:, z, 0, c0:c0 + n], m.unit[j % 2][:, 0:n], ACT.Copy).then_inc(high, 1)

            def level(h, b):
                c0, n = COLS[b]
                act.wait_ge(rowed, 3 * h + b + 1)
                if h >= 2 and b == 0:
                    act.wait_ge(weighed, STEPS * (h - 1))
                nc.scalar.activation(m.ops[64:65, h % 2, 2, c0:c0 + n], c.ps[0:1, 4 + (h + b) % 2, 0:n],
                                     ACT.Copy).then_inc(levelled, 1)

            def exp(at):
                q, i0, ni, j = TURNS[at % STEPS]
                w = (i0 + ni) * P - max(i0, j) * P
                act.wait_ge(turned, at + 1)
                if at >= 3:
                    act.wait_ge(weighed, at - 2)
                nc.scalar.activation(m.probs[:, at % 3, 0:w], c.ps[0:P, at % 2, w % 2:w % 2 + w], ACT.Exp).then_inc(exped, 1)

            for j in range(6):
                square(0, j)
                if j >= 1:
                    take_root(0, j - 1)
                if j >= 1:
                    take_high(0, j - 1)
            take_root(0, 5)
            take_high(0, 5)
            for b in range(3):
                level(0, b)
            exp(0)
            for h in range(HEADS):
                for g in range(STEPS):
                    if STEPS * h + g + 1 < STEPS * HEADS:
                        exp(STEPS * h + g + 1)
                    if h + 1 < HEADS and g == ROWS_AT:
                        for b in range(3):
                            level(h + 1, b)
                    if h % 2 == 0 and h // 2 + 1 < PAIRS:
                        if g in HIGH_AT:
                            take_high(h // 2 + 1, HIGH_AT.index(g))
                        if g in SQUARES_AT:
                            take_root(h // 2 + 1, SQUARES_AT.index(g))
                        if g in PROJECT_AT:
                            square(h // 2 + 1, PROJECT_AT.index(g))

        @block.vector
        def _(v):
            def make_unit(p, j):
                z, c0, n = tiles[j]
                v.wait_ge(rooted, 6 * p + j + 1)
                v.wait_ge(taken, 6 * p + j + 1)
                root = m.root[:, j % 2, 0:n]
                nc.vector.reciprocal(root, root).then_inc(inverted, 1)
                v.wait_ge(inverted, 6 * p + j + 1)
                unit = m.unit[j % 2][:, 0:n]
                nc.vector.scalar_tensor_tensor(unit, unit, gains[z], root, ALU.mult,
                                               ALU.mult).then_inc(united, 1)

            def take_low(p, j):
                z, c0, n = tiles[j]
                v.wait_ge(high, 6 * p + j + 1)
                if p and j == 0:
                    for par in range(2):
                        v.wait_ge(placed[par], 64 * p)
                        v.wait_ge(high_placed[par], 32 * p)
                nc.vector.tensor_tensor(m.split[:, z, 1, c0:c0 + n], m.unit[j % 2][:, 0:n], m.split[:, z, 0, c0:c0 + n].bitcast(F32),
                                        ALU.subtract).then_inc(low, 1)

            def reduce(h, k):
                i, c0, w = piece(k)
                v.wait_ge(scored, 18 * h + k + 1)
                nc.vector.tensor_reduce(m.peaks[:, i, PIECES[k][1]:PIECES[k][1] + 1], c.ps[0:P, 4 + (h + k) % 2, 0:w], AX.X,
                                        ALU.max).then_inc(maxed, 1)

            def diagonal(h):
                v.wait_ge(maxed, 18 * h + 18)
                nc.vector.tensor_reduce(m.peak, m.peaks, AX.X, ALU.max).then_inc(peaked, 1)
                v.wait_ge(peaked, h + 1)
                if h:
                    v.wait_ge(rowed, 3 * h)
                nc.vector.tensor_tensor(m.dm[:].rearrange("p (i q) -> p i q", q=P),
                                        c.ident[0:P, 0:P].unsqueeze(1).to_broadcast([P, T, P]),
                                        m.peak.unsqueeze(2).to_broadcast([P, T, P]), ALU.mult).then_inc(diag, 1)

            def divide(h, q):
                i0, ni = QUERIES[q]
                last = sum(a + b for a, b in QUERIES[0:q + 1])
                v.wait_ge(weighed, STEPS * h + last)
                if 3 * h + q:
                    v.wait_ge(divided, 3 * h + q)
                mine, ones = rows(h), rows(h + 1)
                ps = c.ps[:, 2 + (3 * h + q) % 2, 0:ni * P]
                nc.vector.reciprocal(m.rd[mine, 0:ni * P], ps[ones]).then_inc(sides, 1)
                v.wait_ge(sides, 3 * h + q + 1)
                nc.vector.tensor_tensor(ot[mine, h // 2, i0 * P:(i0 + ni) * P], ps[mine], m.rd[mine, 0:ni * P],
                                        ALU.mult).then_inc(divided, 1)

            for j in range(6):
                make_unit(0, j)
                take_low(0, j)
            for k in range(len(PIECES)):
                reduce(0, k)
            diagonal(0)
            for h in range(HEADS):
                for g in range(STEPS):
                    if h + 1 < HEADS:
                        for k in PIECES_AT.get(g, ()):
                            reduce(h + 1, k)
                        if g == DIAGONAL_AT:
                            diagonal(h + 1)
                    if h % 2 == 0 and h // 2 + 1 < PAIRS:
                        if g in LOW_AT:
                            take_low(h // 2 + 1, LOW_AT.index(g))
                        if g in UNIT_AT:
                            make_unit(h // 2 + 1, UNIT_AT.index(g))
                    for q in range(2):
                        if g == DIVIDE_AT[q]:
                            divide(h, q)
                    if g == DIVIDE_AT[2] and h:
                        divide(h - 1, 2)
            divide(HEADS - 1, 2)


def stage_gate(c, logits, coef):
    nc = c.nc
    s8 = [P, T, 8]
    red = c.small[0:P, 200:230].rearrange("p (a t) -> p a t", a=3)
    with ExitStack() as s:
        step, exped = (c.semaphore(n) for n in ("step", "exped"))
        block = s.enter_context(nc.Block())

        @block.vector
        def _(v):
            link = chain(v, step)
            link(nc.vector.tensor_reduce(red[:, 0, :], logits, AX.X, ALU.max))
            link(nc.vector.tensor_tensor(coef, logits, red[:, 0, :].unsqueeze(2).to_broadcast(s8), ALU.subtract))
            v.wait_ge(exped, 1)
            link(nc.vector.tensor_reduce(red[:, 1, :], coef, AX.X, ALU.add))
            link(nc.vector.reciprocal(red[:, 2, :], red[:, 1, :]))
            link(nc.vector.tensor_tensor(coef, coef, red[:, 2, :].unsqueeze(2).to_broadcast(s8), ALU.mult))

        @block.scalar
        def _(act):
            act.wait_ge(step, 2)
            nc.scalar.activation(coef, coef, ACT.Exp).then_inc(exped, 1)


CAPACITY = 512


def stage_route(c, logits, coef, work):
    nc = c.nc
    s8 = [P, T, 8]
    f = work[0:P, 0:20 * 80].rearrange("p (a t e) -> p a t e", a=20, t=T)
    expert, left, same, key, one, two, both, slots, keep, spare = (f[:, k] for k in range(10))
    r = f[:, 10].rearrange("p t e -> p (t e)").rearrange("p (a t) -> p a t", t=T)
    m1, i1, m2, i2, d, e, w1, w2 = (r[:, k] for k in range(8))
    upper = work[0:P, 1700:1825]
    wide = lambda x: x.unsqueeze(2).to_broadcast(s8)
    with ExitStack() as s:
        consts, step, counted, exped = map(c.semaphore, ("consts", "step", "counted", "exped"))
        block = s.enter_context(nc.Block())

        @block.gpsimd
        def _(pool):
            nc.gpsimd.iota(expert, [[0, T], [1, 8]], base=0, channel_multiplier=0,
                           allow_small_or_imprecise_dtypes=True).then_inc(consts, 1)
            nc.gpsimd.memset(upper, 1.0).then_inc(consts, 1)
            pool.wait_ge(consts, 2)
            nc.gpsimd.affine_select(out=upper, in_=upper, compare_op=ALU.is_gt, fill=0.0, base=0,
                                    pattern=[[1, P]], channel_multiplier=-1).then_inc(consts, 1)

        @block.vector
        def _(v):
            link = chain(v, step)
            v.wait_ge(consts, 3)

            def first(of, m, i, hot):
                link(nc.vector.tensor_reduce(m, of, AX.X, ALU.max))
                link(nc.vector.tensor_tensor(same, of, wide(m), ALU.is_equal))
                link(nc.vector.scalar_tensor_tensor(key, same, -100.0, expert, ALU.mult, ALU.add))
                link(nc.vector.tensor_reduce(i, key, AX.X, ALU.min))
                link(nc.vector.tensor_tensor(hot, key, wide(i), ALU.is_equal))

            first(logits, m1, i1, one)
            link(nc.vector.tensor_scalar(spare, one, -1.0, 1.0, ALU.mult, ALU.add))
            link(nc.vector.tensor_tensor(left, logits, spare, ALU.mult))
            link(nc.vector.scalar_tensor_tensor(left, one, -3e38, left, ALU.mult, ALU.add))
            first(left, m2, i2, two)
            link(nc.vector.tensor_tensor(both, one, two, ALU.add))
            link(nc.vector.tensor_tensor(d, m2, m1, ALU.subtract))
            v.wait_ge(exped, 1)
            link(nc.vector.tensor_scalar(w1, e, 1.0, None, ALU.add))
            link(nc.vector.reciprocal(w1, w1))
            link(nc.vector.tensor_tensor(w2, e, w1, ALU.mult))
            v.wait_ge(counted, 1)
            link(nc.vector.memset(spare[:, 0, :], 0.0))
            for t in range(1, T):
                link(nc.vector.tensor_tensor(spare[:, t, :], spare[:, t - 1, :], c.ps[0:P, 1, 8 * t - 8:8 * t], ALU.add))
            link(nc.vector.tensor_tensor(slots, spare, c.ps[0:P, 0, 0:80].rearrange("p (t e) -> p t e", e=8), ALU.add))
            link(nc.vector.tensor_scalar(keep, slots, float(CAPACITY), None, ALU.is_lt))
            link(nc.vector.tensor_tensor(one, one, wide(w1), ALU.mult))
            link(nc.vector.tensor_tensor(two, two, wide(w2), ALU.mult))
            link(nc.vector.tensor_tensor(one, one, two, ALU.add))
            link(nc.vector.tensor_tensor(coef, one, keep, ALU.mult))

        @block.scalar
        def _(act):
            act.wait_ge(step, 5 + 3 + 5 + 2)
            nc.scalar.activation(e, d, ACT.Exp).then_inc(exped, 1)

        @block.tensor
        def _(pe):
            pe.wait_ge(step, 5 + 3 + 5 + 1)
            flat = both.rearrange("p t e -> p (t e)")
            nc.tensor.matmul(c.ps[0:P, 0, 0:80], upper, flat, start=True, stop=True)
            nc.tensor.matmul(c.ps[0:P, 1, 0:80], c.ones[0:P, 0:P], flat, start=True, stop=True).then_inc(counted, 1)


class Experts:

    def __init__(self, nc, ctx, name):
        self.nc, self.ctx, self.name = nc, ctx, name
        self.raw = self.sb("raw", [128, 2, 2 * KC * 256])
        self.coef = self.sb("coef", [P, T, 8])[:, :, :]
        self.b1 = self.sb("b1", [128, 20])[:, :]

    def sb(self, part, shape, dt=F32):
        return self.ctx.enter_context(self.nc.sbuf_tensor(f"{self.name}_{part}", shape, dt))

    def place(self):
        self.split = self.sb("split", [128, 2, 2, 2 * KC * 256], F32R)
        self.hid = self.sb("hid", [128, 2, 2, N], F32R)
        self.gelu = self.sb("gelu", [128, 2, 418])

    def loads(self, e, par, w1, w2):
        raw = self.raw[:, par]
        return [(raw[:, 0:KC * 256].rearrange("p (k f) -> p k f", k=KC), w1[bass.ds(e, 1)].rearrange("a (k p) f -> p (a k) f", p=128)),
                (raw[:, KC * 256:].rearrange("p (k f) -> p k f", k=2), w2[bass.ds(e, 1)].rearrange("a (k p) f -> p (a k) f", p=128))]


def split_product(nc, ps, left, right):
    pairs = [(l[i], r[j]) for l, r in zip(left, right) for i, j in ((0, 0), (0, 1), (1, 0))]
    for k, (l, r) in enumerate(pairs):
        ins = nc.tensor.matmul(ps, l, r, start=(k == 0), stop=(k == len(pairs) - 1))
    return ins


def stage_experts(c, y, m, w1_d, w2_d):
    nc = c.nc
    w1 = [[m.split[:, par, part, 0:KC * 256].rearrange("p (k f) -> p k f", k=KC) for part in range(2)] for par in range(2)]
    w2 = [[m.split[:, par, part, KC * 256:].rearrange("p (k f) -> p k f", k=2) for part in range(2)] for par in range(2)]
    halves = slice(0, KC * 256), slice(KC * 256, 2 * KC * 256)
    tiles = [(f, c0, n) for c0, n in COLS for f in range(2)]
    with ExitStack() as s:
        names = ("loaded0", "loaded1", "split_high", "split_low", "hid_made", "gelued", "hid_high", "hid_low", "eo_made",
                 "eo_out", "biased")
        (loaded0, loaded1, split_high, split_low, hid_made, gelued, hid_high, hid_low, eo_made, eo_out,
         biased) = map(c.semaphore, names)
        loaded = (loaded0, loaded1)
        block = s.enter_context(nc.Block())

        @block.sync
        def _(sp):
            with sp.Fori(1, 4) as i:
                for par in range(2):
                    sp.wait_ge(split_low, i * 4 + 2 * (par - 1))
                    for to, of in m.loads(i * 2 + par, par, w1_d, w2_d):
                        sp.dma_start(to, of).then_inc(loaded[par], 16)

        @block.gpsimd
        def _(pool):
            with pool.Fori(0, 4) as i:
                for par in range(2):
                    for k, half in enumerate(halves):
                        pool.wait_ge(split_high, i * 4 + (2 * par + k + 1))
                        nc.gpsimd.tensor_tensor(m.split[:, par, 1, half], m.raw[:, par, half], m.split[:, par, 0, half].bitcast(F32),
                                                ALU.subtract).then_inc(split_low, 1)

        @block.tensor
        def _(pe):
            with pe.Fori(0, 4) as i:
                for par in range(2):
                    e = i * 2 + par
                    pe.wait_ge(split_low, i * 4 + (2 * par + 1))
                    for q, (f, c0, n) in enumerate(tiles):
                        pe.wait_ge(gelued, e * 6 + (q + 1))
                        split_product(nc, c.ps[:, q % 3, 0:n], [[w[:, k, 128 * f:128 * f + 128] for w in w1[par]] for k in range(KC)],
                                      [[part[:, k, c0:c0 + n] for part in y] for k in range(KC)]).then_inc(hid_made, 1)
                    pe.wait_ge(split_low, i * 4 + (2 * par + 2))
                    for t in range(T):
                        if t in (0, 3, 6):
                            pe.wait_ge(hid_low, e * 6 + (4, 6, 8)[t // 3])
                        pe.wait_ge(eo_out, e * T + (t + 1))
                        split_product(nc, c.ps[0:P, 3 + t % 5, :],
                                      [[m.hid[:, part, f, t * P:t * P + P] for part in range(2)] for f in range(2)],
                                      [[w[:, f, :] for w in w2[par]] for f in range(2)]).then_inc(eo_made, 1)

        @block.scalar
        def _(act):
            act.sem_inc(gelued, 3)
            for par in range(2):
                act.sem_inc(loaded[par], 32)
            act.sem_inc(eo_made, 2 * T)
            with act.Fori(0, 4) as i:
                for par in range(2):
                    e = i * 2 + par
                    act.wait_ge(loaded[par], i * 32 + 32)
                    act.wait_ge(eo_made, e * T + T)
                    for half in halves:
                        nc.scalar.activation(m.split[:, par, 0, half], m.raw[:, par, half], ACT.Copy).then_inc(split_high, 1)
                    bias = m.b1[:, 16 + 2 * par:18 + 2 * par]
                    nc.scalar.activation(bias, m.b1[:, bass.ds(e * 2, 2)], ACT.Copy).then_inc(biased, 1)
                    act.wait_ge(biased, e + 1)
                    for q, (f, c0, n) in enumerate(tiles):
                        act.wait_ge(hid_made, e * 6 + (q + 1))
                        act.wait_ge(hid_low, e * 6 + (q + 1))
                        nc.scalar.activation(m.gelu[:, q % 2, 0:n], c.ps[:, q % 3, 0:n], ACT.Gelu_apprx_tanh,
                                             bias=bias[:, f:f + 1]).then_inc(gelued, 1)
                        act.wait_ge(gelued, e * 6 + (q + 4))
                        nc.scalar.activation(m.hid[:, 0, f, c0:c0 + n], m.gelu[:, q % 2, 0:n], ACT.Copy).then_inc(hid_high, 1)

        @block.vector
        def _(v):
            v.sem_inc(eo_out, 5)
            v.sem_inc(hid_low, 2)
            with v.Fori(0, 4) as i:
                for par in range(2):
                    e = i * 2 + par
                    for q, (f, c0, n) in enumerate(tiles):
                        v.wait_ge(hid_high, e * 6 + (q + 1))
                        nc.vector.tensor_tensor(m.hid[:, 1, f, c0:c0 + n], m.gelu[:, q % 2, 0:n],
                                                m.hid[:, 0, f, c0:c0 + n].bitcast(F32), ALU.subtract).then_inc(hid_low, 1)
                    for t in range(T):
                        v.wait_ge(eo_made, e * T + (2 * T + t + 1))
                        x = c.x[0:P, t, :]
                        nc.vector.scalar_tensor_tensor(x, c.ps[0:P, 3 + t % 5, :], m.coef[:, t, bass.ds(e, 1)], x,
                                                       ALU.mult, ALU.add).then_inc(eo_out, 1)


def add_to_x(c, t, extra=None):
    def copy(v, ps, link):
        x = c.x[0:P, t, :]
        if extra is not None:
            link(v.tensor_tensor(x, x, extra, ALU.add))
            link(v.tensor_tensor(x, x, ps, ALU.add))
            return take_moments(c, v, t, link)
        return v.tensor_tensor(x, x, ps, ALU.add)
    return copy


def split_tiles_on_tensor(c, tiles, loads=()):
    nc = c.nc
    with ExitStack() as s:
        made, high_done, low_done, loaded = map(c.semaphore, ("made", "high_done", "low_done", "loaded"))
        block = s.enter_context(nc.Block())
        load_all(block, loads, loaded)

        @block.tensor
        def _(pe):
            for g, (rows, cols, make, _, _) in enumerate(tiles):
                if g >= 8:
                    pe.wait_ge(low_done, g - 7)
                make(c.ps[0:rows, g % 8, 0:cols]).then_inc(made, 1)

        @block.scalar
        def _(act):
            for g, (rows, cols, _, high, _) in enumerate(tiles):
                act.wait_ge(made, g + 1)
                nc.scalar.activation(high, c.ps[0:rows, g % 8, 0:cols], ACT.Copy).then_inc(high_done, 1)

        @block.vector
        def _(v):
            for g, (rows, cols, _, high, low) in enumerate(tiles):
                v.wait_ge(high_done, g + 1)
                nc.vector.tensor_tensor(low, c.ps[0:rows, g % 8, 0:cols], high.bitcast(F32), ALU.subtract).then_inc(low_done, 1)


def product_split(c, w, of, y):
    def make(m, c0, n):
        def on(ps):
            for k in range(KC):
                ins = c.nc.tensor.matmul(ps, w[:, k, 128 * m:128 * m + 128], of[:, k, c0:c0 + n], start=(k == 0), stop=(k == KC - 1))
            return ins
        return on
    return [(128, n, make(m, c0, n)) + tuple(part[:, m, c0:c0 + n] for part in y) for m in range(KC) for c0, n in COLS]


def mixture(c, name, make_y, gate_w, gate_b, b1, w1, b2, w2, route, after=()):
    nc = c.nc
    with ExitStack() as ctx:
        m = Experts(nc, ctx, name)
        split_y = m.sb("y", [128, 2, KC, N], F32R)
        y = [split_y[:, part] for part in range(2)]
        with ExitStack() as gate:
            def sb(part, shape, dt=F32):
                return gate.enter_context(nc.sbuf_tensor(f"{name}_{part}", shape, dt))

            lt, coef_t, logits = sb("lt", [8, N])[:, :], sb("coef_t", [8, N])[:, :], sb("logits", [P, T, 8])[:, :, :]
            gw, gb, b2_sb = sb("gw", [128, KC, 8]), sb("gb", [8, 1])[:, :], sb("b2", [8, D])[:, :]
            gw_split = sb("gw_split", [128, 2, KC, 8], F32R)
            work = sb("work", [128, 1900])
            c.recycle()
            small = [(gw[:], gate_w.rearrange("(k p) e -> p k e", p=128)), (m.b1[:, 0:16], b1.rearrange("e (f p) -> p (e f)", p=128)),
                     (b2_sb, b2)]
            if gate_b is not None:
                small.append((gb, gate_b.rearrange("(e o) -> e o", o=1)))
            with ExitStack() as within:
                make_y(within, y, small + m.loads(0, 0, w1, w2) + m.loads(1, 1, w1, w2))
            stage_split(c, gw[:], gw_split)
            tiles_on_tensor(c, [(8, n, [(gw_split[:, i, k, :], y[j][:, k, c0:c0 + n]) for k in range(KC) for i, j in ((0, 0), (0, 1), (1, 0))],
                                 copy_to(lt[:, c0:c0 + n]) if gate_b is None else biased_to(lt[:, c0:c0 + n], gb)) for c0, n in COLS], after)
            tiles_on_tensor(c, [(P, 80, ("turn", [lt[:, t * P:t * P + P] for t in range(T)]),
                                 copy_to(logits.rearrange("p t e -> p (t e)")))])
            if route:
                stage_route(c, logits, m.coef, work)
            else:
                stage_gate(c, logits, m.coef)
            tiles_on_tensor(c, [(8, n * P, ("turn", [m.coef[:, t, :] for t in range(t0, t0 + n)]),
                                 copy_to(coef_t[:, t0 * P:(t0 + n) * P])) for t0, n in QUERIES])
            tiles_on_tensor(c, [(P, D, [(coef_t[:, t * P:t * P + P], b2_sb)], add_to_x(c, t)) for t in range(T)], only_vector=True)
        m.place()
        stage_experts(c, y, m, w1, w2)


def stage_split(c, of, to):
    nc = c.nc
    with ExitStack() as s:
        high = c.semaphore("high")
        block = s.enter_context(nc.Block())

        @block.vector
        def _(v):
            nc.vector.tensor_copy(to[:, 0], of).then_inc(high, 1)
            v.wait_ge(high, 1)
            nc.vector.tensor_tensor(to[:, 1], of, to[:, 0].bitcast(F32), ALU.subtract)


def stage_queries_and_values(c, xm, wqv, qn, vn, ke):
    nc = c.nc
    r = c.small[:, 0:8]
    tiles = [(t, m) for t in range(T) for m in range(KC)]
    with ExitStack() as s:
        made, scalar_out, vector_out, step, exped = map(c.semaphore, ("made", "scalar_out", "vector_out", "step", "exped"))
        block = s.enter_context(nc.Block())

        @block.tensor
        def _(pe):
            for g, (t, m) in enumerate(tiles):
                if g >= 8:
                    pe.wait_ge(vector_out if g % 2 else scalar_out, (g - 8) // 2 + 1)
                nc.tensor.matmul(c.ps[0:P, g % 8, 0:192], xm[:, m, t * P:t * P + P], wqv, start=True, stop=True).then_inc(made, 1)

        @block.scalar
        def _(act):
            for g, (t, m) in enumerate(tiles):
                if g % 2:
                    continue
                if g == 8:
                    act.wait_ge(step, 2)
                    for j in range(2):
                        nc.scalar.activation(ke[:, j, :], ke[:, j, :], ACT.Exp, bias=r[:, 2 + j:3 + j],
                                             accum_out=r[:, 4 + j:5 + j]).then_inc(exped, 1)
                act.wait_ge(made, g + 1)
                nc.scalar.activation(qn[:, t, 64 * m:64 * m + 64], c.ps[0:P, g % 8, 0:64], ACT.Copy)
                nc.scalar.activation(vn[0:P, t, 128 * m:128 * m + 128], c.ps[0:P, g % 8, 64:192], ACT.Copy).then_inc(scalar_out, 1)

        @block.vector
        def _(v):
            link = chain(v, step)
            link(nc.vector.tensor_reduce(r[:, 0:2], ke, AX.X, ALU.max))
            link(nc.vector.tensor_scalar(r[:, 2:4], r[:, 0:2], -1.0, None, ALU.mult))
            for g, (t, m) in enumerate(tiles):
                if g % 2 == 0:
                    continue
                if g == 25:
                    v.wait_ge(exped, 2)
                    link(nc.vector.reciprocal(r[:, 6:8], r[:, 4:6]))
                    for j in range(2):
                        nc.vector.tensor_scalar(ke[:, j, :], ke[:, j, :], r[:, 6 + j:7 + j], None, ALU.mult)
                v.wait_ge(made, g + 1)
                nc.vector.tensor_copy(qn[:, t, 64 * m:64 * m + 64], c.ps[0:P, g % 8, 0:64])
                nc.vector.tensor_copy(vn[0:P, t, 128 * m:128 * m + 128], c.ps[0:P, g % 8, 64:192]).then_inc(vector_out, 1)


def stage_keys_and_queries(c, q, ke, kn, vn, kvb):
    nc = c.nc
    g = q.rearrange("p t (h s) -> p (t h) s", s=32)
    r = c.small[0:P, 0:240].rearrange("p (a k) -> p a k", a=3)
    wide = lambda x: x.unsqueeze(2).to_broadcast([P, 80, 32])
    with ExitStack() as s:
        step, exped, turned, copied, made = map(c.semaphore, ("step", "exped", "turned", "copied", "made"))
        block = s.enter_context(nc.Block())

        @block.tensor
        def _(pe):
            for t in range(T):
                if t >= 6:
                    pe.wait_ge(copied, t - 5)
                for j in range(2):
                    ins = nc.tensor.transpose(c.ps[0:P, t % 6, 128 * j:128 * j + 128], ke[:, j, t * P:t * P + P], c.ident[:, :])
                ins.then_inc(turned, 1)
            for j in range(2):
                for t in range(T):
                    if j == 0:
                        pe.wait_ge(copied, t + 1)
                    ins = nc.tensor.matmul(c.ps[:, 6 + j, 0:256], kn[:, t, 128 * j:128 * j + 128],
                                           vn[0:P, t, 256 * j:256 * j + 256], start=(t == 0), stop=(t == T - 1))
                ins.then_inc(made, 1)

        @block.scalar
        def _(act):
            for t in range(T):
                act.wait_ge(turned, t + 1)
                nc.scalar.activation(kn[:, t, :], c.ps[0:P, t % 6, 0:256], ACT.Copy).then_inc(copied, 1)
            act.wait_ge(step, 2)
            nc.scalar.activation(q, q, ACT.Exp).then_inc(exped, 1)
            for j in range(2):
                act.wait_ge(made, j + 1)
                for h in range(4):
                    nc.scalar.activation(kvb[32 * h:32 * h + 32, j, 64 * h:64 * h + 64],
                                         c.ps[32 * h:32 * h + 32, 6 + j, 64 * h:64 * h + 64], ACT.Copy)

        @block.vector
        def _(v):
            link = chain(v, step)
            link(nc.vector.tensor_reduce(r[:, 0, :], g, AX.X, ALU.max))
            link(nc.vector.tensor_tensor(g, g, wide(r[:, 0, :]), ALU.subtract))
            v.wait_ge(exped, 1)
            link(nc.vector.tensor_reduce(r[:, 1, :], g, AX.X, ALU.add))
            link(nc.vector.reciprocal(r[:, 2, :], r[:, 1, :]))
            link(nc.vector.tensor_tensor(g, g, wide(r[:, 2, :]), ALU.mult))


def stage_l1_mix(c, a, wk, wqv, b_in, qn, kn):
    big = c.big
    xm = big[:, 0:5000].rearrange("p (k n) -> p k n", k=KC)
    ke = big[:, 5000:7500].rearrange("p (g n) -> p g n", g=2)
    kvb = big[:, 7948:8460].rearrange("p (g d) -> p g d", g=2)
    b_out = big[0:P, 8470:8982]
    out_t = big[:, 9000:14000].rearrange("p (k n) -> p k n", k=KC)
    qt = ke
    vn = c.nat
    memsets(c, [kvb])
    tiles_on_tensor(c, turned_product(c.w[:, 1], c.xt, D, lambda m, cols: biased_to(xm[:, m, cols], b_in[:, m:m + 1])),
                    [weight(c, 0, a["L1_mix_W_out"]), (b_out, a["L1_mix_b_out"].partition_broadcast(P))])
    tiles_on_tensor(c, [(128, n, [(wk[:, k, :], xm[:, 2 * g + k, c0:c0 + n]) for k in range(2)],
                         copy_to(ke[:, g, c0:c0 + n])) for g in range(2) for c0, n in COLS])

    c.recycle()
    stage_queries_and_values(c, xm, wqv, qn, vn, ke)
    stage_keys_and_queries(c, qn, ke, kn, vn, kvb)
    tiles_on_tensor(c, [(128, n * P, ("turn", [qn[:, t, 128 * g:128 * g + 128] for t in range(t0, t0 + n)]),
                         copy_to(qt[:, g, t0 * P:(t0 + n) * P])) for g in range(2) for t0, n in QUERIES])
    tiles_on_tensor(c, [(128, n, [(kvb[:, m // 2, 128 * (m % 2):128 * (m % 2) + 128], qt[:, m // 2, c0:c0 + n])],
                         copy_to(out_t[:, m, c0:c0 + n])) for m in range(KC) for c0, n in COLS])
    tiles_on_tensor(c, natural_product(out_t, c.w[:, 0], lambda t: add_to_x(c, t, extra=b_out)), only_vector=True)



def build(nc, a, out):
    with ExitStack() as ctx:
        ctx.enter_context(nc.allow_non_contiguous_dma(reason="bias and gain vectors of 512 values, by feature"))
        c = Chip(nc, ctx)
        with ExitStack() as graph:
            c.nat = graph.enter_context(nc.sbuf_tensor("first_nat", [128, T, D], F32))
            with ExitStack() as edges:
                m = Edges(nc, edges)
                stage_codes(c, m, a["x"], a["src"], a["dst"])
                stage_adjacency(c, m, c.nat)
            layer0_graph(c, a)
        layer0_attention(c, a)
        layer1(c, a)
        finish(c, out)


def layer0_graph(c, a):
    nc = c.nc
    with ExitStack() as ctx:
        def sb(within, name, shape, dt=F32):
            return within.enter_context(nc.sbuf_tensor("graph_" + name, shape, dt))

        c.xt = sb(ctx, "xt", [128, KC, N])
        c.inv_t = sb(ctx, "inv_t", [128, N])[:, :]
        c.w = sb(ctx, "w", [128, 3, KC, D])
        with ExitStack() as first:
            c.big = sb(first, "big", [128, 15250])
            wq, wkv = a["L0_mix_Wq"], a["L0_mix_Wkv"]
            stage_degrees(c, c.nat, [weight(c, 0, wq), weight(c, 1, wkv[0:D]), weight(c, 2, wkv[D:2 * D])])
            c.recycle()
            neigh, own, biases = a["L0_gnn_Ws_neigh"], a["L0_gnn_Ws_self"], a["L0_gnn_bs"]
            stage_l0_mix(c, a, [weight(c, 0, neigh[0]), weight(c, 1, own[0])]
                         + [(c.gain[:, KC * k:KC * k + KC], column(biases[k])) for k in range(2)])
            c.recycle()
        with ExitStack() as second:
            ha = c.nat[:].rearrange("p t d -> p (t d)")[:, 0:KC * N].rearrange("p (k n) -> p k n", k=KC)
            hb = sb(second, "hb", [128, KC, N])
            u = sb(second, "u", [128, 2, T, D], F32R)
            c.scratch = sb(second, "scratch", [128, 2, 418])
            b_all = sb(second, "b_all", [P, D])[:, :]
            h = c.xt
            for layer in range(3):
                slot, own_slot = (2 * layer) % 3, (2 * layer + 1) % 3
                later = layer < 2
                stage_split_product(c, h, c.w[:, slot], u, None, [weight(c, (2 * layer + 2) % 3, neigh[layer + 1])] if later else
                                    [(b_all, biases[2].partition_broadcast(P))])
                if later:
                    to = (ha, hb)[layer]
                    stage_aggregate(c, h, to, u, c.gain[:, KC * layer:KC * layer + KC], c.w[:, own_slot],
                                    [weight(c, slot, own[layer + 1])], layer == 0)
                    h = to
                else:
                    stage_aggregate_natural(c, h, u, b_all, c.w[:, own_slot])


def layer0_attention(c, a):
    nc = c.nc
    with ExitStack() as ctx:
        c.recycle()
        c.xt = ctx.enter_context(nc.sbuf_tensor("ffn_xt", [128, KC, N], F32))
        kept = nc.dram_tensor("kept_x", (N, D), F32, kind="Internal").ap().rearrange("(t p) d -> p t d", p=P)
        qg, kg = c.gain[:, 8:9], c.gain[:, 9:10]
        ot = c.x[:].rearrange("p t d -> p (t d)")[:, 0:KC * N].rearrange("p (k n) -> p k n", k=KC)
        with ExitStack() as inner:
            vh = inner.enter_context(nc.sbuf_tensor("ffn_v", [128, T, PAIRS * 192], F32))
            split_v = vh[:].rearrange("p t (a b d) -> p t a b d", a=PAIRS, b=3)
            with ExitStack() as first:
                c.nat = first.enter_context(nc.sbuf_tensor("ffn_nat", [128, T, D], F32))
                c.w = first.enter_context(nc.sbuf_tensor("ffn_w", [128, 1, KC, D], F32))
                g, b = c.gain[:, 0:4], c.gain[:, 4:8]
                loads = [(g, column(a["L0_ffn_ln_g"])), (b, column(a["L0_ffn_ln_b"])), weight(c, 0, a["L0_ffn_Wv"])]
                for k in range(2):
                    loads.append((qg[64 * k:64 * k + 64], a["L0_ffn_qn_g"].rearrange("(p o) -> p o", o=1)))
                    loads.append((kg[64 * k:64 * k + 64], a["L0_ffn_kn_g"].rearrange("(p o) -> p o", o=1)))
                memsets(c, [split_v[0:P, :, :, 1, :]], 1.0)
                stage_layernorm(c, c.nat, [c.xt], (g, b), loads, True, True)

                def to_v(t):
                    def copy(e, ps, link):
                        to, of = split_v[0:P, t, :, 0:3:2, :], ps.rearrange("p (a b d) -> p a b d", a=PAIRS, b=2)
                        return e.activation(to, of, ACT.Copy) if is_scalar(e) else e.tensor_copy(to, of)
                    return copy
                tiles_on_tensor(c, natural_product(c.xt, c.w[:, 0], to_v), [(kept, c.x[0:P])])
            with ExitStack() as second:
                m = Attention(nc, second)
                m.peaks = c.small[0:P, 0:30].rearrange("p (i b) -> p i b", b=3)
                m.peak = c.small[0:P, 30:40]
                m.unit = (m.unit, c.small[:, 44:462])
                stage_attention_constants(c, m, kg, m.loads(0, a["L0_ffn_Wk"], a["L0_ffn_Wq"]))
                c.recycle()
                stage_attention(c, m, vh, (kg, qg), a["L0_ffn_Wq"], a["L0_ffn_Wk"], ot)
                c.recycle()

    def outputs(stack, y, loads):
        w = stack.enter_context(nc.sbuf_tensor("ffn_wo", [128, KC, D], F32))
        tiles_on_tensor(c, [], [(w[:], a["L0_ffn_Wo"].rearrange("(k p) n -> p k n", p=128))])
        split_tiles_on_tensor(c, product_split(c, w, ot, y), loads)
    mixture(c, "mix0", outputs, a["L0_ffn_gate_W"], a["L0_ffn_gate_b"],
            a["L0_ffn_b1"], a["L0_ffn_W1"], a["L0_ffn_b2"], a["L0_ffn_W2"], False, [(c.x[0:P], kept)])


def layer1(c, a):
    nc = c.nc
    with ExitStack() as ctx:
        def sb(within, name, shape, dt=F32):
            return within.enter_context(nc.sbuf_tensor("layer1_" + name, shape, dt))

        c.recycle()
        c.xt = sb(ctx, "xt", [128, KC, N])
        c.w = sb(ctx, "w", [128, 2, KC, D])
        wk, wqv, b_in = sb(ctx, "wk", [128, 2, 128])[:, :, :], sb(ctx, "wqv", [128, 192])[:, :], sb(ctx, "b_in", [128, 4])[:, :]
        heads = [(b_in, column(a["L1_mix_b_in"]))]
        for h in range(2):
            rows = slice(64 * h, 64 * h + 64)
            for k in range(2):
                heads.append((wk[rows, k, 64 * k + 32 * h:64 * k + 32 * h + 32], a["L1_mix_Wk"]))
            heads.append((wqv[rows, 32 * h:32 * h + 32], a["L1_mix_Wq"]))
            heads.append((wqv[rows, 64 + 64 * h:128 + 64 * h], a["L1_mix_Wv"]))
        memsets(c, [wk, wqv])
        with ExitStack() as first:
            c.nat = sb(first, "norm", [128, T, D])
            stage_layernorm(c, c.nat, [c.xt], None, [weight(c, 0, a["L1_gnn_weight"])])
        with ExitStack() as second:
            rev = sb(second, "rev", [P, T, N], F32R)
            u = sb(second, "u", [128, 2, T, D], F32R)
            c.scratch = sb(second, "scratch", [128, 4, 512])
            stage_turn_counts(c, rev, c.scratch[0:P])
            c.recycle()
            stage_split_product(c, c.xt, c.w[:, 0], u, c.out_n[0:P, :], [weight(c, 1, a["L1_mix_W_in"])] + heads)
            stage_graph_product(c, rev, u)
        c.big, c.nat = sb(ctx, "big", [128, 14000]), sb(ctx, "nat", [128, T, D])
        with ExitStack() as third:
            stage_l1_mix(c, a, wk, wqv, b_in, sb(third, "qn", [P, T, 256])[:, :, :], sb(third, "kn", [P, T, 256])[:, :, :])

    def normalised(stack, y, loads):
        nat = stack.enter_context(nc.sbuf_tensor("mix1_nat", [128, T, D], F32))
        stage_layernorm(c, nat, y, None, loads, False, True)
    mixture(c, "mix1", normalised, a["L1_ffn_router_w"], None, a["L1_ffn_b1"],
            a["L1_ffn_w1"], a["L1_ffn_b2"], a["L1_ffn_w2"], True)


def finish(c, out):
    nc = c.nc
    with ExitStack() as s:
        stored = c.semaphore("stored")
        block = s.enter_context(nc.Block())

        @block.sync
        def _(sp):
            sp.dma_start(out.rearrange("(t p) d -> p t d", p=P), c.x[0:P]).then_inc(stored, 16)
            sp.wait_ge(stored, 16)


def kernel(**inputs):
    import concourse.bacc as bacc
    from concourse.bass_utils import run_bass_kernel_spmd

    nc = bacc.Bacc("TRN2", target_bir_lowering=False, num_devices=1)
    arrays, aps = {}, {}
    for name, value in inputs.items():
        a = np.ascontiguousarray(value)
        arrays["in_" + name] = a
        aps[name] = nc.dram_tensor("in_" + name, a.shape, mybir.dt.from_np(a.dtype), kind="ExternalInput").ap()
    out = nc.dram_tensor("out", (N, D), F32, kind="ExternalOutput").ap()
    build(nc, aps, out)
    return run_bass_kernel_spmd(nc, [arrays], core_ids=[0]).results[0]["out"]
```
